# Optimizing a Trainium2 kernel written in Bass

```python
import numpy as np
import jax
import jax.numpy as jnp

def _softmax(x, axis=-1):
    return jax.nn.softmax(x, axis=axis)

def _gelu(x):
    return jax.nn.gelu(x, approximate=True)

def _silu(x):
    return jax.nn.silu(x)

def _sigmoid(x):
    return jax.nn.sigmoid(x)

def _layernorm(x, axis=-1, eps=1e-05):
    m = jnp.mean(x, axis=axis, keepdims=True)
    v = jnp.var(x, axis=axis, keepdims=True)
    return (x - m) / jnp.sqrt(v + eps)

def _scatter_add(tgt, idx, src, axis=0):
    return tgt.at[idx].add(src)

def _segment_sum(src, seg, n):
    return jax.ops.segment_sum(src, seg, n)
kernel_name = 'mk_cond_resid_d2_seqx_r4_e79297'

def setup_inputs(seed: int=0):
    np.random.seed(seed)
    _w = jnp.asarray

    def _rec_inputs():
        import jax
        import jax.numpy as jnp
        _rk = jax.random.key(seed)
        x = -0.0003929 + 0.9999 * jax.random.normal(jax.random.fold_in(_rk, 1), (128, 64, 256), jnp.float32)
        _lenS = 64 - jax.random.randint(jax.random.fold_in(_rk, 7), (128,), 0, max(1, 64 // 4) + 1, jnp.int32)
        _lenS2 = 64 - jax.random.randint(jax.random.fold_in(_rk, 8), (128,), 0, max(1, 64 // 4) + 1, jnp.int32)
        cond_2048 = 0.00782532 + 1.00527 * jax.random.normal(jax.random.fold_in(_rk, 11), (128, 512), jnp.float32)
        return (x, cond_2048)
    x, cond_2048 = _rec_inputs()

    def _L0_cond_setup():
        import jax, jax.numpy as jnp
        import numpy as np
        B, S, D_MODEL, D_INNER, D_STATE = (4, 1024, 256, 512, 16)
        key = jax.random.key(seed)
        ks = jax.random.split(key, 12)
        inp = {'x': jax.random.normal(ks[0], (B, S, D_MODEL), jnp.float32), 't_emb': jax.random.normal(ks[1], (B, D_INNER), jnp.float32), 'W_in': jax.random.normal(ks[2], (2 * D_INNER, D_MODEL), jnp.float32) * 0.02, 'W_conv': jax.random.normal(ks[3], (D_INNER, 1, 4), jnp.float32) * 0.1, 'b_conv': jnp.zeros((D_INNER,), jnp.float32), 'ln_g': jnp.ones((D_INNER,), jnp.float32), 'ln_b': jnp.zeros((D_INNER,), jnp.float32), 'W_xproj': jax.random.normal(ks[4], (3 * D_STATE, D_INNER), jnp.float32) * 0.02, 'W_dt': jax.random.normal(ks[5], (D_STATE, D_STATE), jnp.float32) * 0.01, 'b_dt': jax.random.uniform(ks[6], (D_STATE,), jnp.float32) * 0.1, 'A_log': jax.random.normal(ks[7], (D_STATE,), jnp.float32) * 0.1, 'D': jnp.ones((D_INNER,), jnp.float32) * 0.1, 'W_out': jax.random.normal(ks[8], (D_MODEL, D_INNER), jnp.float32) * 0.02}
        return inp
    _L0_cond_all = _L0_cond_setup()
    _L0_cond_in = {k: v for k, v in _L0_cond_all.items() if k in ('W_in', 'W_conv', 'b_conv', 'ln_g', 'ln_b', 'W_xproj', 'W_dt', 'b_dt', 'A_log', 'D', 'W_out')}
    del _L0_cond_all

    def _L1_cond_setup():
        import jax, jax.numpy as jnp
        import numpy as np
        EPS_IN = 1e-05
        EPS_DM = 1e-08

        def _dcoef(weight, style):
            return jax.lax.rsqrt(jnp.einsum('oi,bi->bo', jnp.square(weight), jnp.square(style)) + EPS_DM)
        key = jax.random.key(seed)
        ks = jax.random.split(key, 7)
        B, S, H = (8, 256, 256)
        lim = 1.0 / np.sqrt(H)
        u = lambda k, shp: jax.random.uniform(k, shp, jnp.float32, -lim, lim)
        return {'x': jax.random.normal(ks[0], (B, S, H), jnp.float32), 'q_weight': u(ks[1], (H, H)), 'k_weight': u(ks[2], (H, H)), 'v_weight': u(ks[3], (H, H)), 'w_weight': u(ks[4], (H, H)), 'u_weight': u(ks[5], (H, H)), 'styles': jax.random.normal(ks[6], (B, 2 * H), jnp.float32) * 0.5 + 1.0, 'num_heads': 16}
    _L1_cond_all = _L1_cond_setup()
    _L1_cond_in = {k: v for k, v in _L1_cond_all.items() if k in ('q_weight', 'k_weight', 'v_weight', 'w_weight', 'u_weight')}
    del _L1_cond_all
    return {'x': x, 'cond_2048': cond_2048, 'L0_cond_W_in': _L0_cond_in['W_in'], 'L0_cond_W_conv': _L0_cond_in['W_conv'], 'L0_cond_b_conv': _L0_cond_in['b_conv'], 'L0_cond_ln_g': _L0_cond_in['ln_g'], 'L0_cond_ln_b': _L0_cond_in['ln_b'], 'L0_cond_W_xproj': _L0_cond_in['W_xproj'], 'L0_cond_W_dt': _L0_cond_in['W_dt'], 'L0_cond_b_dt': _L0_cond_in['b_dt'], 'L0_cond_A_log': _L0_cond_in['A_log'], 'L0_cond_D': _L0_cond_in['D'], 'L0_cond_W_out': _L0_cond_in['W_out'], 'L1_cond_q_weight': _L1_cond_in['q_weight'], 'L1_cond_k_weight': _L1_cond_in['k_weight'], 'L1_cond_v_weight': _L1_cond_in['v_weight'], 'L1_cond_w_weight': _L1_cond_in['w_weight'], 'L1_cond_u_weight': _L1_cond_in['u_weight']}

def reference(x, cond_2048, L0_cond_W_in, L0_cond_W_conv, L0_cond_b_conv, L0_cond_ln_g, L0_cond_ln_b, L0_cond_W_xproj, L0_cond_W_dt, L0_cond_b_dt, L0_cond_A_log, L0_cond_D, L0_cond_W_out, L1_cond_q_weight, L1_cond_k_weight, L1_cond_v_weight, L1_cond_w_weight, L1_cond_u_weight):
    import jax
    import jax.numpy as jnp

    def _L0_cond_ref(x, t_emb, W_in, W_conv, b_conv, ln_g, ln_b, W_xproj, W_dt, b_dt, A_log, D, W_out):
        import jax, jax.numpy as jnp
        import numpy as np
        B, S, D_MODEL, D_INNER, D_STATE = (4, 1024, 256, 512, 16)
        d_inner = W_conv.shape[0]
        d_state = A_log.shape[0]
        xr, gate = jnp.split(x @ W_in.T, 2, axis=-1)
        xr = xr + t_emb[:, None, :]
        xc = jax.lax.conv_general_dilated(xr.transpose(0, 2, 1), W_conv, (1,), [(3, 0)], feature_group_count=d_inner, dimension_numbers=('NCH', 'OIH', 'NCH')) + b_conv[None, :, None]
        xc = jax.nn.silu(xc).transpose(0, 2, 1)
        mu = xc.mean(-1, keepdims=True)
        var = xc.var(-1, keepdims=True)
        xn = (xc - mu) / jnp.sqrt(var + 1e-05) * ln_g + ln_b
        Bm, Cm, dt = jnp.split(xn @ W_xproj.T, 3, axis=-1)
        dt = jnp.tanh(dt @ W_dt.T + b_dt) * 0.01
        A = -jnp.tanh(A_log)
        Ad = 1.0 + dt * A
        Bd = Bm * jnp.minimum(jnp.linalg.norm(xn, axis=-1, keepdims=True), 1.0)
        h0 = jnp.zeros((xn.shape[0], d_state, d_inner), xn.dtype)

        def step(h, inputs):
            ad, bd, xt, ct = inputs
            h = jnp.clip(h * ad[:, :, None] + bd[:, :, None] * xt[:, None, :], -10.0, 10.0)
            yt = jnp.einsum('bd,bdh->bh', ct, h)
            return (h, yt)
        _, ys = jax.lax.scan(step, h0, (Ad.transpose(1, 0, 2), Bd.transpose(1, 0, 2), xn.transpose(1, 0, 2), Cm.transpose(1, 0, 2)))
        y = ys.transpose(1, 0, 2) + D * xn
        return y * jax.nn.silu(gate) @ W_out.T

    def _L1_cond_ref(x, q_weight, k_weight, v_weight, w_weight, u_weight, styles, num_heads):
        import jax, jax.numpy as jnp
        import numpy as np
        EPS_IN = 1e-05
        EPS_DM = 1e-08

        def _dcoef(weight, style):
            return jax.lax.rsqrt(jnp.einsum('oi,bi->bo', jnp.square(weight), jnp.square(style)) + EPS_DM)
        B, S, H = x.shape
        nh = num_heads
        d = H // nh
        scale = jnp.asarray(d, x.dtype) ** (-0.5)
        s1 = styles[:, :H]
        s2 = styles[:, H:]
        x = x * s1[:, None, :]
        mu = jnp.mean(x, axis=-1, keepdims=True)
        var = jnp.mean(jnp.square(x - mu), axis=-1, keepdims=True)
        x = (x - mu) * jax.lax.rsqrt(var + EPS_IN)
        q_dc = _dcoef(q_weight, s1)
        k_dc = _dcoef(k_weight, s1)
        v_dc = _dcoef(v_weight, s1)
        w_dc = _dcoef(w_weight, s2)
        u_dc = _dcoef(u_weight, s2)

        def heads(t):
            return t.reshape(B, S, nh, d).transpose(0, 2, 1, 3)
        q = heads(jnp.einsum('bsh,oh->bso', x, q_weight) * q_dc[:, None, :])
        k = heads(jnp.einsum('bsh,oh->bso', x, k_weight) * k_dc[:, None, :])
        v_flat = jnp.einsum('bsh,oh->bso', x, v_weight) * v_dc[:, None, :] * s2[:, None, :]
        skip = v_flat
        v = heads(v_flat)
        attn = jnp.einsum('bhqd,bhkd->bhqk', q, k) * scale
        attn = jax.nn.softmax(attn, axis=-1)
        out = jnp.einsum('bhqk,bhkd->bhqd', attn, v).transpose(0, 2, 1, 3).reshape(B, S, H)
        out = jnp.einsum('bsh,oh->bso', out, w_weight) * w_dc[:, None, :]
        skip = jnp.einsum('bsh,oh->bso', skip, u_weight) * u_dc[:, None, :]
        return out + skip
    x = x + _L0_cond_ref(x, cond_2048, L0_cond_W_in, L0_cond_W_conv, L0_cond_b_conv, L0_cond_ln_g, L0_cond_ln_b, L0_cond_W_xproj, L0_cond_W_dt, L0_cond_b_dt, L0_cond_A_log, L0_cond_D, L0_cond_W_out)
    x = x + _L1_cond_ref(x, L1_cond_q_weight, L1_cond_k_weight, L1_cond_v_weight, L1_cond_w_weight, L1_cond_u_weight, cond_2048, 16)
    return x

_drawn_inputs = setup_inputs


def setup_inputs(seed=0):
    import zlib

    import numpy as np

    out = dict(_drawn_inputs(seed))
    spreads = {'L0_cond_b_conv': (0.0, 0.1),
     'L0_cond_ln_g': (1.0, 0.2),
     'L0_cond_ln_b': (0.0, 0.1),
     'L0_cond_D': (0.10000000149011612, 0.6)}
    factors = {'L0_cond_W_dt': 200.0, 'L0_cond_b_dt': 155.279, 'L0_cond_A_log': 28.773}
    for name, (base, spread) in spreads.items():
        noise = np.random.default_rng([zlib.crc32(name.encode()), seed]).standard_normal(out[name].shape)
        drawn = base * np.exp(spread * noise) if base else spread * noise
        out[name] = jnp.asarray(drawn.astype(out[name].dtype))
    for name, factor in factors.items():
        out[name] = (out[name] * factor).astype(out[name].dtype)
    return out
```

```python
from contextlib import ExitStack

import concourse.bass as bass
from concourse import mybir

F32 = mybir.dt.float32
BF16 = mybir.dt.bfloat16
ALU = mybir.AluOpType
ACT = mybir.ActivationFunctionType
AX_X = mybir.AxisListType.X
ds = bass.ds


def mamba_attention_kernel(nc, x, cond, W_in, W_conv, b_conv, ln_g, ln_b, W_xproj, W_dt, b_dt, A_log, D,
                           W_out, q_w, k_w, v_w, w_w, u_w, out):
    B, S, DM = x.shape
    DI = W_conv.shape[0]
    DS = A_log.shape[0]
    TAPS = W_conv.shape[2]
    P = 128
    TOK = 2 * S
    PAIRS = 8
    TPP = B // 2 // PAIRS
    MC = DI // P
    KC = DM // P
    HEADS = 16
    HD = DM // HEADS
    HPC = P // HD
    STEPS = 8
    SLICES = S // STEPS
    HALF = STEPS // 2
    PARTS = 3
    NPROJ = 3 * DS
    CLIP = 10.0
    VW = HD + 1
    assert TOK == P and TPP == 8 and TPP * DS == P and SLICES == TPP and HPC * HD == P

    ctx = ExitStack()
    with ctx:
        def sb(name, shape, dt=F32):
            return ctx.enter_context(nc.sbuf_tensor(name, shape, dt))

        def pb(name, shape=(P, 512), dt=F32):
            return ctx.enter_context(nc.psum_tensor(name, list(shape), dt))

        def sem(name):
            return ctx.enter_context(nc.semaphore(name))

        xs_dram = nc.dram_tensor("xn_parts", [PAIRS, 2, PARTS, TPP, S, DI], BF16).ap()
        bct_dram = nc.dram_tensor("b_c_dt", [PAIRS, 2, TPP, NPROJ, S], F32).ap()
        dx_dram = nc.dram_tensor("skip_d_xn", [PAIRS, TPP, P, MC * TOK], F32).ap()
        row_dram = nc.dram_tensor("style_rows", [B, 3 * DM], F32).ap()

        ident = sb("ident", [P, P])
        sel = sb("sel", [PARTS * TPP, P], BF16)
        band = sb("band", [PARTS * TPP, 3, P])
        mask = sb("mask", [P, HPC])
        half_pow = sb("half_pow", [P, 2])
        eps = sb("eps", [P, 2])
        WinT = sb("WinT", [P, KC, 2 * DI])
        WoutT = sb("WoutT", [P, MC, DM])
        WxT = sb("WxT", [P, MC, NPROJ])
        L1T = sb("L1T", [P, 5, KC, DM])
        condT = sb("condT", [P, MC, B])
        qk_scale = sb("qk_scale", [P, KC, B])
        v_scale = sb("v_scale", [P, KC, B])
        conv_w = sb("conv_w", [P, MC, TAPS])
        conv_b = sb("conv_b", [P, MC])
        d_col = sb("d_col", [P, MC])
        g_row = sb("g_row", [P, DI])
        b_row = sb("b_row", [P, DI])
        a_col = sb("a_col", [P, 2])
        bdt_col = sb("bdt_col", [NPROJ, 1])
        wdtT = sb("wdtT", [DS, DS])
        stage = sb("stage", [P, 6144])
        dco = sb("dco", [P, 5, DM])

        st_in = stage[:, 0:2048].rearrange("p (c i) -> p c i", c=8)
        st_out = stage[:, 2048:3072].rearrange("p (c i) -> p c i", c=2)
        st_l1 = stage[:, 3072:5632].rearrange("p (w c i) -> p w c i", w=5, c=2)
        st_x = stage[0:NPROJ, 5632:6144]
        cond_nat = sb("cond_nat", [P, DI])
        st_dt = sb("st_dt", [DS, DI])
        sq_l1 = stage[:, 0:2560].rearrange("p (w k o) -> p w k o", w=5, k=KC)
        sq_cond = stage[:, 2560:3072].rearrange("p (m b) -> p m b", m=MC)

        a_x = sb("a_x", [P, DM])
        a_xT = sb("a_xT", [P, KC, TOK])
        PADT = S + TAPS - 1
        a_xr = sb("a_xr", [P, MC, 2, PADT])
        a_acc = sb("a_acc", [P, MC, 2, S])
        a_th = sb("a_th", [P, MC * TOK])
        a_xc = sb("a_xc", [P, MC, TOK])
        a_bn = sb("a_bn", [P, 6])
        a_mv = sb("a_mv", [P, 2])
        a_ve = sb("a_ve", [P, 1])
        a_rs = sb("a_rs", [P, 1])
        a_z = sb("a_z", [P, DI])
        a_xg = sb("a_xg", [P, DI])
        a_xn = sb("a_xn", [P, DI])
        a_r1 = sb("a_r1", [P, DI])
        a_parts = sb("a_parts", [P, PARTS, DI], BF16)
        a_ss = sb("a_ss", [P, 1])
        a_nrm = sb("a_nrm", [P, 2])
        a_xnT = sb("a_xnT", [P, MC, TOK])
        a_dx = sb("a_dx", [P, MC, TOK])
        a_bc = sb("a_bc", [P, P])
        a_bcT = sb("a_bcT", [NPROJ, TOK])

        xs_sb = [[sb(f"xs_{r}_{h}", [PARTS * TPP, HALF, DI], BF16) for h in range(2)] for r in range(2)]
        raw = [sb(f"raw_{r}", [P, 3, S]) for r in range(2)]
        ad = [sb(f"ad_{r}", [P, S]) for r in range(2)]
        pr = [sb(f"pr_{r}", [P, S]) for r in range(2)]
        rp = [sb(f"rp_{r}", [P, S]) for r in range(2)]
        hi = [sb(f"hi_{r}", [P, S]) for r in range(2)]
        lo = [sb(f"lo_{r}", [P, S]) for r in range(2)]
        bd = [sb(f"bd_{r}", [P, S]) for r in range(2)]
        cp = [sb(f"cp_{r}", [P, S]) for r in range(2)]
        cm = [sb(f"cm_{r}", [P, S, TPP]) for r in range(2)]
        RING = 4
        gu = [sb(f"gu_{r}", [P, DI]) for r in range(2)]
        gc = [sb(f"gc_{r}", [P, RING, DI]) for r in range(2)]
        zeros = sb("zeros", [P, S])
        yT = sb("yT", [P, MC, TPP, 2, S])

        c_x = sb("c_x", [P, DM])
        c_dx = sb("c_dx", [P, MC, TOK])
        c_rows = sb("c_rows", [P, 3, DM])
        c_xT = sb("c_xT", [P, KC, TOK])
        c_th = sb("c_th", [P, MC * TOK])
        c_sg = sb("c_sg", [P, MC * TOK])
        c_yd = sb("c_yd", [P, MC, TOK])
        c_yg = sb("c_yg", [P, MC, TOK])
        c_x1 = sb("c_x1", [P, DM])
        c_xm = sb("c_xm", [P, DM])
        c_bn = sb("c_bn", [P, 6])
        c_mv = sb("c_mv", [P, 2])
        c_ve = sb("c_ve", [P, 1])
        c_rs = sb("c_rs", [P, 1])
        c_z = sb("c_z", [P, DM])
        c_zT = sb("c_zT", [P, KC, TOK])
        c_zz = sb("c_zz", [P, KC, 2, 2, S])
        c_q = sb("c_q", [P, KC, TOK])
        c_vsT = sb("c_vsT", [P, KC, TOK])
        c_kbd = sb("c_kbd", [P, HPC, KC, TOK])
        c_vbd = sb("c_vbd", [P, 2, HEADS // 2, 2, VW])
        c_mx = sb("c_mx", [P, HEADS])
        c_s = sb("c_s", [P, KC, HPC, S])
        c_e = sb("c_e", [P, KC, HPC * S])
        c_pT = sb("c_pT", [P, KC, HPC // 2, TOK])
        c_rc = sb("c_rc", [P, HEADS])
        c_o = sb("c_o", [P, HEADS, HD])
        c_oT = sb("c_oT", [P, KC, TOK])
        c_f = sb("c_f", [P, 2, DM])
        c_f2 = sb("c_f2", [P, DM])
        c_out = sb("c_out", [P, DM])

        ps_x = [[pb(f"ps_x_{r}_{h}") for h in range(2)] for r in range(2)]
        ps_y = pb("ps_y")
        ps_a = pb("ps_a")
        ps_c1 = pb("ps_c1")
        ps_c2 = pb("ps_c2")

        names = """w_bc a_st w_ld w_cst w_tp w_ev w_sq w_dp w_de w_dpow w_scale w_row w_a w_pool
            a_ld a_s_xTp a_s_xT a_s_inp a_s_xr a_s_tap a_s_conv a_s_th a_s_xc a_s_xcT a_s_st a_s_seen a_s_mv a_s_ve a_s_rs
            a_s_z a_s_xg a_s_xn a_s_p1 a_s_r1 a_s_p2 a_s_p3 a_s_ss a_s_nr a_s_nm a_s_xnTp a_s_xnT a_s_dx a_s_proj
            a_s_bc a_s_bcTp a_s_bcT 
            b_ld_raw b_prep b_cm b_ld_xs0 b_ld_xs1 b_xrep b_u b_g b_ymm b_yev
            c_ld_x c_ld_dx c_ld_rows c_s_xTp c_s_xT c_s_gate c_s_th c_s_sg c_s_yd c_s_yg c_s_wout c_s_x1 c_s_xm c_s_st c_s_seen
            c_s_mv c_s_ve c_s_rs c_s_z c_s_zTp c_s_zT c_s_qv c_s_q c_s_vs c_s_k c_s_kbd c_s_v c_s_vbd c_s_sc
            c_s_mx c_s_sub c_s_e c_s_pTp c_s_pT0 c_s_pT1 c_s_pv c_s_rc c_s_o c_s_oTp c_s_oT c_s_fin c_s_f c_s_f2
            c_s_out c_st""".split()
        s = {n: sem(n) for n in names}
        block = ctx.enter_context(nc.Block())

        head_start = {
            "dve": """a_s_xr:1 a_s_conv:3 a_s_xc:1 a_s_st:1 a_s_mv:1 a_s_z:1 a_s_nm:1 a_s_bc:2 b_prep:14 b_cm:4
                b_u:16 b_g:16 c_s_sg:1 c_s_yg:1 c_s_x1:1 c_s_st:1 c_s_mv:1 c_s_z:1 c_s_q:1 c_s_vs:1 c_s_mx:2 c_s_sub:2
                c_s_pT1:1 c_s_rc:1 c_s_o:1 c_s_oT:1 c_s_f:1""",
            "pe": """a_s_xTp:1 a_s_inp:1 a_s_xcT:1 a_s_xnTp:1 a_s_proj:1 a_s_bcTp:1 b_xrep:16 b_ymm:16 c_s_xTp:1
                c_s_gate:1 c_s_wout:1 c_s_zTp:1 c_s_qv:1 c_s_k:1 c_s_v:1 c_s_sc:2 c_s_pTp:2 c_s_pv:1 c_s_oTp:1
                c_s_fin:1""",
            "act": """a_s_xT:1 a_s_tap:1 a_s_th:1 a_s_p1:1 a_s_ss:1 a_s_p2:1 a_s_xnT:1 a_s_bcT:2 b_yev:2 c_s_xT:1
                c_s_th:1 c_s_zT:2 c_s_kbd:1 c_s_vbd:1 c_s_e:2 c_s_pT0:1""",
            "pool": """a_s_ve:1 a_s_rs:1 a_s_xg:1 a_s_xn:1 a_s_r1:1 a_s_p3:1 a_s_nr:1 a_s_dx:1 c_s_yd:1 c_s_xm:1
                c_s_ve:1 c_s_rs:1 c_s_f2:1 c_s_out:1""",
            "sp": "a_ld:16 a_st:80 b_ld_raw:96 b_ld_xs0:32 b_ld_xs1:32 c_ld_x:16 c_ld_dx:16 c_ld_rows:32 c_st:16",
        }

        def give_head_start(eng, name):
            for item in head_start[name].split():
                which, count = item.split(":")
                eng.sem_inc(s[which], int(count))

        groups = []
        for k in range(KC):
            for h in range(2):
                groups.append(([(q * P, st_in[:, 4 * h + q, k * P:(k + 1) * P]) for q in range(4)],
                               WinT[:, k, h * 512:(h + 1) * 512], 512))
        for mp in range(2):
            groups.append(([((2 * a + c) * P, st_out[:, c, (2 * mp + a) * P:(2 * mp + a + 1) * P])
                            for a in range(2) for c in range(2)],
                           WoutT[:, 2 * mp:2 * mp + 2, :].rearrange("p a o -> p (a o)"), 512))
        for w in range(5):
            groups.append(([((2 * k + c) * P, st_l1[:, w, c, k * P:(k + 1) * P]) for k in range(2) for c in range(2)],
                           L1T[:, w, :, :].rearrange("p k o -> p (k o)"), 512))
        groups.append(([(m * P, cond_nat[:, m * P:(m + 1) * P]) for m in range(MC)],
                       condT[:, :, :].rearrange("p m b -> p (m b)"), 512))
        NG = len(groups)
        W_LOADS = 5 + 3

        def bcast_mid(ap, n):
            return ap.unsqueeze(2).to_broadcast([ap.shape[0], ap.shape[1], n])

        @block.sync
        def _(sp):
            give_head_start(sp, "sp")
            sp.dma_start(st_in, W_in.rearrange("(c p) i -> p c i", p=P)).then_inc(s["w_ld"], 16)
            sp.dma_start(st_out, W_out.rearrange("(c p) i -> p c i", p=P)).then_inc(s["w_ld"], 16)
            for w, src in enumerate((q_w, k_w, v_w, w_w, u_w)):
                sp.dma_start(st_l1[:, w], src.rearrange("(c p) i -> p c i", p=P)).then_inc(s["w_ld"], 16)
            sp.dma_start(cond_nat[:, :], cond).then_inc(s["w_ld"], 16)
            sp.dma_start(st_x, W_xproj).then_inc(s["w_cst"], 16)
            sp.dma_start(st_dt[:, :], W_xproj[2 * DS:3 * DS, :]).then_inc(s["w_cst"], 16)
            sp.dma_start(wdtT[:, :], W_dt.rearrange("a b -> b a"), allow_slow_non_contiguous=True).then_inc(s["w_cst"], 16)
            for dst, src in ((conv_b, b_conv), (d_col, D)):
                sp.dma_start(dst[:, :], src.rearrange("(m p) -> p m", p=P),
                             allow_slow_non_contiguous=True).then_inc(s["w_cst"], 16)
            sp.dma_start(conv_w[:, :, :], W_conv.rearrange("(m p) o k -> p m (o k)", p=P),
                         allow_slow_non_contiguous=True).then_inc(s["w_cst"], 16)
            sp.dma_start(g_row[:, :], ln_g.partition_broadcast(P)).then_inc(s["w_cst"], 16)
            sp.dma_start(b_row[:, :], ln_b.partition_broadcast(P)).then_inc(s["w_cst"], 16)
            for j in range(TPP):
                sp.dma_start(a_col[j * DS:(j + 1) * DS, 0:1], A_log.unsqueeze(1),
                             allow_slow_non_contiguous=True).then_inc(s["w_cst"], 16)
            sp.dma_start(bdt_col[2 * DS:3 * DS, :], b_dt.unsqueeze(1),
                         allow_slow_non_contiguous=True).then_inc(s["w_cst"], 16)
            sp.wait_ge(s["w_ld"], 16 * W_LOADS)
            sp.dma_start(row_dram[:, 0:DM], cond_nat[:, 0:DM]).then_inc(s["w_row"], 16)
            sp.wait_ge(s["w_dpow"], 1)
            sp.dma_start(row_dram[:, DM:3 * DM], dco[:, 3:5, :].rearrange("p w o -> p (w o)")).then_inc(s["w_row"], 16)
            sp.wait_ge(s["w_row"], 32)

            def load_a(n):
                sp.wait_ge(s["a_s_xTp"], n)
                sp.dma_start(a_x[:, :], x_tok[ds((n - 1) * TOK, TOK), :]).then_inc(s["a_ld"], 16)

            def store_a(i, j, n):
                sp.wait_ge(s["a_s_p3"], n + 1)
                sp.wait_ge(s["a_s_p2"], n + 1)
                for r in range(2):
                    sp.dma_start(xs_dram[ds(i, 1), r, :, ds(j, 1)].rearrange("o q u t c -> (o u t) q c"),
                                 a_parts[r * S:(r + 1) * S, :, :]).then_inc(s["a_st"], 16)
                sp.wait_ge(s["a_s_dx"], n + 1)
                sp.dma_start(dx_dram[ds(i, 1), ds(j, 1)].rearrange("o u p c -> (o u p) c"),
                             a_dx[:, :, :].rearrange("p m t -> p (m t)")).then_inc(s["a_st"], 16)
                sp.wait_ge(s["a_s_bcT"], 2 * n + 2)
                for r in range(2):
                    sp.dma_start(bct_dram[ds(i, 1), r, ds(j, 1)].rearrange("o u k t -> (o u k) t"),
                                 a_bcT[:, r * S:(r + 1) * S]).then_inc(s["a_st"], 16)

            def load_b_params(i):
                used, stored = sp.snap(14 * (i + 1)), sp.snap(80 * TPP * (i + 1) + 80)
                sp.wait_ge(s["b_prep"], used)
                sp.wait_ge(s["a_st"], stored)
                for r in range(2):
                    for k in range(3):
                        sp.dma_start(raw[r][:, k, :],
                                     bct_dram[ds(i, 1), r].rearrange("o j (k d) t -> k (o j) d t", k=3)[k])\
                            .then_inc(s["b_ld_raw"], 16)

            def load_b_xs(i, j, h):
                sl = i * SLICES + j + 1
                sp.wait_ge(s["b_xrep"], sl * 2 * STEPS)
                for r in range(2):
                    sp.dma_start(xs_sb[r][h][:, :, :],
                                 xs_dram[ds(i, 1), r, :, :, ds(j * STEPS + h * HALF, HALF)]
                                 .rearrange("o q j t c -> (o q j) t c")).then_inc(s[f"b_ld_xs{h}"], 16)

            def load_c(i, j, n):
                sp.wait_ge(s["c_s_x1"], n)
                sp.wait_ge(s["c_s_xTp"], n)
                sp.dma_start(c_x[:, :], x_tok[ds((n - 1) * TOK, TOK), :]).then_inc(s["c_ld_x"], 16)
                sp.wait_ge(s["c_s_yd"], n)
                sp.dma_start(c_dx[:, :, :].rearrange("p m t -> p (m t)"),
                             dx_dram[ds(i, 1), ds(j, 1)].rearrange("o u p c -> (o u p) c")).then_inc(s["c_ld_dx"], 16)
                sp.wait_ge(s["c_s_f"], n)
                for r in range(2):
                    sp.dma_start(c_rows[r * S:(r + 1) * S, :, :].rearrange("p w o -> p (w o)"),
                                 row_dram[ds((n - 1) * 2 + r, 1), :].to_broadcast([S, 3 * DM])).then_inc(s["c_ld_rows"], 16)

            def store_c(n):
                sp.wait_ge(s["c_s_out"], n + 1)
                sp.dma_start(o_tok[ds((n - 1) * TOK, TOK), :], c_out[:, :]).then_inc(s["c_st"], 16)

            x_tok = x.rearrange("b t c -> (b t) c")
            o_tok = out.rearrange("b t c -> (b t) c")
            with sp.Fori(0, PAIRS) as i:
                with sp.Fori(0, TPP) as j:
                    n = i * TPP + j + 1
                    load_a(n)
                    store_a(i, j, n)
                load_b_params(i)
                with sp.Fori(0, SLICES) as j:
                    for h in range(2):
                        load_b_xs(i, j, h)
                with sp.Fori(0, TPP) as j:
                    n = i * TPP + j + 1
                    load_c(i, j, n)
                    store_c(n)
            sp.wait_ge(s["c_st"], 16 * (PAIRS * TPP + 1))
            sp.wait_ge(s["a_st"], 80 * (PAIRS * TPP + 1))

        @block.gpsimd
        def _(pool):
            give_head_start(pool, "pool")
            pool.memset(ident[:, :], 0.0).then_inc(s["w_pool"], 1)
            pool.memset(mask[:, :], 1.0).then_inc(s["w_pool"], 1)
            pool.memset(band[:, :, :], 1.0).then_inc(s["w_pool"], 1)
            pool.memset(half_pow[:, 0:1], -0.5).then_inc(s["w_pool"], 1)
            pool.memset(half_pow[:, 1:2], 0.5).then_inc(s["w_pool"], 1)
            pool.memset(eps[:, 0:1], 4e-5)
            pool.memset(eps[:, 1:2], 1e-5)
            pool.memset(a_bc[:, :], 0.0).then_inc(s["w_bc"], 1)
            pool.wait_ge(s["w_pool"], 5)
            pool.affine_select(out=ident[:, :], in_=ident[:, :], compare_op=ALU.not_equal, fill=1.0, base=0,
                               pattern=[[-1, P]], channel_multiplier=1).then_inc(s["w_pool"], 1)
            pool.affine_select(out=mask[:, :], in_=mask[:, :], compare_op=ALU.is_ge, fill=0.0, base=0,
                               pattern=[[-HD, HPC]], channel_multiplier=1).then_inc(s["w_pool"], 1)
            for q in range(PARTS):
                pool.affine_select(out=band[:, q, :], in_=band[:, q, :], compare_op=ALU.is_ge, fill=0.0,
                                   base=DS * TPP * q, pattern=[[1, P]], channel_multiplier=-DS).then_inc(s["w_pool"], 1)
            pool.wait_ge(s["w_pool"], 10)
            pool.affine_select(out=mask[:, :], in_=mask[:, :], compare_op=ALU.is_ge, fill=0.0, base=HD - 1,
                               pattern=[[HD, HPC]], channel_multiplier=-1).then_inc(s["w_pool"], 1)
            for q in range(PARTS):
                pool.affine_select(out=band[:, q, :], in_=band[:, q, :], compare_op=ALU.is_ge, fill=0.0,
                                   base=DS - 1 - DS * TPP * q, pattern=[[-1, P]],
                                   channel_multiplier=DS).then_inc(s["w_pool"], 1)
            pool.wait_ge(s["w_pool"], 14)
            pool.tensor_tensor(band[:, 0, :], band[:, 0, :], band[:, 1, :], ALU.add).then_inc(s["w_pool"], 1)
            pool.wait_ge(s["w_pool"], 15)
            pool.tensor_tensor(sel[:, :], band[:, 0, :], band[:, 2, :], ALU.add).then_inc(s["w_pool"], 1)
            pool.wait_ge(s["w_de"], 5)
            pool.tensor_tensor(dco[:, :, :].rearrange("p w o -> p (w o)"), dco[:, :, :].rearrange("p w o -> p (w o)"),
                               half_pow[:, 0:1].to_broadcast([P, 5 * DM]), ALU.pow).then_inc(s["w_dpow"], 1)

            def stage_a(n):
                pool.wait_ge(s["a_s_mv"], n + 1)
                pool.tensor_tensor(a_ve[:, :], a_mv[:, 1:2], eps[:, 0:1], ALU.add).then_inc(s["a_s_ve"], 1)
                pool.wait_ge(s["a_s_ve"], n + 1)
                pool.wait_ge(s["a_s_z"], n)
                pool.tensor_tensor(a_rs[:, :], a_ve[:, :], half_pow[:, 0:1], ALU.pow).then_inc(s["a_s_rs"], 1)
                pool.wait_ge(s["a_s_z"], n + 1)
                pool.tensor_tensor(a_xg[:, :], a_z[:, :], g_row[:, :], ALU.mult).then_inc(s["a_s_xg"], 1)
                pool.wait_ge(s["a_s_xg"], n + 1)
                pool.wait_ge(s["a_s_xnTp"], n)
                pool.wait_ge(s["a_s_ss"], n)
                pool.wait_ge(s["a_s_p1"], n)
                pool.tensor_tensor(a_xn[:, :], a_xg[:, :], b_row[:, :], ALU.add).then_inc(s["a_s_xn"], 1)
                pool.wait_ge(s["a_s_p1"], n + 1)
                pool.wait_ge(s["a_s_p2"], n)
                pool.tensor_tensor(a_r1[:, :], a_xn[:, :], a_parts[:, 0, :], ALU.subtract).then_inc(s["a_s_r1"], 1)
                pool.wait_ge(s["a_s_p2"], n + 1)
                pool.wait_ge(s["a_st"], 80 * n)
                pool.wait_ge(s["a_s_r1"], n + 1)
                pool.tensor_tensor(a_parts[:, 2, :], a_r1[:, :], a_parts[:, 1, :], ALU.subtract).then_inc(s["a_s_p3"], 1)
                pool.wait_ge(s["a_s_ss"], n + 1)
                pool.wait_ge(s["a_s_nm"], n)
                pool.tensor_tensor(a_nrm[:, 0:1], a_ss[:, :], half_pow[:, 1:2], ALU.pow).then_inc(s["a_s_nr"], 1)
                pool.wait_ge(s["a_s_xnT"], n + 1)
                pool.wait_ge(s["a_st"], 80 * n)
                pool.tensor_tensor(a_dx[:, :, :], a_xnT[:, :, :], bcast_mid(d_col[:, :], TOK), ALU.mult)\
                    .then_inc(s["a_s_dx"], 1)

            def stage_c(i, j, n):
                pool.wait_ge(s["c_ld_dx"], 16 * (n + 1))
                pool.wait_ge(s["b_yev"], 2 * SLICES * (i + 1) + 2)
                pool.wait_ge(s["c_s_yg"], n)
                pool.tensor_tensor(c_yd[:, :, :], c_dx[:, :, :],
                                   yT[:, :, ds(j, 1)].rearrange("p m u r t -> p m (u r t)"), ALU.add)\
                    .then_inc(s["c_s_yd"], 1)
                pool.wait_ge(s["c_s_x1"], n + 1)
                pool.wait_ge(s["c_ld_rows"], 32 * (n + 1))
                pool.wait_ge(s["c_s_z"], n)
                pool.tensor_tensor(c_xm[:, :], c_x1[:, :], c_rows[:, 0, :], ALU.mult).then_inc(s["c_s_xm"], 1)
                pool.wait_ge(s["c_s_mv"], n + 1)
                pool.tensor_tensor(c_ve[:, :], c_mv[:, 1:2], eps[:, 1:2], ALU.add).then_inc(s["c_s_ve"], 1)
                pool.wait_ge(s["c_s_ve"], n + 1)
                pool.tensor_tensor(c_rs[:, :], c_ve[:, :], half_pow[:, 0:1], ALU.pow).then_inc(s["c_s_rs"], 1)
                pool.wait_ge(s["c_s_f"], n + 1)
                pool.tensor_tensor(c_f2[:, :], c_f[:, 0, :], c_f[:, 1, :], ALU.add).then_inc(s["c_s_f2"], 1)
                pool.wait_ge(s["c_s_f2"], n + 1)
                pool.wait_ge(s["c_st"], 16 * n)
                pool.tensor_tensor(c_out[:, :], c_f2[:, :], c_x1[:, :], ALU.add).then_inc(s["c_s_out"], 1)

            with pool.Fori(0, PAIRS) as i:
                with pool.Fori(0, TPP) as j:
                    stage_a(i * TPP + j + 1)
                with pool.Fori(0, TPP) as j:
                    stage_c(i, j, i * TPP + j + 1)

        @block.tensor
        def _(pe):
            give_head_start(pe, "pe")
            banks = (ps_c1, ps_c2)
            pe.wait_ge(s["w_pool"], 16)
            pe.wait_ge(s["w_ld"], 16 * W_LOADS)
            for g, (moves, _, _) in enumerate(groups):
                if g >= 2:
                    pe.wait_ge(s["w_ev"], g - 1)
                for at, src in moves:
                    mm = pe.transpose(banks[g % 2][:, at:at + P], src, ident[:, :])
                mm.then_inc(s["w_tp"], 1)
            pe.wait_ge(s["w_cst"], 17 * 16)
            pe.wait_ge(s["w_ev"], NG)
            for m in range(MC):
                pe.transpose(ps_c1[:, m * NPROJ:(m + 1) * NPROJ], st_x[:, m * P:(m + 1) * P],
                             ident[0:NPROJ, 0:NPROJ])
            for m in range(MC):
                mm = pe.matmul(ps_c2[:, m * DS:(m + 1) * DS], st_dt[:, m * P:(m + 1) * P], wdtT[:, :],
                               start=True, stop=True)
            mm.then_inc(s["w_tp"], 1)
            pe.wait_ge(s["w_sq"], 2)
            for w in range(5):
                if w < 3:
                    dst = (ps_a, ps_y, ps_x[0][0])[w]
                    for c in range(KC):
                        for k in range(KC):
                            mm = pe.matmul(dst[:, c * B:(c + 1) * B], sq_l1[:, w, k, c * P:(c + 1) * P],
                                           sq_cond[:, k, :], start=(k == 0), stop=(k == KC - 1))
                else:
                    dst = (ps_x[0][1], ps_x[1][0])[w - 3]
                    for k in range(KC):
                        mm = pe.matmul(dst[:, 0:DM], sq_cond[:, KC + k, :], sq_l1[:, w, k, :],
                                       start=(k == 0), stop=(k == KC - 1))
                mm.then_inc(s["w_dp"], 1)
            pe.wait_ge(s["w_de"], 5)
            pe.wait_ge(s["w_ev"], NG + 2)

            def stage_a(n):
                pe.wait_ge(s["a_ld"], 16 * (n + 1))
                pe.wait_ge(s["a_s_bcT"], 2 * n)
                pe.wait_ge(s["a_s_xT"], n)
                for k in range(KC):
                    mm = pe.transpose(ps_a[:, k * TOK:(k + 1) * TOK], a_x[:, k * P:(k + 1) * P], ident[:, :])
                mm.then_inc(s["a_s_xTp"], 1)
                pe.wait_ge(s["a_s_xT"], n + 1)
                for m in range(MC):
                    for k in range(KC):
                        mm = pe.matmul(ps_a[:, m * TOK:(m + 1) * TOK], WinT[:, k, m * P:(m + 1) * P], a_xT[:, k, :],
                                       start=(k == 0), stop=(k == KC - 1))
                mm.then_inc(s["a_s_inp"], 1)
                pe.wait_ge(s["a_s_xc"], n + 1)
                pe.wait_ge(s["a_s_xr"], n + 1)
                for m in range(MC):
                    mm = pe.transpose(ps_a[:, m * P:(m + 1) * P], a_xc[:, m, :], ident[:, :])
                mm.then_inc(s["a_s_xcT"], 1)
                pe.wait_ge(s["a_s_xn"], n + 1)
                pe.wait_ge(s["a_s_z"], n + 1)
                for m in range(MC):
                    mm = pe.transpose(ps_a[:, m * TOK:(m + 1) * TOK], a_xn[:, m * P:(m + 1) * P], ident[:, :])
                mm.then_inc(s["a_s_xnTp"], 1)
                pe.wait_ge(s["a_s_xnT"], n + 1)
                for m in range(MC):
                    mm = pe.matmul(ps_a[:, 0:NPROJ], a_xnT[:, m, :], WxT[:, m, :], start=(m == 0), stop=(m == MC - 1))
                mm.then_inc(s["a_s_proj"], 1)
                pe.wait_ge(s["a_s_bc"], 2 * n + 2)
                pe.wait_ge(s["w_pool"], 16)
                pe.transpose(ps_a[:, 0:TOK], a_bc[:, :], ident[:, :]).then_inc(s["a_s_bcTp"], 1)

            def spread(sl, t, r):
                h, tt = t // HALF, t % HALF
                if tt == 0:
                    pe.wait_ge(s[f"b_ld_xs{h}"], 32 * (sl + 1))
                pe.wait_ge(s["b_u"], (sl * STEPS + t) * 2 + r + 1 - 4 + 4)
                mm = pe.matmul(ps_x[r][t % 2][:, :], sel[:, :], xs_sb[r][h][:, tt, :], start=True, stop=True)
                mm.then_inc(s["b_xrep"], 1)

            def read_out(i, j, t, r):
                step = (i * SLICES + j + 1) * STEPS + t
                pe.wait_ge(s["b_g"], step * 2 + r + 1)
                if t == 0 and r == 0:
                    pe.wait_ge(s["b_cm"], 4 * (i + 2))
                    pe.wait_ge(s["b_yev"], 2 * (i * SLICES + j + 1))
                for m in range(MC):
                    at = ((m * 2 + r) * STEPS + t) * TPP
                    mm = pe.matmul(ps_y[:, at:at + TPP], gc[r][:, t % RING, m * P:(m + 1) * P],
                                   cm[r][:, ds(j * STEPS + t, 1), :].rearrange("p u b -> p (u b)"),
                                   start=True, stop=True)
                mm.then_inc(s["b_ymm"], 1)

            def stage_b(i, j):
                sl = i * SLICES + j + 1
                for t in range(STEPS):
                    for r in range(2):
                        spread(sl, t, r)
                    if t >= 1:
                        for r in range(2):
                            read_out(i, j, t - 1, r)
                for r in range(2):
                    read_out(i, j, STEPS - 1, r)

            def stage_c(n):
                pe.wait_ge(s["c_ld_x"], 16 * (n + 1))
                pe.wait_ge(s["c_s_f"], n)
                pe.wait_ge(s["c_s_xT"], n)
                for k in range(KC):
                    mm = pe.transpose(ps_c1[:, k * TOK:(k + 1) * TOK], c_x[:, k * P:(k + 1) * P], ident[:, :])
                mm.then_inc(s["c_s_xTp"], 1)
                pe.wait_ge(s["c_s_xT"], n + 1)
                for m in range(MC):
                    for k in range(KC):
                        mm = pe.matmul(ps_c1[:, m * TOK:(m + 1) * TOK], WinT[:, k, DI + m * P:DI + (m + 1) * P],
                                       c_xT[:, k, :], start=(k == 0), stop=(k == KC - 1))
                mm.then_inc(s["c_s_gate"], 1)
                pe.wait_ge(s["c_s_yg"], n + 1)
                pe.wait_ge(s["c_s_oT"], n)
                for m in range(MC):
                    mm = pe.matmul(ps_c2[:, 0:DM], c_yg[:, m, :], WoutT[:, m, :], start=(m == 0), stop=(m == MC - 1))
                mm.then_inc(s["c_s_wout"], 1)
                pe.wait_ge(s["c_s_z"], n + 1)
                pe.wait_ge(s["c_s_sg"], n + 1)
                for k in range(KC):
                    mm = pe.transpose(ps_c1[:, k * TOK:(k + 1) * TOK], c_z[:, k * P:(k + 1) * P], ident[:, :])
                mm.then_inc(s["c_s_zTp"], 1)
                pe.wait_ge(s["c_s_zT"], 2 * n + 2)
                pe.wait_ge(s["c_s_x1"], n + 1)
                for o, w in ((0, 0), (KC, 2)):
                    for c in range(KC):
                        for k in range(KC):
                            mm = pe.matmul(ps_c2[:, (o + c) * TOK:(o + c + 1) * TOK], L1T[:, w, k, c * P:(c + 1) * P],
                                           c_zT[:, k, :], start=(k == 0), stop=(k == KC - 1))
                mm.then_inc(s["c_s_qv"], 1)
                for c in range(KC):
                    for k in range(KC):
                        mm = pe.matmul(ps_c1[:, c * TOK:(c + 1) * TOK], L1T[:, 1, k, c * P:(c + 1) * P],
                                       c_zT[:, k, :], start=(k == 0), stop=(k == KC - 1))
                mm.then_inc(s["c_s_k"], 1)
                pe.wait_ge(s["c_s_q"], n + 1)
                pe.wait_ge(s["c_s_vs"], n + 1)
                for r in range(2):
                    for k in range(KC):
                        mm = pe.matmul(ps_c2[:, r * DM:(r + 1) * DM],
                                       c_zz[:, k, r].rearrange("p a t -> p (a t)"),
                                       L1T[:, 2, k, :], start=(k == 0), stop=(k == KC - 1))
                mm.then_inc(s["c_s_v"], 1)
                for c, (bank, freed) in enumerate(((ps_c1, "c_s_kbd"), (ps_c2, "c_s_vbd"))):
                    pe.wait_ge(s[freed], n + 1)
                    for r in range(2):
                        mm = pe.matmul(bank[r * S:(r + 1) * S, :], c_q[:, c, r * S:(r + 1) * S],
                                       c_kbd[:, :, c, r * S:(r + 1) * S], start=True, stop=True)
                    mm.then_inc(s["c_s_sc"], 1)
                for c, bank in enumerate((ps_c1, ps_c2)):
                    pe.wait_ge(s["c_s_sub"], 2 * n + c + 1)
                    pe.wait_ge(s["c_s_e"], 2 * n + c + 1)
                    for pr_ in range(HPC // 2):
                        mm = pe.transpose(bank[:, pr_ * TOK:(pr_ + 1) * TOK], c_e[:, c, pr_ * P:(pr_ + 1) * P],
                                          ident[:, :])
                    mm.then_inc(s["c_s_pTp"], 1)
                pe.wait_ge(s["c_s_pT0"], n + 1)
                pe.wait_ge(s["c_s_pT1"], n + 1)
                for pair in range(HEADS // 2):
                    for r in range(2):
                        mm = pe.matmul(ps_c1[r * S:(r + 1) * S, pair * 2 * VW:(pair + 1) * 2 * VW],
                                       c_pT[:, pair // 4, pair % 4, r * S:(r + 1) * S],
                                       c_vbd[:, r, pair, :, :].rearrange("p a v -> p (a v)"), start=True, stop=True)
                mm.then_inc(s["c_s_pv"], 1)
                pe.wait_ge(s["c_s_o"], n + 1)
                for c in range(KC):
                    mm = pe.transpose(ps_c2[:, c * TOK:(c + 1) * TOK],
                                      c_o[:, c * HPC:(c + 1) * HPC, :].rearrange("p h d -> p (h d)"), ident[:, :])
                mm.then_inc(s["c_s_oTp"], 1)
                pe.wait_ge(s["c_s_oT"], n + 1)
                for a, (lhs, w) in enumerate(((c_oT, 3), (c_vsT, 4))):
                    for k in range(KC):
                        mm = pe.matmul(ps_c1[:, a * DM:(a + 1) * DM], lhs[:, k, :], L1T[:, w, k, :],
                                       start=(k == 0), stop=(k == KC - 1))
                mm.then_inc(s["c_s_fin"], 1)

            with pe.Fori(0, PAIRS) as i:
                with pe.Fori(0, TPP) as j:
                    stage_a(i * TPP + j + 1)
                with pe.Fori(0, SLICES) as j:
                    stage_b(i, j)
                with pe.Fori(0, TPP) as j:
                    stage_c(i * TPP + j + 1)

        @block.scalar
        def _(act):
            give_head_start(act, "act")
            banks = (ps_c1, ps_c2)
            for g, (_, dst, width) in enumerate(groups):
                act.wait_ge(s["w_tp"], g + 1)
                act.activation(dst, banks[g % 2][:, 0:width], ACT.Copy).then_inc(s["w_ev"], 1)
            act.wait_ge(s["w_tp"], NG + 1)
            act.activation(WxT[:, :, 0:2 * DS],
                           ps_c1[:, 0:MC * NPROJ].rearrange("p (m k) -> p m k", m=MC)[:, :, 0:2 * DS],
                           ACT.Copy).then_inc(s["w_ev"], 1)
            act.activation(WxT[:, :, 2 * DS:NPROJ], ps_c2[:, 0:MC * DS].rearrange("p (m k) -> p m k", m=MC),
                           ACT.Copy).then_inc(s["w_ev"], 1)
            act.wait_ge(s["w_cst"], 17 * 16)
            act.activation(a_col[:, 1:2], a_col[:, 0:1], ACT.Tanh).then_inc(s["w_a"], 1)
            act.wait_ge(s["w_ev"], NG + 2)
            act.activation(stage[:, 0:2560], L1T[:, :, :, :].rearrange("p w k o -> p (w k o)"), ACT.Square)\
                .then_inc(s["w_sq"], 1)
            act.activation(stage[:, 2560:3072], condT[:, :, :].rearrange("p m b -> p (m b)"), ACT.Square)\
                .then_inc(s["w_sq"], 1)

            def stage_a(n):
                act.wait_ge(s["a_s_xTp"], n + 1)
                act.wait_ge(s["a_s_inp"], n)
                act.activation(a_xT[:, :, :].rearrange("p k t -> p (k t)"), ps_a[:, 0:KC * TOK], ACT.Copy)\
                    .then_inc(s["a_s_xT"], 1)
                act.wait_ge(s["a_s_xr"], n + 1)
                act.wait_ge(s["a_s_xc"], n)
                for m in range(MC):
                    ins = act.activation(a_acc[:, m], a_xr[:, m, :, TAPS - 1:PADT], ACT.Identity,
                                         bias=conv_b[:, m:m + 1], scale=conv_w[:, m, TAPS - 1:TAPS])
                ins.then_inc(s["a_s_tap"], 1)
                act.wait_ge(s["a_s_conv"], 3 * n + 3)
                act.activation(a_th[:, :], a_acc[:, :, :, :].rearrange("p m r t -> p (m r t)"), ACT.Tanh, scale=0.5)\
                    .then_inc(s["a_s_th"], 1)
                act.wait_ge(s["a_s_xn"], n + 1)
                act.wait_ge(s["a_st"], 80 * n)
                act.wait_ge(s["a_s_r1"], n)
                act.activation(a_parts[:, 0, :], a_xn[:, :], ACT.Copy).then_inc(s["a_s_p1"], 1)
                act.wait_ge(s["a_s_nr"], n)
                act.activation(a_th[:, :], a_xn[:, :], ACT.Square, accum_out=a_ss[:, :]).then_inc(s["a_s_ss"], 1)
                act.wait_ge(s["a_s_r1"], n + 1)
                act.activation(a_parts[:, 1, :], a_r1[:, :], ACT.Copy).then_inc(s["a_s_p2"], 1)
                act.wait_ge(s["a_s_xnTp"], n + 1)
                act.wait_ge(s["a_s_proj"], n)
                act.wait_ge(s["a_s_dx"], n)
                act.activation(a_xnT[:, :, :].rearrange("p m t -> p (m t)"), ps_a[:, :], ACT.Copy)\
                    .then_inc(s["a_s_xnT"], 1)
                act.wait_ge(s["a_s_bcTp"], n + 1)
                act.wait_ge(s["a_st"], 80 * n)
                act.activation(a_bcT[0:2 * DS, :], ps_a[0:2 * DS, 0:TOK], ACT.Copy).then_inc(s["a_s_bcT"], 1)
                act.activation(a_bcT[2 * DS:NPROJ, :], ps_a[2 * DS:NPROJ, 0:TOK], ACT.Tanh,
                               bias=bdt_col[2 * DS:NPROJ, :]).then_inc(s["a_s_bcT"], 1)

            def stage_b(i, j):
                sl = i * SLICES + j + 1
                act.wait_ge(s["b_ymm"], 2 * STEPS * (sl + 1) + 2 * RING)
                act.wait_ge(s["c_s_yd"], i * TPP + 1)
                for r in range(2):
                    act.activation(yT[:, :, :, r, ds(j * STEPS, STEPS)].rearrange("p m b t -> p m t b"),
                                   ps_y[:, :].rearrange("p (m r t b) -> p m r t b", m=MC, r=2, t=STEPS)[:, :, r],
                                   ACT.Copy).then_inc(s["b_yev"], 1)

            def stage_c(n):
                act.wait_ge(s["c_s_xTp"], n + 1)
                act.wait_ge(s["c_s_gate"], n)
                act.activation(c_xT[:, :, :].rearrange("p k t -> p (k t)"), ps_c1[:, 0:KC * TOK], ACT.Copy)\
                    .then_inc(s["c_s_xT"], 1)
                act.wait_ge(s["c_s_gate"], n + 1)
                act.wait_ge(s["c_s_sg"], n)
                act.activation(c_th[:, :], ps_c1[:, :], ACT.Tanh, scale=0.5).then_inc(s["c_s_th"], 1)
                act.wait_ge(s["c_s_zTp"], n + 1)
                act.wait_ge(s["c_s_v"], n)
                act.activation(c_zT[:, :, :].rearrange("p k t -> p (k t)"), ps_c1[:, 0:KC * TOK], ACT.Copy)\
                    .then_inc(s["c_s_zT"], 1)
                act.activation(c_zz[:, :, :, :, :].rearrange("p k r a t -> p (k r) a t"),
                               ps_c1[:, 0:KC * TOK].rearrange("p (k t) -> p k t", t=S).unsqueeze(2)
                               .to_broadcast([P, 2 * KC, 2, S]), ACT.Copy).then_inc(s["c_s_zT"], 1)
                act.wait_ge(s["c_s_k"], n + 1)
                act.wait_ge(s["c_s_sc"], 2 * n)
                for h in range(HPC):
                    ins = act.activation(c_kbd[:, h, :, :].rearrange("p k t -> p (k t)"), ps_c1[:, 0:KC * TOK],
                                         ACT.Copy, scale=mask[:, h:h + 1])
                ins.then_inc(s["c_s_kbd"], 1)
                act.wait_ge(s["c_s_v"], n + 1)
                act.wait_ge(s["c_s_pv"], n)
                for r in range(2):
                    for a in range(2):
                        ins = act.activation(
                            c_vbd[a * S:(a + 1) * S, r, :, a, 0:HD],
                            ps_c2[a * S:(a + 1) * S, r * DM:(r + 1) * DM]
                            .rearrange("p (h a d) -> p h a d", a=2, d=HD)[:, :, a, :], ACT.Copy)
                ins.then_inc(s["c_s_vbd"], 1)
                for c in range(KC):
                    act.wait_ge(s["c_s_sub"], 2 * n + c + 1)
                    act.wait_ge(s["c_s_pTp"], 2 * n)
                    act.activation(c_e[:, c, :], c_s[:, c, :, :].rearrange("p h t -> p (h t)"), ACT.Exp)\
                        .then_inc(s["c_s_e"], 1)
                act.wait_ge(s["c_s_pTp"], 2 * n + 1)
                act.wait_ge(s["c_s_pv"], n)
                act.activation(c_pT[:, 0, :, :].rearrange("p a t -> p (a t)"), ps_c1[:, :], ACT.Copy)\
                    .then_inc(s["c_s_pT0"], 1)

            for w, src in enumerate((ps_a, ps_y, ps_x[0][0], ps_x[0][1], ps_x[1][0])):
                act.wait_ge(s["w_dp"], w + 1)
                act.activation(dco[:, w, :], src[:, 0:DM], ACT.Copy, bias=1e-8).then_inc(s["w_de"], 1)
            with act.Fori(0, PAIRS) as i:
                with act.Fori(0, TPP) as j:
                    stage_a(i * TPP + j + 1)
                with act.Fori(0, SLICES) as j:
                    stage_b(i, j)
                with act.Fori(0, TPP) as j:
                    stage_c(i * TPP + j + 1)

        @block.vector
        def _(dve):
            give_head_start(dve, "dve")
            dve.memset(a_xr[:, :, :, :], 0.0).then_inc(s["w_scale"], 1)
            dve.memset(c_vbd[:, :, :, :, :], 0.0).then_inc(s["w_scale"], 1)
            dve.memset(gu[0][:, 0:1], 0.0).then_inc(s["b_ymm"], 2 * RING)
            dve.memset(gu[1][:, 0:1], 0.0).then_inc(s["b_u"], 4)
            dve.memset(zeros[:, :], 0.0).then_inc(s["w_scale"], 1)
            dve.wait_ge(s["w_scale"], 3)
            for a in range(2):
                dve.memset(c_vbd[a * S:(a + 1) * S, :, :, a, HD:VW], 1.0).then_inc(s["w_scale"], 1)
            dve.wait_ge(s["w_a"], 1)
            dve.tensor_scalar(a_col[:, 1:2], a_col[:, 1:2], -0.01, None, ALU.mult).then_inc(s["w_scale"], 1)
            dve.wait_ge(s["w_dpow"], 1)
            dve.scalar_tensor_tensor(qk_scale[:, :, :].rearrange("p c b -> p (c b)"), dco[:, 0, :], HD ** -0.5,
                                     dco[:, 1, :], ALU.mult, ALU.mult).then_inc(s["w_scale"], 1)
            dve.tensor_tensor(v_scale[:, :, :].rearrange("p c b -> p (c b)"), dco[:, 2, :],
                              condT[:, KC:2 * KC, :].rearrange("p c b -> p (c b)"), ALU.mult)\
                .then_inc(s["w_scale"], 1)
            dve.wait_ge(s["w_scale"], 8)
            dve.wait_ge(s["w_bc"], 1)

            def stage_a(n):
                dve.wait_ge(s["a_s_inp"], n + 1)
                dve.wait_ge(s["a_s_tap"], n)
                dve.tensor_tensor(a_xr[:, :, :, TAPS - 1:PADT],
                                  ps_a[:, :].rearrange("p (m r t) -> p m r t", m=MC, r=2),
                                  condT[:, :, ds((n - 1) * 2, 2)].unsqueeze(3).to_broadcast([P, MC, 2, S]), ALU.add)\
                    .then_inc(s["a_s_xr"], 1)
                dve.wait_ge(s["a_s_tap"], n + 1)
                for tap in range(TAPS - 1):
                    if tap:
                        dve.wait_ge(s["a_s_conv"], 3 * n + tap)
                    for m in range(MC):
                        ins = dve.scalar_tensor_tensor(a_acc[:, m], a_xr[:, m, :, tap:tap + S],
                                                       conv_w[:, m, tap:tap + 1], a_acc[:, m], ALU.mult, ALU.add)
                    ins.then_inc(s["a_s_conv"], 1)
                dve.wait_ge(s["a_s_th"], n + 1)
                dve.wait_ge(s["a_s_xcT"], n)
                dve.scalar_tensor_tensor(a_xc[:, :, :].rearrange("p m t -> p (m t)"), a_th[:, :], 1.0,
                                         a_acc[:, :, :, :].rearrange("p m r t -> p (m r t)"), ALU.add, ALU.mult)\
                    .then_inc(s["a_s_xc"], 1)
                dve.wait_ge(s["a_s_xcT"], n + 1)
                dve.bn_stats(a_bn[:, :], ps_a[:, :]).then_inc(s["a_s_st"], 1)
                dve.wait_ge(s["a_s_st"], n + 1)
                dve.wait_ge(s["a_s_ve"], n)
                dve.sem_inc(s["a_s_seen"], 1)
                dve.bn_aggr(a_mv[:, :], a_bn[:, :]).then_inc(s["a_s_mv"], 1)
                dve.wait_ge(s["a_s_rs"], n + 1)
                dve.wait_ge(s["a_s_xg"], n)
                dve.tensor_scalar(a_z[:, :], ps_a[:, :], a_mv[:, 0:1], a_rs[:, :], ALU.subtract, ALU.mult)\
                    .then_inc(s["a_s_z"], 1)
                dve.wait_ge(s["a_s_nr"], n + 1)
                dve.tensor_scalar(a_nrm[:, 1:2], a_nrm[:, 0:1], 1.0, None, ALU.min).then_inc(s["a_s_nm"], 1)
                dve.wait_ge(s["a_s_proj"], n + 1)
                dve.wait_ge(s["a_s_nm"], n + 1)
                dve.wait_ge(s["a_s_bcTp"], n)
                dve.tensor_scalar(a_bc[:, 0:DS], ps_a[:, 0:DS], a_nrm[:, 1:2], None, ALU.mult).then_inc(s["a_s_bc"], 1)
                dve.tensor_copy(a_bc[:, DS:NPROJ], ps_a[:, DS:NPROJ]).then_inc(s["a_s_bc"], 1)

            def prep_b(i):
                dve.wait_ge(s["b_ld_raw"], 96 * (i + 2))
                dve.wait_ge(s["b_ymm"], 2 * S * i + 2 * STEPS + 2 * RING)
                for r in range(2):
                    dve.tensor_scalar(ad[r][:, :], raw[r][:, 2, :], a_col[:, 1:2], 1.0, ALU.mult, ALU.add)\
                        .then_inc(s["b_prep"], 1)
                dve.wait_ge(s["b_prep"], 14 * (i + 1) + 2)
                for r in range(2):
                    dve.tensor_tensor_scan(pr[r][:, :], ad[r][:, :], zeros[:, :], 1.0, ALU.mult, ALU.add)\
                        .then_inc(s["b_prep"], 1)
                dve.wait_ge(s["b_prep"], 14 * (i + 1) + 4)
                for r in range(2):
                    dve.reciprocal(rp[r][:, :], pr[r][:, :]).then_inc(s["b_prep"], 1)
                    dve.tensor_tensor(cp[r][:, :], raw[r][:, 1, :], pr[r][:, :], ALU.mult).then_inc(s["b_prep"], 1)
                dve.wait_ge(s["b_prep"], 14 * (i + 1) + 8)
                for r in range(2):
                    dve.tensor_scalar(hi[r][:, :], rp[r][:, :], CLIP, None, ALU.mult).then_inc(s["b_prep"], 1)
                    dve.tensor_scalar(lo[r][:, :], rp[r][:, :], -CLIP, None, ALU.mult).then_inc(s["b_prep"], 1)
                    dve.tensor_tensor(bd[r][:, :], raw[r][:, 0, :], rp[r][:, :], ALU.mult).then_inc(s["b_prep"], 1)
                    dve.tensor_tensor(cm[r][:, :, :], bcast_mid(cp[r][:, :], TPP),
                                      mask[:, :].unsqueeze(1).to_broadcast([P, S, TPP]), ALU.mult)\
                        .then_inc(s["b_cm"], 1)
                    dve.memset(gc[r][:, RING - 1, :], 0.0).then_inc(s["b_cm"], 1)

            def stage_b(i, j):
                sl = i * SLICES + j + 1
                dve.wait_ge(s["b_prep"], 14 * (i + 1) + 14)
                dve.wait_ge(s["b_cm"], 4 * (i + 2))
                for t in range(STEPS):
                    step = sl * STEPS + t
                    at = j * STEPS + t
                    for r in range(2):
                        dve.wait_ge(s["b_xrep"], 2 * step + r + 1)
                        if t:
                            dve.wait_ge(s["b_g"], 2 * step + r - 1)
                        else:
                            dve.wait_ge(s["b_g"], 2 * step)
                        dve.scalar_tensor_tensor(gu[r][:, :], ps_x[r][t % 2][:, :],
                                                 bd[r][:, ds(at, 1)], gc[r][:, (t - 1) % RING, :],
                                                 ALU.mult, ALU.add).then_inc(s["b_u"], 1)
                    for r in range(2):
                        dve.wait_ge(s["b_u"], 2 * step + r + 1 + 4)
                        dve.wait_ge(s["b_ymm"], 2 * step + r + 1)
                        dve.tensor_scalar(gc[r][:, t % RING, :], gu[r][:, :], hi[r][:, ds(at, 1)],
                                          lo[r][:, ds(at, 1)], ALU.min, ALU.max).then_inc(s["b_g"], 1)

            def stage_c(n):
                dve.wait_ge(s["c_s_th"], n + 1)
                dve.wait_ge(s["c_s_yg"], n)
                dve.scalar_tensor_tensor(c_sg[:, :], c_th[:, :], 1.0, ps_c1[:, :], ALU.add, ALU.mult)\
                    .then_inc(s["c_s_sg"], 1)
                dve.wait_ge(s["c_s_sg"], n + 1)
                dve.wait_ge(s["c_s_yd"], n + 1)
                dve.wait_ge(s["c_s_wout"], n)
                dve.tensor_tensor(c_yg[:, :, :].rearrange("p m t -> p (m t)"),
                                  c_yd[:, :, :].rearrange("p m t -> p (m t)"), c_sg[:, :], ALU.mult)\
                    .then_inc(s["c_s_yg"], 1)
                dve.wait_ge(s["c_s_wout"], n + 1)
                dve.wait_ge(s["c_s_out"], n)
                dve.scalar_tensor_tensor(c_x1[:, :], ps_c2[:, 0:DM], 0.5, c_x[:, :], ALU.mult, ALU.add)\
                    .then_inc(s["c_s_x1"], 1)
                dve.wait_ge(s["c_s_xm"], n + 1)
                dve.bn_stats(c_bn[:, :], c_xm[:, :]).then_inc(s["c_s_st"], 1)
                dve.wait_ge(s["c_s_st"], n + 1)
                dve.sem_inc(s["c_s_seen"], 1)
                dve.bn_aggr(c_mv[:, :], c_bn[:, :]).then_inc(s["c_s_mv"], 1)
                dve.wait_ge(s["c_s_rs"], n + 1)
                dve.wait_ge(s["c_s_zTp"], n)
                dve.tensor_scalar(c_z[:, :], c_xm[:, :], c_mv[:, 0:1], c_rs[:, :], ALU.subtract, ALU.mult)\
                    .then_inc(s["c_s_z"], 1)
                dve.wait_ge(s["c_s_qv"], n + 1)
                dve.wait_ge(s["c_s_sc"], 2 * n)
                dve.wait_ge(s["c_s_fin"], n)
                for dst, at, scale, done in ((c_q, 0, qk_scale, "c_s_q"), (c_vsT, KC * TOK, v_scale, "c_s_vs")):
                    dve.tensor_tensor(dst[:, :, :].rearrange("p c (r t) -> p c r t", r=2),
                                      ps_c2[:, at:at + KC * TOK].rearrange("p (c r t) -> p c r t", c=KC, r=2),
                                      scale[:, :, ds((n - 1) * 2, 2)].unsqueeze(3).to_broadcast([P, KC, 2, S]),
                                      ALU.mult).then_inc(s[done], 1)
                for c, bank in enumerate((ps_c1, ps_c2)):
                    sc = bank[:, :].rearrange("p (h t) -> p h t", h=HPC)
                    dve.wait_ge(s["c_s_sc"], 2 * n + c + 1)
                    dve.reduce_max(c_mx[:, c * HPC:(c + 1) * HPC], sc, AX_X).then_inc(s["c_s_mx"], 1)
                    dve.wait_ge(s["c_s_mx"], 2 * n + c + 1)
                    dve.wait_ge(s["c_s_e"], 2 * n)
                    dve.tensor_tensor(c_s[:, c], sc, bcast_mid(c_mx[:, c * HPC:(c + 1) * HPC], S), ALU.subtract)\
                        .then_inc(s["c_s_sub"], 1)
                dve.wait_ge(s["c_s_pTp"], 2 * n + 2)
                dve.wait_ge(s["c_s_pv"], n)
                dve.tensor_copy(c_pT[:, 1, :, :].rearrange("p a t -> p (a t)"), ps_c2[:, :]).then_inc(s["c_s_pT1"], 1)
                dve.wait_ge(s["c_s_pv"], n + 1)
                pv = ps_c1[:, 0:HEADS * VW].rearrange("p (h v) -> p h v", h=HEADS)
                dve.reciprocal(c_rc[:, :].unsqueeze(2), pv[:, :, HD:VW]).then_inc(s["c_s_rc"], 1)
                dve.wait_ge(s["c_s_rc"], n + 1)
                dve.wait_ge(s["c_s_oTp"], n)
                dve.tensor_tensor(c_o[:, :, :], pv[:, :, 0:HD], bcast_mid(c_rc[:, :], HD), ALU.mult)\
                    .then_inc(s["c_s_o"], 1)
                dve.wait_ge(s["c_s_oTp"], n + 1)
                dve.tensor_tensor(c_oT[:, :, :].rearrange("p c (r t) -> p c r t", r=2),
                                  ps_c2[:, 0:KC * TOK].rearrange("p (c r t) -> p c r t", c=KC, r=2),
                                  v_scale[:, :, ds((n - 1) * 2, 2)].unsqueeze(3).to_broadcast([P, KC, 2, S]),
                                  ALU.mult).then_inc(s["c_s_oT"], 1)
                dve.wait_ge(s["c_s_fin"], n + 1)
                dve.wait_ge(s["c_s_f2"], n)
                dve.tensor_tensor(c_f[:, :, :].rearrange("p w o -> p (w o)"), ps_c1[:, :],
                                  c_rows[:, 1:3, :].rearrange("p w o -> p (w o)"), ALU.mult).then_inc(s["c_s_f"], 1)

            with dve.Fori(0, PAIRS) as i:
                with dve.Fori(0, TPP) as j:
                    stage_a(i * TPP + j + 1)
                prep_b(i)
                with dve.Fori(0, SLICES) as j:
                    stage_b(i, j)
                with dve.Fori(0, TPP) as j:
                    stage_c(i * TPP + j + 1)


_INS = ['x', 'cond_2048', 'L0_cond_W_in', 'L0_cond_W_conv', 'L0_cond_b_conv', 'L0_cond_ln_g', 'L0_cond_ln_b',
        'L0_cond_W_xproj', 'L0_cond_W_dt', 'L0_cond_b_dt', 'L0_cond_A_log', 'L0_cond_D', 'L0_cond_W_out',
        'L1_cond_q_weight', 'L1_cond_k_weight', 'L1_cond_v_weight', 'L1_cond_w_weight', 'L1_cond_u_weight']
_OUTS = [((128, 64, 256), 'float32')]


def kernel(**inputs):
    import numpy as _np
    import concourse.bacc as _bacc
    from concourse import mybir as _mybir
    from concourse.bass_utils import run_bass_kernel_spmd as _run

    nc = _bacc.Bacc("TRN2", target_bir_lowering=False, num_devices=1)
    arrays, args = {}, []
    for name in _INS:
        a = _np.ascontiguousarray(inputs[name])
        arrays[f"in_{name}_dram"] = a
        args.append(nc.dram_tensor(f"in_{name}_dram", a.shape, _mybir.dt.from_np(a.dtype), kind="ExternalInput").ap())
    for i, (shape, dtype) in enumerate(_OUTS):
        dt = _mybir.dt.from_np(_np.dtype(dtype))
        args.append(nc.dram_tensor(f"out_{i}_dram", shape, dt, kind="ExternalOutput").ap())
    mamba_attention_kernel(nc, *args)
    r = _run(nc, [arrays], core_ids=[0])
    got = tuple(r.results[0][f"out_{i}_dram"] for i in range(len(_OUTS)))
    return got[0]
```

```python
from contextlib import ExitStack

import concourse.bass as bass
from concourse import mybir

F32 = mybir.dt.float32
BF16 = mybir.dt.bfloat16
ALU = mybir.AluOpType
ACT = mybir.ActivationFunctionType
AX_X = mybir.AxisListType.X
ds = bass.ds


def mamba_attention_kernel(nc, x, cond, W_in, W_conv, b_conv, ln_g, ln_b, W_xproj, W_dt, b_dt, A_log, D,
                           W_out, q_w, k_w, v_w, w_w, u_w, out):
    B, S, DM = x.shape
    DI = W_conv.shape[0]
    DS = A_log.shape[0]
    TAPS = W_conv.shape[2]
    P = 128
    TOK = 2 * S
    PAIRS = 8
    TPP = B // 2 // PAIRS
    MC = DI // P
    KC = DM // P
    HEADS = 16
    HD = DM // HEADS
    HPC = P // HD
    STEPS = 8
    SLICES = S // STEPS
    HALF = STEPS // 2
    PARTS = 3
    NPROJ = 3 * DS
    CLIP = 10.0
    VW = HD + 1
    assert TOK == P and TPP == 8 and TPP * DS == P and SLICES == TPP and HPC * HD == P

    ctx = ExitStack()
    with ctx:
        def sb(name, shape, dt=F32):
            return ctx.enter_context(nc.sbuf_tensor(name, shape, dt))

        def pb(name, shape=(P, 512), dt=F32):
            return ctx.enter_context(nc.psum_tensor(name, list(shape), dt))

        def sem(name):
            return ctx.enter_context(nc.semaphore(name))

        xs_dram = nc.dram_tensor("xn_parts", [PAIRS * SLICES, 2, PARTS * TPP, STEPS, DI], BF16).ap()
        bct_dram = nc.dram_tensor("b_c_dt", [PAIRS, 2, TPP, NPROJ, S], F32).ap()
        dx_dram = nc.dram_tensor("skip_d_xn", [PAIRS * TPP, TOK, DI], F32).ap()
        y_dram = nc.dram_tensor("scan_out", [PAIRS, TPP, 2, S, DI], F32).ap()
        row_dram = nc.dram_tensor("style_rows", [B, 3 * DM], F32).ap()

        ident = sb("ident", [P, P])
        sel = sb("sel", [P, P], BF16)
        mask = sb("mask", [P, HPC])
        neg_one = sb("neg_one", [P, 1])
        half_pow = sb("half_pow", [P, 2])
        eps = sb("eps", [P, 2])
        WinT = sb("WinT", [P, KC, 2 * DI])
        WoutT = sb("WoutT", [P, MC, DM])
        WxT = sb("WxT", [P, MC, NPROJ])
        L1T = sb("L1T", [P, 5, KC, DM])
        condT = sb("condT", [P, MC, B])
        qk_scale = sb("qk_scale", [P, KC, B])
        v_scale = sb("v_scale", [P, KC, B])
        conv_w = sb("conv_w", [P, MC, TAPS])
        d_row = sb("d_row", [P, DI])
        g_row = sb("g_row", [P, DI])
        b_row = sb("b_row", [P, DI])
        a_col = sb("a_col", [P, 2])
        bdt_col = sb("bdt_col", [NPROJ, 1])
        wdtT = sb("wdtT", [DS, DS])
        stage = sb("stage", [P, 7936])
        dco = stage[:, 6144:7424].rearrange("p (w o) -> p w o", w=5)
        cond_nat = stage[:, 7424:7936]
        dm_x = stage[:, 3072:4352]
        dm_t = stage[:, 4352:5632]

        st_in = stage[:, 0:2048].rearrange("p (c i) -> p c i", c=8)
        st_out = stage[:, 2048:3072].rearrange("p (c i) -> p c i", c=2)
        st_l1 = stage[:, 3072:5632].rearrange("p (w c i) -> p w c i", w=5, c=2)
        st_x = stage[0:NPROJ, 5632:6144]
        st_dt = sb("st_dt", [DS, DI])
        sq_l1 = stage[:, 0:2560].rearrange("p (w k o) -> p w k o", w=5, k=KC)
        sq_cond = stage[:, 2560:3072].rearrange("p (m b) -> p m b", m=MC)

        a_x = sb("a_x", [P, DM])
        a_xT = sb("a_xT", [P, KC, TOK])
        PADT = S + TAPS - 1
        a_xr = sb("a_xr", [P, MC, 2, PADT])
        conv_diag = sb("conv_diag", [P, MC, TAPS, P])
        bias_in = sb("bias_in", [P, DI], BF16)
        ones = sb("ones", [P, P], BF16)
        a_th = sb("a_th", [P, MC * TOK])
        a_xc = sb("a_xc", [P, MC, TOK])
        a_bn = sb("a_bn", [P, 6])
        a_mv = sb("a_mv", [P, 2])
        a_ve = sb("a_ve", [P, 1])
        a_nmu = sb("a_nmu", [P, 1])
        a_nb = sb("a_nb", [P, 1])
        a_rs = sb("a_rs", [P, 1])
        a_z = sb("a_z", [P, DI])
        a_xg = sb("a_xg", [P, DI])
        a_xn = sb("a_xn", [P, DI])
        a_r1 = sb("a_r1", [P, DI])
        a_parts = sb("a_parts", [P, PARTS, DI], BF16)
        a_ss = sb("a_ss", [P, 1])
        a_nrm = sb("a_nrm", [P, 2])
        a_xnT = sb("a_xnT", [P, MC, TOK])
        a_dx = sb("a_dx", [P, DI])
        a_bc = sb("a_bc", [P, P])
        a_bcT = sb("a_bcT", [NPROJ, TOK])

        xs_sb = sb("xs_sb", [P, HALF, DI], BF16)
        raw = [sb(f"raw_{r}", [P, 3, S]) for r in range(2)]
        ad = [sb(f"ad_{r}", [P, S]) for r in range(2)]
        pr = [sb(f"pr_{r}", [P, S]) for r in range(2)]
        rp = [sb(f"rp_{r}", [P, S]) for r in range(2)]
        hi = [sb(f"hi_{r}", [P, S]) for r in range(2)]
        lo = [sb(f"lo_{r}", [P, S]) for r in range(2)]
        bd = [sb(f"bd_{r}", [P, S]) for r in range(2)]
        cp = sb("cp", [P, 2, S])
        UNITS = STEPS // 2
        cms = sb("cms", [P, 2, 2, UNITS * 40])
        RING = 4
        gu = [sb(f"gu_{r}", [P, DI]) for r in range(2)]
        gc = [sb(f"gc_{r}", [P, RING, DI]) for r in range(2)]
        zeros = sb("zeros", [P, S])
        y_sb = sb("y_sb", [P, DI])

        band = gc[0][:, :, :].rearrange("p k (a m) -> p (k a) m", m=P)

        c_x = sb("c_x", [P, DM])
        c_dx = sb("c_dx", [P, DI])
        c_y = sb("c_y", [P, DI])
        c_s1 = sb("c_s1", [P, DM])
        c_wu = sb("c_wu", [P, 2, DM])
        c_xT = sb("c_xT", [P, KC, TOK])
        c_th = sb("c_th", [P, DI])
        c_sg = sb("c_sg", [P, DI])
        c_yd = sb("c_yd", [P, DI])
        c_yg = sb("c_yg", [P, DI])
        c_ygT = sb("c_ygT", [P, MC, TOK])
        c_x1 = sb("c_x1", [P, DM])
        c_xm = sb("c_xm", [P, DM])
        c_bn = sb("c_bn", [P, 6])
        c_mv = sb("c_mv", [P, 2])
        c_ve = sb("c_ve", [P, 1])
        c_nmu = sb("c_nmu", [P, 1])
        c_nb = sb("c_nb", [P, 1])
        c_rs = sb("c_rs", [P, 1])
        c_z = sb("c_z", [P, DM])
        c_zT = sb("c_zT", [P, KC, TOK])
        c_vd = sb("c_vd", [P, KC, 2, 2, S])
        c_q = sb("c_q", [P, KC, TOK])
        c_vsT = sb("c_vsT", [P, KC, TOK])
        c_kbd = sb("c_kbd", [P, HPC, KC, TOK])
        c_vbd = sb("c_vbd", [P, 2, HEADS // 2, 2, VW])
        c_mx = sb("c_mx", [P, HEADS])
        c_s = sb("c_s", [P, KC, HPC, S])
        c_e = sb("c_e", [P, KC, HPC * S])
        c_pT = sb("c_pT", [P, KC, HPC // 2, TOK])
        c_rc = sb("c_rc", [P, HEADS])
        c_o = sb("c_o", [P, HEADS, HD])
        c_oT = sb("c_oT", [P, KC, TOK])
        c_f = sb("c_f", [P, 2, DM])
        c_f2 = sb("c_f2", [P, DM])
        c_out = sb("c_out", [P, DM])

        ps_x = [[pb(f"ps_x_{r}_{h}") for h in range(2)] for r in range(2)]
        ps_y = pb("ps_y")
        ps_a = pb("ps_a")
        ps_c1 = pb("ps_c1")
        ps_c2 = pb("ps_c2")

        names = """w_ld w_cst w_tp w_ev w_sq w_dp w_de w_dpow w_scale w_row w_a w_pool w_bc w_diag w_bias w_dm
            a_ld a_st a_xTp a_xT a_inp a_xr a_conv a_th a_xc a_xcT a_st1 a_seen a_mv a_nmu a_ve a_rs a_nb
            a_z a_xg a_xn a_p1 a_r1 a_p2 a_p3 a_ss a_nr a_nm a_xnTp a_xnT a_dx a_proj a_bc a_bcTp a_bcT
            b_ld_raw b_prep b_cm b_ld_xs0 b_ld_xs1 b_spread b_u b_g b_read b_yev b_cms b_yst
            c_ld_x c_ld_dx c_ld_s1 c_ld_wu c_xTp c_xT c_gate c_th c_sg c_yd c_yg c_ygTp c_ygT c_ld_y c_wout c_x1 c_xm c_st1 c_seen
            c_mv c_nmu c_ve c_rs c_nb c_z c_zTp c_zT c_qv c_q c_vs c_k c_kbd c_vd c_vTp c_vbd c_sc
            c_mx c_sub c_e c_pTp c_pT c_pv c_rc c_o c_oTp c_oT c_fin c_f c_f2 c_out c_st""".split()
        s = {n: sem(n) for n in names}
        head_start = {
            "dve": """a_xr:1 a_xc:1 a_st1:1 a_mv:1 a_nm:1 a_bc:2 b_prep:14 b_cm:2 b_cms:2 b_u:20 b_g:16 c_sg:1 c_yg:1
                c_x1:1 c_st1:1 c_mv:1 c_q:1 c_vs:1 c_mx:2 c_sub:2 c_rc:1 c_o:1 c_f:1""",
            "pe": """a_xTp:1 a_inp:1 a_conv:1 a_xcT:1 a_xnTp:1 a_proj:1 a_bcTp:1 b_spread:16 b_read:16 c_xTp:1
                c_gate:1 c_ygTp:1 c_wout:1 c_zTp:1 c_qv:1 c_k:1 c_vTp:1 c_sc:2 c_pTp:2 c_pv:1 c_oTp:1 c_fin:1""",
            "act": """a_xT:1 a_th:1 a_z:1 a_p1:1 a_ss:1 a_p2:1 a_xnT:1 a_bcT:2 b_yev:1 c_xT:1 c_th:1 c_ygT:1 c_z:1 c_zT:1
                c_kbd:1 c_vd:1 c_vbd:1 c_e:2 c_pT:2 c_oT:1""",
            "pool": """a_nmu:1 a_ve:1 a_rs:1 a_nb:1 a_xg:1 a_xn:1 a_r1:1 a_p3:1 a_nr:1 a_dx:1 c_yd:1 c_xm:1
                c_nmu:1 c_ve:1 c_rs:1 c_nb:1 c_f2:1 c_out:1""",
            "sp": "a_ld:16 a_st:144 b_ld_raw:96 b_ld_xs0:32 b_ld_xs1:32 b_yst:64 c_ld_x:16 c_ld_dx:16 c_ld_y:16 c_ld_s1:32 c_ld_wu:32 c_st:16",
        }

        def give_head_start(eng, name):
            for item in head_start[name].split():
                which, count = item.split(":")
                eng.sem_inc(s[which], int(count))

        TILES = PAIRS * TPP
        A_LEAD = TPP + 1
        C1_LAG = TPP
        C2_LAG = TPP + 1
        C3_LAG = TPP + 2
        last = PAIRS - 1
        SEGMENTS = [(-2, 1, TPP - 1, 1, True, False, False, False, False),
                    (-1, 1, 0, TPP, True, False, False, False, False),
                    (0, 1, 0, TPP, True, True, False, False, False),
                    (1, 1, 0, 1, True, True, True, False, False), (1, 1, 1, 1, True, True, True, True, False),
                    (1, 1, 2, TPP - 2, True, True, True, True, True),
                    (2, PAIRS - 4, 0, TPP, True, True, True, True, True),
                    (last - 1, 1, 0, TPP - 1, True, True, True, True, True),
                    (last - 1, 1, TPP - 1, 1, False, True, True, True, True),
                    (last, 1, 0, TPP, False, True, True, True, True),
                    (last + 1, 1, 0, TPP, False, False, True, True, True),
                    (last + 2, 1, 0, 1, False, False, False, True, True),
                    (last + 2, 1, 1, 1, False, False, False, False, True)]

        def run(eng, slice_, before_scan=None, ahead=False):
            for i0, ni, j0, nj, *stages in SEGMENTS:
                def pair(i):
                    if stages[1] and j0 == 0 and before_scan and not ahead:
                        before_scan(i)
                    early = ahead and j0 + nj == TPP and i0 < last
                    inner = nj - 1 if early else nj
                    if inner == 1:
                        slice_(i, j0, *stages)
                    elif inner:
                        with eng.Fori(j0, j0 + inner) as j:
                            slice_(i, j, *stages)
                    if early:
                        if i0 >= -1:
                            before_scan(i + 1)
                        slice_(i, TPP - 1, *stages)
                if ni == 1:
                    pair(i0)
                else:
                    with eng.Fori(i0, i0 + ni) as i:
                        pair(i)

        block = ctx.enter_context(nc.Block())

        groups = []
        for k in range(KC):
            for h in range(2):
                groups.append(([(q * P, st_in[:, 4 * h + q, k * P:(k + 1) * P]) for q in range(4)],
                               WinT[:, k, h * 512:(h + 1) * 512]))
        for mp in range(2):
            groups.append(([((2 * a + c) * P, st_out[:, c, (2 * mp + a) * P:(2 * mp + a + 1) * P])
                            for a in range(2) for c in range(2)],
                           WoutT[:, 2 * mp:2 * mp + 2, :].rearrange("p a o -> p (a o)")))
        for w in range(5):
            groups.append(([((2 * k + c) * P, st_l1[:, w, c, k * P:(k + 1) * P]) for k in range(2) for c in range(2)],
                           L1T[:, w, :, :].rearrange("p k o -> p (k o)")))
        groups.append(([(m * P, cond_nat[:, m * P:(m + 1) * P]) for m in range(MC)],
                       condT[:, :, :].rearrange("p m b -> p (m b)")))
        NG = len(groups)
        W_LOADS = 5 + 3
        W_CONSTS = 8 + TPP
        W_POOL = 12

        def bcast_mid(ap, n):
            return ap.unsqueeze(2).to_broadcast([ap.shape[0], ap.shape[1], n])

        x_tok = x.rearrange("b t c -> (b t) c")
        o_tok = out.rearrange("b t c -> (b t) c")

        @block.sync
        def _(sp):
            sp.dma_start(st_in, W_in.rearrange("(c p) i -> p c i", p=P)).then_inc(s["w_ld"], 16)
            sp.dma_start(st_out, W_out.rearrange("(c p) i -> p c i", p=P)).then_inc(s["w_ld"], 16)
            for w, src in enumerate((q_w, k_w, v_w, w_w, u_w)):
                sp.dma_start(st_l1[:, w], src.rearrange("(c p) i -> p c i", p=P)).then_inc(s["w_ld"], 16)
            sp.dma_start(cond_nat[:, :], cond).then_inc(s["w_ld"], 16)
            sp.dma_start(st_x, W_xproj).then_inc(s["w_cst"], 16)
            sp.dma_start(st_dt[:, :], W_xproj[2 * DS:3 * DS, :]).then_inc(s["w_cst"], 16)
            sp.dma_start(wdtT[:, :], W_dt.rearrange("a b -> b a"), allow_slow_non_contiguous=True).then_inc(s["w_cst"], 16)
            sp.dma_start(d_row[:, :], D.partition_broadcast(P)).then_inc(s["w_cst"], 16)
            sp.dma_start(conv_w[:, :, :], W_conv.rearrange("(m p) o k -> p m (o k)", p=P),
                         allow_slow_non_contiguous=True).then_inc(s["w_cst"], 16)
            sp.dma_start(g_row[:, :], ln_g.partition_broadcast(P)).then_inc(s["w_cst"], 16)
            sp.dma_start(b_row[:, :], ln_b.partition_broadcast(P)).then_inc(s["w_cst"], 16)
            for j in range(TPP):
                sp.dma_start(a_col[j * DS:(j + 1) * DS, 0:1], A_log.unsqueeze(1),
                             allow_slow_non_contiguous=True).then_inc(s["w_cst"], 16)
            sp.dma_start(bdt_col[2 * DS:3 * DS, :], b_dt.unsqueeze(1),
                         allow_slow_non_contiguous=True).then_inc(s["w_cst"], 16)
            sp.dma_start(a_xg[:, :], b_conv.partition_broadcast(P)).then_inc(s["w_bc"], 16)
            give_head_start(sp, "sp")
            sp.dma_start(a_x[:, :], x_tok[0:TOK, :]).then_inc(s["a_ld"], 16)
            sp.wait_ge(s["w_ld"], 16 * W_LOADS)
            sp.dma_start(row_dram[:, 0:DM], cond_nat[:, 0:DM]).then_inc(s["w_row"], 16)
            sp.wait_ge(s["w_dpow"], 1)
            sp.dma_start(row_dram[:, DM:3 * DM], dco[:, 3:5, :].rearrange("p w o -> p (w o)")).then_inc(s["w_row"], 16)
            sp.wait_ge(s["w_row"], 32)

            def load_xs(sl, at, h):
                sp.wait_ge(s["b_spread"], 2 * STEPS * sl - (1 - h) * STEPS)
                for r in range(2):
                    quad = 32 * (2 * h + r)
                    sp.dma_start(xs_sb[quad:quad + PARTS * TPP, :, :],
                                 xs_dram[ds(at, 1), r, :, h * HALF:(h + 1) * HALF, :]
                                 .rearrange("o q t c -> (o q) t c")).then_inc(s[f"b_ld_xs{h}"], 16)

            def slice_(i, j, A, B_, C1, C2, C3):
                sl = i * SLICES + j
                if A:
                    a = sl + A_LEAD
                    na = a + 1
                    sp.wait_ge(s["a_xTp"], na + 1)
                    sp.dma_start(a_x[:, :], x_tok[ds((a + 1) % TILES * TOK, TOK), :]).then_inc(s["a_ld"], 16)
                if C1:
                    c = sl - C1_LAG
                    sp.wait_ge(s["c_yd"], c + 1)
                    sp.dma_start(c_dx[:, :], dx_dram[ds(c, 1)].rearrange("u p c -> (u p) c"))\
                        .then_inc(s["c_ld_dx"], 16)
                    sp.wait_ge(s["b_yst"], 64 * (SLICES * i + 1))
                    sp.dma_start(c_y[:, :], y_dram[ds(i - 1, 1), ds(j, 1)].rearrange("i j r t c -> (i j r t) c"))\
                        .then_inc(s["c_ld_y"], 16)
                if C2:
                    c = sl - C2_LAG
                    sp.wait_ge(s["c_f"], c + 1)
                    for r in range(2):
                        sp.dma_start(c_wu[r * S:(r + 1) * S, :, :].rearrange("p w o -> p (w o)"),
                                     row_dram[ds(c * 2 + r, 1), DM:3 * DM].to_broadcast([S, 2 * DM]))\
                            .then_inc(s["c_ld_wu"], 16)
                if C3:
                    c = sl - C3_LAG
                    sp.wait_ge(s["c_out"], c + 2)
                    sp.dma_start(o_tok[ds(c * TOK, TOK), :], c_out[:, :]).then_inc(s["c_st"], 16)
                if C1:
                    c = sl - C1_LAG
                    sp.wait_ge(s["c_xTp"], c + 1)
                    sp.wait_ge(s["c_x1"], c + 1)
                    sp.dma_start(c_x[:, :], x_tok[ds(c * TOK, TOK), :]).then_inc(s["c_ld_x"], 16)
                    sp.wait_ge(s["c_xm"], c + 1)
                    for r in range(2):
                        sp.dma_start(c_s1[r * S:(r + 1) * S, :],
                                     row_dram[ds(c * 2 + r, 1), 0:DM].to_broadcast([S, DM]))\
                            .then_inc(s["c_ld_s1"], 16)
                if B_:
                    if not (isinstance(i, int) and i == last):
                        sp.wait_ge(s["a_st"], 144 * (sl + A_LEAD + 1))
                    load_xs(sl + 2, (sl + 1) % TILES, 0)
                    load_xs(sl + 2, (sl + 1) % TILES, 1)
                if A:
                    sp.wait_ge(s["a_bcT"], 2 * na + 2)
                    for r in range(2):
                        sp.dma_start(bct_dram[ds(a // TPP, 1), r, ds(a % TPP, 1)].rearrange("o u k t -> (o u k) t"),
                                     a_bcT[:, r * S:(r + 1) * S]).then_inc(s["a_st"], 16)
                if B_:
                    sp.wait_ge(s["b_yev"], sl + 2)
                    for v in range(2):
                        for r in range(2):
                            quad = 32 * (2 * v + r)
                            sp.dma_start(y_dram[ds(i, 1), :, r, ds(j * STEPS + v, UNITS, 2), :]
                                         .rearrange("i b u c -> u (i b) c"),
                                         y_sb[quad:quad + 32, :]).then_inc(s["b_yst"], 16)
                if A:
                    sp.wait_ge(s["a_dx"], na + 1)
                    sp.dma_start(dx_dram[ds(a, 1)].rearrange("u p c -> (u p) c"), a_dx[:, :]).then_inc(s["a_st"], 16)
                    sp.wait_ge(s["a_p3"], na + 1)
                    sp.wait_ge(s["a_p2"], na + 1)
                    for r in range(2):
                        for q in range(PARTS):
                            sp.dma_start(xs_dram[ds(a // TPP * SLICES, SLICES), r, ds(a % TPP + q * TPP, 1), :, :]
                                         .rearrange("l o t c -> l (o t) c"),
                                         a_parts[r * S:(r + 1) * S, q, :]).then_inc(s["a_st"], 16)

            def before_scan(i):
                used, stored = sp.snap(14 * (i + 1)), sp.snap(144 * (TPP * (i + 1) + 1))
                sp.wait_ge(s["b_prep"], used)
                sp.wait_ge(s["a_st"], stored)
                for r in range(2):
                    for k in range(3):
                        sp.dma_start(raw[r][:, k, :],
                                     bct_dram[ds(i, 1), r].rearrange("o j (k d) t -> k (o j) d t", k=3)[k])\
                            .then_inc(s["b_ld_raw"], 16)
                if isinstance(i, int) and i == 0:
                    for h in range(2):
                        load_xs(1, 0, h)

            run(sp, slice_, before_scan, ahead=True)
            sp.wait_ge(s["c_st"], 16 * (TILES + 1))
            sp.wait_ge(s["a_st"], 144 * (TILES + 1))
            sp.wait_ge(s["a_ld"], 16 * (TILES + 2))
            sp.wait_ge(s["b_yst"], 64 * (TILES + 1))
            sp.wait_ge(s["b_ld_xs0"], 32 * (TILES + 2))
            sp.wait_ge(s["b_ld_xs1"], 32 * (TILES + 2))

        @block.gpsimd
        def _(pool):
            give_head_start(pool, "pool")
            pool.memset(ident[:, :], 0.0).then_inc(s["w_pool"], 1)
            pool.memset(mask[:, :], 1.0).then_inc(s["w_pool"], 1)
            pool.memset(band, 1.0).then_inc(s["w_pool"], 1)
            pool.memset(half_pow[:, 0:1], -0.5).then_inc(s["w_pool"], 1)
            pool.memset(half_pow[:, 1:2], 0.5).then_inc(s["w_pool"], 1)
            pool.memset(eps[:, 0:1], 4e-5)
            pool.memset(eps[:, 1:2], 1e-5)
            pool.memset(neg_one[:, :], -1.0)
            pool.memset(bias_in[:, :], 0.0).then_inc(s["w_bc"], 1)
            pool.memset(a_bc[:, :], 0.0).then_inc(s["w_bc"], 1)
            pool.wait_ge(s["w_pool"], 5)
            pool.affine_select(out=ident[:, :], in_=ident[:, :], compare_op=ALU.not_equal, fill=1.0, base=0,
                               pattern=[[-1, P]], channel_multiplier=1).then_inc(s["w_pool"], 1)
            pool.affine_select(out=mask[:, :], in_=mask[:, :], compare_op=ALU.is_ge, fill=0.0, base=0,
                               pattern=[[-HD, HPC]], channel_multiplier=1).then_inc(s["w_pool"], 1)
            pool.affine_select(out=band, in_=band, compare_op=ALU.is_ge, fill=0.0, base=0,
                               pattern=[[DS * TPP, P // TPP], [1, P]], channel_multiplier=-DS).then_inc(s["w_pool"], 1)
            pool.wait_ge(s["w_pool"], 8)
            pool.affine_select(out=mask[:, :], in_=mask[:, :], compare_op=ALU.is_ge, fill=0.0, base=HD - 1,
                               pattern=[[HD, HPC]], channel_multiplier=-1).then_inc(s["w_pool"], 1)
            pool.affine_select(out=band, in_=band, compare_op=ALU.is_ge, fill=0.0, base=DS - 1,
                               pattern=[[-DS * TPP, P // TPP], [-1, P]], channel_multiplier=DS).then_inc(s["w_pool"], 1)

            def a_norm(n):
                pool.wait_ge(s["a_mv"], n + 1)
                pool.wait_ge(s["a_nb"], n)
                pool.tensor_tensor(a_ve[:, :], a_mv[:, 1:2], eps[:, 0:1], ALU.add).then_inc(s["a_ve"], 1)
                pool.tensor_tensor(a_nmu[:, :], a_mv[:, 0:1], neg_one[:, :], ALU.mult).then_inc(s["a_nmu"], 1)
                pool.wait_ge(s["a_ve"], n + 1)
                pool.wait_ge(s["a_z"], n)
                pool.tensor_tensor(a_rs[:, :], a_ve[:, :], half_pow[:, 0:1], ALU.pow).then_inc(s["a_rs"], 1)
                pool.wait_ge(s["a_nmu"], n + 1)
                pool.wait_ge(s["a_rs"], n + 1)
                pool.tensor_tensor(a_nb[:, :], a_rs[:, :], a_nmu[:, :], ALU.mult).then_inc(s["a_nb"], 1)

            def a_affine(n):
                pool.wait_ge(s["a_z"], n + 1)
                pool.tensor_tensor(a_xg[:, :], a_z[:, :], g_row[:, :], ALU.mult).then_inc(s["a_xg"], 1)
                pool.wait_ge(s["a_xg"], n + 1)
                pool.wait_ge(s["a_xnTp"], n)
                pool.wait_ge(s["a_dx"], n)
                pool.wait_ge(s["a_ss"], n)
                pool.wait_ge(s["a_p1"], n)
                pool.tensor_tensor(a_xn[:, :], a_xg[:, :], b_row[:, :], ALU.add).then_inc(s["a_xn"], 1)

            def a_first_rest(n):
                pool.wait_ge(s["a_p1"], n + 1)
                pool.wait_ge(s["a_p2"], n)
                pool.tensor_tensor(a_r1[:, :], a_xn[:, :], a_parts[:, 0, :], ALU.subtract).then_inc(s["a_r1"], 1)

            def a_norm_root(n):
                pool.wait_ge(s["a_ss"], n + 1)
                pool.wait_ge(s["a_nm"], n)
                pool.tensor_tensor(a_nrm[:, 0:1], a_ss[:, :], half_pow[:, 1:2], ALU.pow).then_inc(s["a_nr"], 1)

            def a_second_rest(n):
                pool.wait_ge(s["a_p2"], n + 1)
                pool.wait_ge(s["a_st"], 144 * n)
                pool.wait_ge(s["a_r1"], n + 1)
                pool.tensor_tensor(a_parts[:, 2, :], a_r1[:, :], a_parts[:, 1, :], ALU.subtract).then_inc(s["a_p3"], 1)

            def a_skip(n):
                pool.wait_ge(s["a_st"], 144 * n)
                pool.tensor_tensor(a_dx[:, :], a_xn[:, :], d_row[:, :], ALU.mult).then_inc(s["a_dx"], 1)

            def c_sum_skip(n):
                pool.wait_ge(s["c_ld_dx"], 16 * (n + 1))
                pool.wait_ge(s["c_ld_y"], 16 * (n + 1))
                pool.wait_ge(s["c_yg"], n)
                pool.tensor_tensor(c_yd[:, :], c_dx[:, :], c_y[:, :], ALU.add).then_inc(s["c_yd"], 1)

            def c_style(n):
                pool.wait_ge(s["c_x1"], n + 1)
                pool.wait_ge(s["c_ld_s1"], 32 * (n + 1))
                pool.wait_ge(s["c_z"], n)
                pool.tensor_tensor(c_xm[:, :], c_x1[:, :], c_s1[:, :], ALU.mult).then_inc(s["c_xm"], 1)

            def c_norm(n):
                pool.wait_ge(s["c_mv"], n + 1)
                pool.wait_ge(s["c_nb"], n)
                pool.tensor_tensor(c_ve[:, :], c_mv[:, 1:2], eps[:, 1:2], ALU.add).then_inc(s["c_ve"], 1)
                pool.tensor_tensor(c_nmu[:, :], c_mv[:, 0:1], neg_one[:, :], ALU.mult).then_inc(s["c_nmu"], 1)
                pool.wait_ge(s["c_ve"], n + 1)
                pool.wait_ge(s["c_z"], n)
                pool.tensor_tensor(c_rs[:, :], c_ve[:, :], half_pow[:, 0:1], ALU.pow).then_inc(s["c_rs"], 1)
                pool.wait_ge(s["c_nmu"], n + 1)
                pool.wait_ge(s["c_rs"], n + 1)
                pool.tensor_tensor(c_nb[:, :], c_rs[:, :], c_nmu[:, :], ALU.mult).then_inc(s["c_nb"], 1)

            def c_final(n):
                pool.wait_ge(s["c_f"], n + 1)
                pool.tensor_tensor(c_f2[:, :], c_f[:, 0, :], c_f[:, 1, :], ALU.add).then_inc(s["c_f2"], 1)
                pool.wait_ge(s["c_f2"], n + 1)
                pool.wait_ge(s["c_st"], 16 * n)
                pool.tensor_tensor(c_out[:, :], c_f2[:, :], c_x1[:, :], ALU.add).then_inc(s["c_out"], 1)

            def slice_(i, j, A, B_, C1, C2, C3):
                sl = i * SLICES + j
                na, n1, n2, n3 = sl + A_LEAD + 1, sl - C1_LAG + 1, sl - C2_LAG + 1, sl - C3_LAG + 1
                if C3:
                    c_final(n3)
                if C2:
                    c_style(n2)
                    c_norm(n2)
                if C1:
                    c_sum_skip(n1)
                if A:
                    a_norm(na)
                    a_affine(na)
                    a_first_rest(na)
                    a_norm_root(na)
                    a_skip(na)
                    a_second_rest(na)

            run(pool, slice_)

        @block.tensor
        def _(pe):
            give_head_start(pe, "pe")
            banks = (ps_c1, ps_c2)
            pe.wait_ge(s["w_pool"], W_POOL)
            pe.wait_ge(s["w_ld"], 16 * W_LOADS)
            for g, (moves, _) in enumerate(groups):
                if g >= 2:
                    pe.wait_ge(s["w_ev"], g - 1)
                for at, src in moves:
                    mm = pe.transpose(banks[g % 2][:, at:at + P], src, ident[:, :])
                mm.then_inc(s["w_tp"], 1)
            pe.wait_ge(s["w_cst"], W_CONSTS * 16)
            pe.wait_ge(s["w_ev"], NG)
            for m in range(MC):
                pe.transpose(ps_c1[:, m * NPROJ:(m + 1) * NPROJ], st_x[:, m * P:(m + 1) * P],
                             ident[0:NPROJ, 0:NPROJ])
            for m in range(MC):
                mm = pe.matmul(ps_c2[:, m * DS:(m + 1) * DS], st_dt[:, m * P:(m + 1) * P], wdtT[:, :],
                               start=True, stop=True)
            mm.then_inc(s["w_tp"], 1)
            pe.wait_ge(s["w_sq"], 2)
            for w in range(5):
                if w < 3:
                    dst = (ps_a, ps_y, ps_x[0][0])[w]
                    for c in range(KC):
                        for k in range(KC):
                            mm = pe.matmul(dst[:, c * B:(c + 1) * B], sq_l1[:, w, k, c * P:(c + 1) * P],
                                           sq_cond[:, k, :], start=(k == 0), stop=(k == KC - 1))
                else:
                    dst = (ps_x[0][1], ps_x[1][0])[w - 3]
                    for k in range(KC):
                        mm = pe.matmul(dst[:, 0:DM], sq_cond[:, KC + k, :], sq_l1[:, w, k, :],
                                       start=(k == 0), stop=(k == KC - 1))
                mm.then_inc(s["w_dp"], 1)
            pe.wait_ge(s["w_de"], 5)
            pe.wait_ge(s["w_ev"], NG + 2)
            pe.wait_ge(s["w_diag"], 1)
            pe.wait_ge(s["w_bias"], 6)

            def a_transpose_x(n):
                pe.wait_ge(s["a_ld"], 16 * (n + 1))
                pe.wait_ge(s["a_bcT"], 2 * n)
                for k in range(KC):
                    mm = pe.transpose(ps_a[:, k * TOK:(k + 1) * TOK], a_x[:, k * P:(k + 1) * P], ident[:, :])
                mm.then_inc(s["a_xTp"], 1)

            def a_project_in(n):
                pe.wait_ge(s["a_xT"], n + 1)
                for m in range(MC):
                    for k in range(KC):
                        mm = pe.matmul(ps_a[:, m * TOK:(m + 1) * TOK], WinT[:, k, m * P:(m + 1) * P], a_xT[:, k, :],
                                       start=(k == 0), stop=(k == KC - 1))
                mm.then_inc(s["a_inp"], 1)

            def a_convolve(n):
                pe.wait_ge(s["a_xr"], n + 1)
                for m in range(MC):
                    dst = ps_a[:, m * TOK:(m + 1) * TOK]
                    for tap in range(TAPS):
                        pe.matmul(dst.rearrange("p (r t) -> p r t", r=2), conv_diag[:, m, tap, :],
                                  a_xr[:, m, :, tap:tap + S], start=(tap == 0), stop=False)
                    mm = pe.matmul(dst, bias_in[:, m * P:(m + 1) * P], ones[:, :], start=False, stop=True)
                mm.then_inc(s["a_conv"], 1)

            def a_transpose_xc(n):
                pe.wait_ge(s["a_xc"], n + 1)
                for m in range(MC):
                    mm = pe.transpose(ps_a[:, m * P:(m + 1) * P], a_xc[:, m, :], ident[:, :])
                mm.then_inc(s["a_xcT"], 1)

            def a_transpose_xn(n):
                pe.wait_ge(s["a_z"], n + 1)
                pe.wait_ge(s["a_xn"], n + 1)
                for m in range(MC):
                    mm = pe.transpose(ps_a[:, m * TOK:(m + 1) * TOK], a_xn[:, m * P:(m + 1) * P], ident[:, :])
                mm.then_inc(s["a_xnTp"], 1)

            def a_project_bc(n):
                pe.wait_ge(s["a_xnT"], n + 1)
                for m in range(MC):
                    mm = pe.matmul(ps_a[:, 0:NPROJ], a_xnT[:, m, :], WxT[:, m, :], start=(m == 0), stop=(m == MC - 1))
                mm.then_inc(s["a_proj"], 1)

            def a_transpose_bc(n):
                pe.wait_ge(s["a_bc"], 2 * n + 2)
                pe.transpose(ps_a[:, 0:TOK], a_bc[:, :], ident[:, :]).then_inc(s["a_bcTp"], 1)

            def spread(sl, t, r):
                h, tt = t // HALF, t % HALF
                if tt == 0:
                    pe.wait_ge(s[f"b_ld_xs{h}"], 32 * (sl + 1))
                pe.wait_ge(s["b_u"], (sl * STEPS + t) * 2 + r + 1)
                quad = 32 * (2 * h + r)
                pe.matmul(ps_x[r][t % 2][:, :], sel[quad:quad + PARTS * TPP, :], xs_sb[quad:quad + PARTS * TPP, tt, :],
                          start=True, stop=True).then_inc(s["b_spread"], 1)

            def read_out(sl, u):
                if u == 0:
                    pe.wait_ge(s["b_cms"], 2 * sl + 2)
                    pe.wait_ge(s["b_yev"], sl)
                pe.wait_ge(s["b_g"], (sl * STEPS + 2 * u + 2) * 2)
                for v in range(2):
                    for r in range(2):
                        quad = 32 * (2 * v + r)
                        pe.matmul(ps_y[quad:quad + 32, :], cms[:, v, r, 32 * u:32 * (u + 1)],
                                  gc[r][:, (2 * u + v) % RING, :], start=(u == 0), stop=(u == UNITS - 1))\
                            .then_inc(s["b_read"], 1)

            def c_transpose_x(n):
                pe.wait_ge(s["c_ld_x"], 16 * (n + 1))
                pe.wait_ge(s["c_pT"], 2 * n - 1)
                for k in range(KC):
                    mm = pe.transpose(ps_c1[:, k * TOK:(k + 1) * TOK], c_x[:, k * P:(k + 1) * P], ident[:, :])
                mm.then_inc(s["c_xTp"], 1)

            def c_project_gate(n):
                pe.wait_ge(s["c_xT"], n + 1)
                for k in range(KC):
                    mm = pe.matmul(ps_c1[:, :], c_xT[:, k, :], WinT[:, k, DI:2 * DI], start=(k == 0), stop=(k == KC - 1))
                mm.then_inc(s["c_gate"], 1)

            def c_transpose_yg(n):
                pe.wait_ge(s["c_yg"], n + 1)
                for m in range(MC):
                    mm = pe.transpose(ps_c1[:, m * TOK:(m + 1) * TOK], c_yg[:, m * P:(m + 1) * P], ident[:, :])
                mm.then_inc(s["c_ygTp"], 1)

            def c_project_out(n):
                pe.wait_ge(s["c_ygT"], n + 1)
                for m in range(MC):
                    mm = pe.matmul(ps_c1[:, 0:DM], c_ygT[:, m, :], WoutT[:, m, :], start=(m == 0), stop=(m == MC - 1))
                mm.then_inc(s["c_wout"], 1)

            def c_transpose_z(n):
                pe.wait_ge(s["c_z"], n + 1)
                for k in range(KC):
                    mm = pe.transpose(ps_c1[:, k * TOK:(k + 1) * TOK], c_z[:, k * P:(k + 1) * P], ident[:, :])
                mm.then_inc(s["c_zTp"], 1)

            def c_project_qv(n):
                pe.wait_ge(s["c_zT"], n + 1)
                pe.wait_ge(s["c_f"], n)
                for o, w in ((0, 0), (KC, 2)):
                    for c in range(KC):
                        for k in range(KC):
                            mm = pe.matmul(ps_c2[:, (o + c) * TOK:(o + c + 1) * TOK], L1T[:, w, k, c * P:(c + 1) * P],
                                           c_zT[:, k, :], start=(k == 0), stop=(k == KC - 1))
                mm.then_inc(s["c_qv"], 1)

            def c_project_k(n):
                pe.wait_ge(s["c_zT"], n + 1)
                for c in range(KC):
                    for k in range(KC):
                        mm = pe.matmul(ps_c1[:, c * TOK:(c + 1) * TOK], L1T[:, 1, k, c * P:(c + 1) * P],
                                       c_zT[:, k, :], start=(k == 0), stop=(k == KC - 1))
                mm.then_inc(s["c_k"], 1)

            def c_transpose_v(n):
                pe.wait_ge(s["c_vd"], n + 1)
                pe.wait_ge(s["c_q"], n + 1)
                for r in range(2):
                    for c in range(KC):
                        mm = pe.transpose(ps_c2[:, (r * KC + c) * P:(r * KC + c + 1) * P],
                                          c_vd[:, c, r].rearrange("p a t -> p (a t)"), ident[:, :])
                mm.then_inc(s["c_vTp"], 1)

            def c_scores(n, c):
                bank = (ps_c1, ps_c2)[c]
                pe.wait_ge(s["c_kbd"], n + 1)
                pe.wait_ge(s[("c_q", "c_vbd")[c]], n + 1)
                for r in range(2):
                    mm = pe.matmul(bank[r * S:(r + 1) * S, :], c_q[:, c, r * S:(r + 1) * S],
                                   c_kbd[:, :, c, r * S:(r + 1) * S], start=True, stop=True)
                mm.then_inc(s["c_sc"], 1)

            def c_transpose_p(n, c):
                bank = (ps_c1, ps_c2)[c]
                pe.wait_ge(s["c_e"], 2 * n + c + 1)
                for pair in range(HPC // 2):
                    mm = pe.transpose(bank[:, pair * TOK:(pair + 1) * TOK], c_e[:, c, pair * P:(pair + 1) * P],
                                      ident[:, :])
                mm.then_inc(s["c_pTp"], 1)

            def c_weigh_v(n):
                pe.wait_ge(s["c_pT"], 2 * n + 2)
                for pair in range(HEADS // 2):
                    for r in range(2):
                        mm = pe.matmul(ps_c2[r * S:(r + 1) * S, pair * 2 * VW:(pair + 1) * 2 * VW],
                                       c_pT[:, pair // 4, pair % 4, r * S:(r + 1) * S],
                                       c_vbd[:, r, pair, :, :].rearrange("p a v -> p (a v)"), start=True, stop=True)
                mm.then_inc(s["c_pv"], 1)

            def c_transpose_o(n):
                pe.wait_ge(s["c_o"], n + 1)
                for c in range(KC):
                    mm = pe.transpose(ps_c2[:, c * TOK:(c + 1) * TOK],
                                      c_o[:, c * HPC:(c + 1) * HPC, :].rearrange("p h d -> p (h d)"), ident[:, :])
                mm.then_inc(s["c_oTp"], 1)

            def c_project_wu(n):
                pe.wait_ge(s["c_oT"], n + 1)
                for a, (lhs, w) in enumerate(((c_oT, 3), (c_vsT, 4))):
                    for k in range(KC):
                        mm = pe.matmul(ps_c2[:, a * DM:(a + 1) * DM], lhs[:, k, :], L1T[:, w, k, :],
                                       start=(k == 0), stop=(k == KC - 1))
                mm.then_inc(s["c_fin"], 1)

            def slice_(i, j, A, B_, C1, C2, C3):
                sl = i * SLICES + j
                na, n1, n2, n3 = sl + A_LEAD + 1, sl - C1_LAG + 1, sl - C2_LAG + 1, sl - C3_LAG + 1

                def step(t):
                    if B_:
                        spread(sl + 1, t, 0)
                        spread(sl + 1, t, 1)
                if A:
                    a_transpose_x(na)
                step(0)
                if C3:
                    c_transpose_o(n3)
                if C2:
                    c_transpose_yg(n2)
                step(1)
                if C3:
                    c_project_wu(n3)
                if A:
                    a_project_in(na)
                step(2)
                if C2:
                    c_project_out(n2)
                step(3)
                if A:
                    a_convolve(na)
                step(4)
                if C2:
                    c_transpose_z(n2)
                if B_:
                    read_out(sl + 1, 0)
                if C2:
                    c_project_k(n2)
                if A:
                    a_transpose_xc(na)
                if C2:
                    c_project_qv(n2)
                step(5)
                step(6)
                if C2:
                    c_scores(n2, 0)
                    c_transpose_v(n2)
                step(7)
                if B_:
                    read_out(sl + 1, 1)
                if C2:
                    c_scores(n2, 1)
                    c_transpose_p(n2, 0)
                if A:
                    a_transpose_xn(na)
                if B_:
                    read_out(sl + 1, 2)
                if C1:
                    c_transpose_x(n1)
                if A:
                    a_project_bc(na)
                if C2:
                    c_transpose_p(n2, 1)
                if C1:
                    c_project_gate(n1)
                if C2:
                    c_weigh_v(n2)
                if A:
                    a_transpose_bc(na)
                if B_:
                    read_out(sl + 1, 3)
            run(pe, slice_)

        @block.scalar
        def _(act):
            give_head_start(act, "act")
            banks = (ps_c1, ps_c2)
            for g, (_, dst) in enumerate(groups):
                act.wait_ge(s["w_tp"], g + 1)
                act.activation(dst, banks[g % 2][:, :], ACT.Copy).then_inc(s["w_ev"], 1)
            act.wait_ge(s["w_tp"], NG + 1)
            act.activation(WxT[:, :, 0:2 * DS],
                           ps_c1[:, 0:MC * NPROJ].rearrange("p (m k) -> p m k", m=MC)[:, :, 0:2 * DS],
                           ACT.Copy).then_inc(s["w_ev"], 1)
            act.activation(WxT[:, :, 2 * DS:NPROJ], ps_c2[:, 0:MC * DS].rearrange("p (m k) -> p m k", m=MC),
                           ACT.Copy).then_inc(s["w_ev"], 1)
            act.wait_ge(s["w_cst"], W_CONSTS * 16)
            act.activation(a_col[:, 1:2], a_col[:, 0:1], ACT.Tanh).then_inc(s["w_a"], 1)
            act.wait_ge(s["w_ev"], NG + 2)
            act.activation(stage[:, 0:2560], L1T[:, :, :, :].rearrange("p w k o -> p (w k o)"), ACT.Square)\
                .then_inc(s["w_sq"], 1)
            act.activation(stage[:, 2560:3072], condT[:, :, :].rearrange("p m b -> p (m b)"), ACT.Square)\
                .then_inc(s["w_sq"], 1)
            for w, src in enumerate((ps_a, ps_y, ps_x[0][0], ps_x[0][1], ps_x[1][0])):
                act.wait_ge(s["w_dp"], w + 1)
                act.activation(dm_x[:, w * DM:(w + 1) * DM], src[:, 0:DM], ACT.Copy, bias=1e-8).then_inc(s["w_de"], 1)
            act.wait_ge(s["w_de"], 5)
            act.activation(dco[:, :, :].rearrange("p w o -> p (w o)"), dm_x, ACT.Sqrt).then_inc(s["w_de"], 1)

            def a_take_xT(n):
                act.wait_ge(s["a_xTp"], n + 1)
                act.wait_ge(s["a_inp"], n)
                act.activation(a_xT[:, :, :].rearrange("p k t -> p (k t)"), ps_a[:, 0:KC * TOK], ACT.Copy)\
                    .then_inc(s["a_xT"], 1)

            def a_tanh(n):
                act.wait_ge(s["a_conv"], n + 1)
                act.wait_ge(s["a_ss"], n)
                act.wait_ge(s["a_xc"], n)
                act.activation(a_th[:, :], ps_a[:, :], ACT.Tanh, scale=0.5).then_inc(s["a_th"], 1)

            def a_normalise(n):
                act.wait_ge(s["a_nb"], n + 1)
                act.wait_ge(s["a_st1"], n + 1)
                act.wait_ge(s["a_xg"], n)
                act.activation(a_z[:, :], ps_a[:, :], ACT.Identity, bias=a_nb[:, :], scale=a_rs[:, :])\
                    .then_inc(s["a_z"], 1)

            def a_first_part(n):
                act.wait_ge(s["a_xn"], n + 1)
                act.wait_ge(s["a_st"], 144 * n)
                act.wait_ge(s["a_r1"], n)
                act.activation(a_parts[:, 0, :], a_xn[:, :], ACT.Copy).then_inc(s["a_p1"], 1)

            def a_square_sum(n):
                act.wait_ge(s["a_xn"], n + 1)
                act.wait_ge(s["a_nr"], n)
                act.activation(a_th[:, :], a_xn[:, :], ACT.Square, accum_out=a_ss[:, :]).then_inc(s["a_ss"], 1)

            def a_second_part(n):
                act.wait_ge(s["a_r1"], n + 1)
                act.activation(a_parts[:, 1, :], a_r1[:, :], ACT.Copy).then_inc(s["a_p2"], 1)

            def a_take_xnT(n):
                act.wait_ge(s["a_xnTp"], n + 1)
                act.wait_ge(s["a_proj"], n)
                act.activation(a_xnT[:, :, :].rearrange("p m t -> p (m t)"), ps_a[:, :], ACT.Copy)\
                    .then_inc(s["a_xnT"], 1)

            def a_take_bcT(n):
                act.wait_ge(s["a_bcTp"], n + 1)
                act.wait_ge(s["a_st"], 144 * n)
                act.activation(a_bcT[0:2 * DS, :], ps_a[0:2 * DS, 0:TOK], ACT.Copy).then_inc(s["a_bcT"], 1)
                act.activation(a_bcT[2 * DS:NPROJ, :], ps_a[2 * DS:NPROJ, 0:TOK], ACT.Tanh,
                               bias=bdt_col[2 * DS:NPROJ, :]).then_inc(s["a_bcT"], 1)

            def b_take_y(sl):
                act.wait_ge(s["b_read"], 2 * STEPS * (sl + 1))
                act.wait_ge(s["b_yst"], 64 * sl)
                act.activation(y_sb[:, :], ps_y[:, :], ACT.Copy).then_inc(s["b_yev"], 1)

            def c_take_xT(n):
                act.wait_ge(s["c_xTp"], n + 1)
                act.wait_ge(s["c_gate"], n)
                act.activation(c_xT[:, :, :].rearrange("p k t -> p (k t)"), ps_c1[:, 0:KC * TOK], ACT.Copy)\
                    .then_inc(s["c_xT"], 1)

            def c_tanh(n):
                act.wait_ge(s["c_gate"], n + 1)
                act.wait_ge(s["c_sg"], n)
                act.activation(c_th[:, :], ps_c1[:, :], ACT.Tanh, scale=0.5).then_inc(s["c_th"], 1)

            def c_take_ygT(n):
                act.wait_ge(s["c_ygTp"], n + 1)
                act.wait_ge(s["c_wout"], n)
                act.activation(c_ygT[:, :, :].rearrange("p m t -> p (m t)"), ps_c1[:, :], ACT.Copy)\
                    .then_inc(s["c_ygT"], 1)

            def c_normalise(n):
                act.wait_ge(s["c_nb"], n + 1)
                act.wait_ge(s["c_zTp"], n)
                act.activation(c_z[:, :], c_xm[:, :], ACT.Identity, bias=c_nb[:, :], scale=c_rs[:, :])\
                    .then_inc(s["c_z"], 1)

            def c_take_zT(n):
                act.wait_ge(s["c_zTp"], n + 1)
                act.wait_ge(s["c_k"], n)
                act.activation(c_zT[:, :, :].rearrange("p k t -> p (k t)"), ps_c1[:, 0:KC * TOK], ACT.Copy)\
                    .then_inc(s["c_zT"], 1)

            def c_double_v(n):
                act.wait_ge(s["c_vs"], n + 1)
                act.wait_ge(s["c_vTp"], n)
                act.activation(c_vd[:, :, :, :, :].rearrange("p k r a t -> p (k r) a t"),
                               c_vsT[:, :, :].rearrange("p k (r t) -> p (k r) t", r=2).unsqueeze(2)
                               .to_broadcast([P, 2 * KC, 2, S]), ACT.Copy).then_inc(s["c_vd"], 1)

            def c_block_keys(n):
                act.wait_ge(s["c_k"], n + 1)
                act.wait_ge(s["c_sc"], 2 * n)
                for h in range(HPC):
                    ins = act.activation(c_kbd[:, h, :, :].rearrange("p k t -> p (k t)"), ps_c1[:, 0:KC * TOK],
                                         ACT.Copy, scale=mask[:, h:h + 1])
                ins.then_inc(s["c_kbd"], 1)

            def c_block_values(n):
                act.wait_ge(s["c_vTp"], n + 1)
                act.wait_ge(s["c_pv"], n)
                for r in range(2):
                    for a in range(2):
                        ins = act.activation(
                            c_vbd[a * S:(a + 1) * S, r, :, a, 0:HD],
                            ps_c2[a * S:(a + 1) * S, r * DM:(r + 1) * DM]
                            .rearrange("p (h a d) -> p h a d", a=2, d=HD)[:, :, a, :], ACT.Copy)
                ins.then_inc(s["c_vbd"], 1)

            def c_exp(n, c):
                act.wait_ge(s["c_sub"], 2 * n + c + 1)
                act.wait_ge(s["c_pTp"], 2 * n)
                act.activation(c_e[:, c, :], c_s[:, c, :, :].rearrange("p h t -> p (h t)"), ACT.Exp)\
                    .then_inc(s["c_e"], 1)

            def c_take_pT(n, c):
                act.wait_ge(s["c_pTp"], 2 * n + c + 1)
                act.wait_ge(s["c_pv"], n)
                act.activation(c_pT[:, c, :, :].rearrange("p a t -> p (a t)"), (ps_c1, ps_c2)[c][:, :], ACT.Copy)\
                    .then_inc(s["c_pT"], 1)

            def c_take_oT(n):
                act.wait_ge(s["c_oTp"], n + 1)
                act.wait_ge(s["c_fin"], n)
                act.activation(c_oT[:, :, :].rearrange("p c t -> p (c t)"), ps_c2[:, 0:KC * TOK], ACT.Copy)\
                    .then_inc(s["c_oT"], 1)

            def slice_(i, j, A, B_, C1, C2, C3):
                sl = i * SLICES + j
                na, n1, n2, n3 = sl + A_LEAD + 1, sl - C1_LAG + 1, sl - C2_LAG + 1, sl - C3_LAG + 1
                if C3:
                    c_take_oT(n3)
                if C2:
                    c_take_ygT(n2)
                if A:
                    a_take_xT(na)
                if C2:
                    c_normalise(n2)
                if A:
                    a_tanh(na)
                if C2:
                    c_take_zT(n2)
                    c_block_keys(n2)
                    c_double_v(n2)
                if A:
                    a_normalise(na)
                if C2:
                    c_block_values(n2)
                    c_exp(n2, 0)
                    c_take_pT(n2, 0)
                if A:
                    a_take_xnT(na)
                if C2:
                    c_exp(n2, 1)
                if C1:
                    c_take_xT(n1)
                if A:
                    a_first_part(na)
                if C2:
                    c_take_pT(n2, 1)
                if A:
                    a_square_sum(na)
                if C1:
                    c_tanh(n1)
                if A:
                    a_take_bcT(na)
                    a_second_part(na)
                if B_:
                    b_take_y(sl + 1)
            run(act, slice_)

        @block.vector
        def _(dve):
            dve.memset(a_xr[:, :, :, :], 0.0).then_inc(s["w_scale"], 1)
            dve.memset(c_vbd[:, :, :, :, :], 0.0).then_inc(s["w_scale"], 1)
            dve.memset(zeros[:, :], 0.0).then_inc(s["w_scale"], 1)
            dve.memset(cms[:, :, :, :], 0.0).then_inc(s["w_scale"], 1)
            dve.memset(ones[:, :], 1.0).then_inc(s["w_scale"], 1)
            give_head_start(dve, "dve")
            dve.wait_ge(s["w_scale"], 5)
            for a in range(2):
                dve.memset(c_vbd[a * S:(a + 1) * S, :, :, a, HD:VW], 1.0).then_inc(s["w_scale"], 1)
            dve.wait_ge(s["w_cst"], W_CONSTS * 16)
            dve.wait_ge(s["w_pool"], W_POOL - 2)
            dve.tensor_reduce(gc[1][:, 0, 0:P], band.rearrange("p g m -> p m g"), AX_X, ALU.add).then_inc(s["w_pool"], 1)
            dve.wait_ge(s["w_pool"], W_POOL - 1)
            dve.tensor_copy(sel[:, :], gc[1][:, 0, 0:P]).then_inc(s["w_pool"], 1)
            for m in range(MC):
                for tap in range(TAPS):
                    ins = dve.tensor_scalar(conv_diag[:, m, tap, :], ident[:, :], conv_w[:, m, tap:tap + 1], None,
                                            ALU.mult)
            ins.then_inc(s["w_diag"], 1)
            dve.wait_ge(s["w_bc"], 18)
            dve.tensor_copy(a_parts[:, 0, :], a_xg[:, :]).then_inc(s["w_bias"], 1)
            dve.wait_ge(s["w_bias"], 1)
            dve.tensor_tensor(a_r1[:, :], a_xg[:, :], a_parts[:, 0, :], ALU.subtract).then_inc(s["w_bias"], 1)
            dve.wait_ge(s["w_bias"], 2)
            dve.tensor_copy(a_parts[:, 1, :], a_r1[:, :]).then_inc(s["w_bias"], 1)
            dve.wait_ge(s["w_bias"], 3)
            dve.tensor_copy(bias_in[0:1, :], a_parts[0:1, 0, :]).then_inc(s["w_bias"], 1)
            dve.tensor_copy(bias_in[32:33, :], a_parts[32:33, 1, :]).then_inc(s["w_bias"], 1)
            dve.tensor_tensor(bias_in[64:65, :], a_r1[64:65, :], a_parts[64:65, 1, :], ALU.subtract)\
                .then_inc(s["w_bias"], 1)
            dve.wait_ge(s["w_a"], 1)
            dve.tensor_scalar(a_col[:, 1:2], a_col[:, 1:2], -0.01, None, ALU.mult).then_inc(s["w_scale"], 1)
            rsq = dco[:, :, :].rearrange("p w o -> p (w o)")
            dve.wait_ge(s["w_de"], 6)
            dve.reciprocal(rsq, rsq).then_inc(s["w_dm"], 1)
            for step in range(2):
                dve.wait_ge(s["w_dm"], 4 * step + 1)
                dve.tensor_tensor(dm_t, rsq, rsq, ALU.mult).then_inc(s["w_dm"], 1)
                dve.wait_ge(s["w_dm"], 4 * step + 2)
                dve.tensor_tensor(dm_t, dm_t, dm_x, ALU.mult).then_inc(s["w_dm"], 1)
                dve.wait_ge(s["w_dm"], 4 * step + 3)
                dve.tensor_scalar(dm_t, dm_t, -0.5, 1.5, ALU.mult, ALU.add).then_inc(s["w_dm"], 1)
                dve.wait_ge(s["w_dm"], 4 * step + 4)
                dve.tensor_tensor(rsq, rsq, dm_t, ALU.mult).then_inc(s["w_dm"], 1)
            dve.wait_ge(s["w_dm"], 9)
            dve.sem_inc(s["w_dpow"], 1)
            dve.scalar_tensor_tensor(qk_scale[:, :, :].rearrange("p c b -> p (c b)"), dco[:, 0, :], HD ** -0.5,
                                     dco[:, 1, :], ALU.mult, ALU.mult).then_inc(s["w_scale"], 1)
            dve.tensor_tensor(v_scale[:, :, :].rearrange("p c b -> p (c b)"), dco[:, 2, :],
                              condT[:, KC:2 * KC, :].rearrange("p c b -> p (c b)"), ALU.mult)\
                .then_inc(s["w_scale"], 1)
            dve.wait_ge(s["w_scale"], 10)

            def a_add_style(a, n):
                dve.wait_ge(s["a_inp"], n + 1)
                dve.wait_ge(s["a_conv"], n)
                dve.tensor_tensor(a_xr[:, :, :, TAPS - 1:PADT],
                                  ps_a[:, :].rearrange("p (m r t) -> p m r t", m=MC, r=2),
                                  condT[:, :, ds(a * 2, 2)].unsqueeze(3).to_broadcast([P, MC, 2, S]), ALU.add)\
                    .then_inc(s["a_xr"], 1)

            def a_silu(n):
                dve.wait_ge(s["a_th"], n + 1)
                dve.wait_ge(s["a_xcT"], n)
                dve.scalar_tensor_tensor(a_xc[:, :, :].rearrange("p m t -> p (m t)"), a_th[:, :], 1.0,
                                         ps_a[:, :], ALU.add, ALU.mult).then_inc(s["a_xc"], 1)

            def a_stats(n):
                dve.wait_ge(s["a_xcT"], n + 1)
                dve.bn_stats(a_bn[:, :], ps_a[:, :]).then_inc(s["a_st1"], 1)
                dve.wait_ge(s["a_ve"], n)
                dve.wait_ge(s["a_nmu"], n)
                dve.wait_ge(s["a_st1"], n + 1)
                dve.sem_inc(s["a_seen"], 1)
                dve.bn_aggr(a_mv[:, :], a_bn[:, :]).then_inc(s["a_mv"], 1)

            def a_bound_norm(n):
                dve.wait_ge(s["a_nr"], n + 1)
                dve.tensor_scalar(a_nrm[:, 1:2], a_nrm[:, 0:1], 1.0, None, ALU.min).then_inc(s["a_nm"], 1)

            def a_scale_b(n):
                dve.wait_ge(s["a_proj"], n + 1)
                dve.wait_ge(s["a_nm"], n + 1)
                dve.wait_ge(s["a_bcTp"], n)
                dve.tensor_copy(a_bc[:, DS:NPROJ], ps_a[:, DS:NPROJ]).then_inc(s["a_bc"], 1)
                dve.tensor_scalar(a_bc[:, 0:DS], ps_a[:, 0:DS], a_nrm[:, 1:2], None, ALU.mult).then_inc(s["a_bc"], 1)

            def prep_b(i):
                dve.wait_ge(s["b_ld_raw"], 96 * (i + 2))
                for r in range(2):
                    dve.tensor_scalar(ad[r][:, :], raw[r][:, 2, :], a_col[:, 1:2], 1.0, ALU.mult, ALU.add)\
                        .then_inc(s["b_prep"], 1)
                dve.wait_ge(s["b_prep"], 14 * (i + 1) + 2)
                for r in range(2):
                    dve.tensor_tensor_scan(pr[r][:, :], ad[r][:, :], zeros[:, :], 1.0, ALU.mult, ALU.add)\
                        .then_inc(s["b_prep"], 1)
                dve.wait_ge(s["b_prep"], 14 * (i + 1) + 4)
                for r in range(2):
                    dve.reciprocal(rp[r][:, :], pr[r][:, :]).then_inc(s["b_prep"], 1)
                    dve.tensor_tensor(cp[:, r, :], raw[r][:, 1, :], pr[r][:, :], ALU.mult).then_inc(s["b_prep"], 1)
                dve.wait_ge(s["b_prep"], 14 * (i + 1) + 8)
                for r in range(2):
                    dve.tensor_scalar(hi[r][:, :], rp[r][:, :], CLIP, None, ALU.mult).then_inc(s["b_prep"], 1)
                    dve.tensor_scalar(lo[r][:, :], rp[r][:, :], -CLIP, None, ALU.mult).then_inc(s["b_prep"], 1)
                    dve.tensor_tensor(bd[r][:, :], raw[r][:, 0, :], rp[r][:, :], ALU.mult).then_inc(s["b_prep"], 1)
                dve.wait_ge(s["b_read"], 2 * S * i + 2 * STEPS)
                for r in range(2):
                    dve.memset(gc[r][:, RING - 1, :], 0.0).then_inc(s["b_cm"], 1)

            def scan_add(sl, at, t, r):
                step = sl * STEPS + t
                dve.wait_ge(s["b_spread"], 2 * step + r + 1)
                dve.wait_ge(s["b_g"], 2 * step + r - 1)
                dve.scalar_tensor_tensor(gu[r][:, :], ps_x[r][t % 2][:, :], bd[r][:, ds(at, 1)],
                                         gc[r][:, (t - 1) % RING, :], ALU.mult, ALU.add).then_inc(s["b_u"], 1)

            def scan_clip(sl, at, t, r):
                step = sl * STEPS + t
                dve.wait_ge(s["b_u"], 2 * step + r + 1 + 4)
                dve.wait_ge(s["b_read"], 2 * STEPS * sl + 4 * (t // 2) - 4)
                dve.tensor_scalar(gc[r][:, t % RING, :], gu[r][:, :], hi[r][:, ds(at, 1)],
                                  lo[r][:, ds(at, 1)], ALU.min, ALU.max).then_inc(s["b_g"], 1)

            def spread_c(i, j):
                sl = i * SLICES + j + 1
                dve.wait_ge(s["b_read"], 2 * STEPS * sl)
                for v in range(2):
                    dve.tensor_tensor(
                        cms[:, v].rearrange("p r (u c) -> p r u c", c=40)[:, :, :, 0:TPP],
                        cp[:, :, ds(j * STEPS + v, UNITS, 2)].unsqueeze(3).to_broadcast([P, 2, UNITS, TPP]),
                        mask[:, :].unsqueeze(1).unsqueeze(1).to_broadcast([P, 2, UNITS, TPP]), ALU.mult)\
                        .then_inc(s["b_cms"], 1)

            def c_silu(n):
                dve.wait_ge(s["c_th"], n + 1)
                dve.wait_ge(s["c_yg"], n)
                dve.scalar_tensor_tensor(c_sg[:, :], c_th[:, :], 1.0, ps_c1[:, :], ALU.add, ALU.mult)\
                    .then_inc(s["c_sg"], 1)

            def c_gate_product(n):
                dve.wait_ge(s["c_sg"], n + 1)
                dve.wait_ge(s["c_yd"], n + 1)
                dve.wait_ge(s["c_ygTp"], n)
                dve.tensor_tensor(c_yg[:, :], c_yd[:, :], c_sg[:, :], ALU.mult).then_inc(s["c_yg"], 1)

            def c_residual(n):
                dve.wait_ge(s["c_wout"], n + 1)
                dve.wait_ge(s["c_out"], n)
                dve.scalar_tensor_tensor(c_x1[:, :], ps_c1[:, 0:DM], 0.5, c_x[:, :], ALU.mult, ALU.add)\
                    .then_inc(s["c_x1"], 1)

            def c_stats(n):
                dve.wait_ge(s["c_xm"], n + 1)
                dve.bn_stats(c_bn[:, :], c_xm[:, :]).then_inc(s["c_st1"], 1)
                dve.wait_ge(s["c_ve"], n)
                dve.wait_ge(s["c_nmu"], n)
                dve.wait_ge(s["c_st1"], n + 1)
                dve.sem_inc(s["c_seen"], 1)
                dve.bn_aggr(c_mv[:, :], c_bn[:, :]).then_inc(s["c_mv"], 1)

            def c_scale_qv(c, n):
                dve.wait_ge(s["c_qv"], n + 1)
                dve.wait_ge(s["c_sc"], 2 * n)
                dve.wait_ge(s["c_fin"], n)
                for dst, at, scale, done in ((c_vsT, KC * TOK, v_scale, "c_vs"), (c_q, 0, qk_scale, "c_q")):
                    dve.tensor_tensor(dst[:, :, :].rearrange("p c (r t) -> p c r t", r=2),
                                      ps_c2[:, at:at + KC * TOK].rearrange("p (c r t) -> p c r t", c=KC, r=2),
                                      scale[:, :, ds(c * 2, 2)].unsqueeze(3).to_broadcast([P, KC, 2, S]),
                                      ALU.mult).then_inc(s[done], 1)

            def c_sub_max(n, c):
                sc = (ps_c1, ps_c2)[c][:, :].rearrange("p (h t) -> p h t", h=HPC)
                dve.wait_ge(s["c_sc"], 2 * n + c + 1)
                dve.reduce_max(c_mx[:, c * HPC:(c + 1) * HPC], sc, AX_X).then_inc(s["c_mx"], 1)
                dve.wait_ge(s["c_mx"], 2 * n + c + 1)
                dve.wait_ge(s["c_e"], 2 * n)
                dve.tensor_tensor(c_s[:, c], sc, bcast_mid(c_mx[:, c * HPC:(c + 1) * HPC], S), ALU.subtract)\
                    .then_inc(s["c_sub"], 1)

            def c_divide(n):
                pv = ps_c2[:, 0:HEADS * VW].rearrange("p (h v) -> p h v", h=HEADS)
                dve.wait_ge(s["c_pv"], n + 1)
                dve.reciprocal(c_rc[:, :].unsqueeze(2), pv[:, :, HD:VW]).then_inc(s["c_rc"], 1)
                dve.wait_ge(s["c_rc"], n + 1)
                dve.wait_ge(s["c_oTp"], n)
                dve.tensor_tensor(c_o[:, :, :], pv[:, :, 0:HD], bcast_mid(c_rc[:, :], HD), ALU.mult)\
                    .then_inc(s["c_o"], 1)

            def c_demodulate(n):
                dve.wait_ge(s["c_fin"], n + 1)
                dve.wait_ge(s["c_f2"], n)
                dve.wait_ge(s["c_ld_wu"], 32 * (n + 1))
                dve.tensor_tensor(c_f[:, :, :].rearrange("p w o -> p (w o)"), ps_c2[:, :],
                                  c_wu[:, :, :].rearrange("p w o -> p (w o)"), ALU.mult).then_inc(s["c_f"], 1)

            def slice_(i, j, A, B_, C1, C2, C3):
                sl = i * SLICES + j
                a, c2 = sl + A_LEAD, sl - C2_LAG
                na, n1, n2, n3 = a + 1, sl - C1_LAG + 1, c2 + 1, sl - C3_LAG + 1
                if B_:
                    dve.wait_ge(s["b_prep"], 14 * (i + 1) + 14)
                    dve.wait_ge(s["b_cm"], 2 * (i + 2))
                if B_:
                    scan_add(sl + 1, j * STEPS + 0, 0, 0)
                    scan_add(sl + 1, j * STEPS + 0, 0, 1)
                    scan_clip(sl + 1, j * STEPS + 0, 0, 0)
                    spread_c(i, j)
                    scan_clip(sl + 1, j * STEPS + 0, 0, 1)
                    scan_add(sl + 1, j * STEPS + 1, 1, 0)
                if C3:
                    c_demodulate(n3)
                if B_:
                    scan_add(sl + 1, j * STEPS + 1, 1, 1)
                    scan_clip(sl + 1, j * STEPS + 1, 1, 0)
                if A:
                    a_add_style(a, na)
                if B_:
                    scan_clip(sl + 1, j * STEPS + 1, 1, 1)
                    scan_add(sl + 1, j * STEPS + 2, 2, 0)
                if C2:
                    c_residual(n2)
                if B_:
                    scan_add(sl + 1, j * STEPS + 2, 2, 1)
                    scan_clip(sl + 1, j * STEPS + 2, 2, 0)
                if C2:
                    c_stats(n2)
                if B_:
                    scan_clip(sl + 1, j * STEPS + 2, 2, 1)
                    scan_add(sl + 1, j * STEPS + 3, 3, 0)
                    scan_add(sl + 1, j * STEPS + 3, 3, 1)
                    scan_clip(sl + 1, j * STEPS + 3, 3, 0)
                    scan_clip(sl + 1, j * STEPS + 3, 3, 1)
                if A:
                    a_silu(na)
                if B_:
                    scan_add(sl + 1, j * STEPS + 4, 4, 0)
                    scan_add(sl + 1, j * STEPS + 4, 4, 1)
                if A:
                    a_stats(na)
                if B_:
                    scan_clip(sl + 1, j * STEPS + 4, 4, 0)
                    scan_clip(sl + 1, j * STEPS + 4, 4, 1)
                if C2:
                    c_scale_qv(c2, n2)
                if B_:
                    scan_add(sl + 1, j * STEPS + 5, 5, 0)
                    scan_add(sl + 1, j * STEPS + 5, 5, 1)
                if C2:
                    c_sub_max(n2, 0)
                if B_:
                    scan_clip(sl + 1, j * STEPS + 5, 5, 0)
                    scan_clip(sl + 1, j * STEPS + 5, 5, 1)
                if C2:
                    c_sub_max(n2, 1)
                if B_:
                    scan_add(sl + 1, j * STEPS + 6, 6, 0)
                    scan_add(sl + 1, j * STEPS + 6, 6, 1)
                    scan_clip(sl + 1, j * STEPS + 6, 6, 0)
                    scan_clip(sl + 1, j * STEPS + 6, 6, 1)
                    scan_add(sl + 1, j * STEPS + 7, 7, 0)
                    scan_add(sl + 1, j * STEPS + 7, 7, 1)
                    scan_clip(sl + 1, j * STEPS + 7, 7, 0)
                if A:
                    a_bound_norm(na)
                if B_:
                    scan_clip(sl + 1, j * STEPS + 7, 7, 1)
                if C1:
                    c_silu(n1)
                if A:
                    a_scale_b(na)
                if C2:
                    c_divide(n2)
                if C1:
                    c_gate_product(n1)
            run(dve, slice_, prep_b)


_INS = ['x', 'cond_2048', 'L0_cond_W_in', 'L0_cond_W_conv', 'L0_cond_b_conv', 'L0_cond_ln_g', 'L0_cond_ln_b',
        'L0_cond_W_xproj', 'L0_cond_W_dt', 'L0_cond_b_dt', 'L0_cond_A_log', 'L0_cond_D', 'L0_cond_W_out',
        'L1_cond_q_weight', 'L1_cond_k_weight', 'L1_cond_v_weight', 'L1_cond_w_weight', 'L1_cond_u_weight']
_OUTS = [((128, 64, 256), 'float32')]


def kernel(**inputs):
    import numpy as _np
    import concourse.bacc as _bacc
    from concourse import mybir as _mybir
    from concourse.bass_utils import run_bass_kernel_spmd as _run

    nc = _bacc.Bacc("TRN2", target_bir_lowering=False, num_devices=1)
    arrays, args = {}, []
    for name in _INS:
        a = _np.ascontiguousarray(inputs[name])
        arrays[f"in_{name}_dram"] = a
        args.append(nc.dram_tensor(f"in_{name}_dram", a.shape, _mybir.dt.from_np(a.dtype), kind="ExternalInput").ap())
    for i, (shape, dtype) in enumerate(_OUTS):
        dt = _mybir.dt.from_np(_np.dtype(dtype))
        args.append(nc.dram_tensor(f"out_{i}_dram", shape, dt, kind="ExternalOutput").ap())
    mamba_attention_kernel(nc, *args)
    r = _run(nc, [arrays], core_ids=[0])
    got = tuple(r.results[0][f"out_{i}_dram"] for i in range(len(_OUTS)))
    return got[0]
```

```python
from contextlib import ExitStack

import concourse.bass as bass
from concourse import mybir

F32 = mybir.dt.float32
BF16 = mybir.dt.bfloat16
ALU = mybir.AluOpType
ACT = mybir.ActivationFunctionType
AX_X = mybir.AxisListType.X
ds = bass.ds


def mamba_attention_kernel(nc, x, cond, W_in, W_conv, b_conv, ln_g, ln_b, W_xproj, W_dt, b_dt, A_log, D,
                           W_out, q_w, k_w, v_w, w_w, u_w, out):
    B, S, DM = x.shape
    DI = W_conv.shape[0]
    DS = A_log.shape[0]
    TAPS = W_conv.shape[2]
    P = 128
    TOK = 2 * S
    PAIRS = 8
    TPP = B // 2 // PAIRS
    MC = DI // P
    KC = DM // P
    HEADS = 16
    HD = DM // HEADS
    HPC = P // HD
    STEPS = 8
    SLICES = S // STEPS
    HALF = STEPS // 2
    PARTS = 3
    NPROJ = 3 * DS
    CLIP = 10.0
    VW = HD + 1
    assert TOK == P and TPP == 8 and TPP * DS == P and SLICES == TPP and HPC * HD == P

    ctx = ExitStack()
    with ctx:
        def sb(name, shape, dt=F32):
            return ctx.enter_context(nc.sbuf_tensor(name, shape, dt))

        def pb(name, shape=(P, 512), dt=F32):
            return ctx.enter_context(nc.psum_tensor(name, list(shape), dt))

        def sem(name):
            return ctx.enter_context(nc.semaphore(name))

        xs_dram = nc.dram_tensor("xn_parts", [PAIRS * SLICES, 2, PARTS * TPP, STEPS, DI], BF16).ap()
        bct_dram = nc.dram_tensor("b_c_dt", [PAIRS, 2, TPP, NPROJ, S], F32).ap()
        dx_dram = nc.dram_tensor("skip_d_xn", [PAIRS * TPP, TOK, DI], F32).ap()
        y_dram = nc.dram_tensor("scan_out", [PAIRS, TPP, 2, S, DI], F32).ap()
        row_dram = nc.dram_tensor("style_rows", [B, 3 * DM], F32).ap()

        ident = sb("ident", [P, P])
        sel = sb("sel", [P, P], BF16)
        table_in = sb("table_in", [P, 1])
        mask = sb("mask", [P, HPC])
        neg_one = sb("neg_one", [P, 1])
        half_pow = sb("half_pow", [P, 2])
        eps = sb("eps", [P, 2])
        WinT = sb("WinT", [P, KC, 2 * DI])
        WoutT = sb("WoutT", [P, MC, DM])
        WxT = sb("WxT", [P, MC, NPROJ])
        L1T = sb("L1T", [P, 5, KC, DM])
        condT = sb("condT", [P, MC, B])
        qk_scale = sb("qk_scale", [P, KC, B])
        v_scale = sb("v_scale", [P, KC, B])
        conv_w = sb("conv_w", [P, MC, TAPS])
        d_row = sb("d_row", [P, DI])
        g_row = sb("g_row", [P, DI])
        b_row = sb("b_row", [P, DI])
        a_col = sb("a_col", [P, 2])
        bdt_col = sb("bdt_col", [NPROJ, 1])
        wdtT = sb("wdtT", [DS, DS])
        stage = sb("stage", [P, 7936])
        dco = stage[:, 6144:7424].rearrange("p (w o) -> p w o", w=5)
        cond_nat = stage[:, 7424:7936]
        dm_x = stage[:, 3072:4352]
        dm_t = stage[:, 4352:5632]

        st_in = stage[:, 0:2048].rearrange("p (c i) -> p c i", c=8)
        st_out = stage[:, 2048:3072].rearrange("p (c i) -> p c i", c=2)
        st_l1 = stage[:, 3072:5632].rearrange("p (w c i) -> p w c i", w=5, c=2)
        st_x = stage[0:NPROJ, 5632:6144]
        st_dt = sb("st_dt", [DS, DI])
        sq_l1 = stage[:, 0:2560].rearrange("p (w k o) -> p w k o", w=5, k=KC)
        sq_cond = stage[:, 2560:3072].rearrange("p (m b) -> p m b", m=MC)

        a_x = sb("a_x", [P, DM])
        a_xT = sb("a_xT", [P, KC, TOK])
        PADT = S + TAPS - 1
        a_xr = sb("a_xr", [P, MC, 2, PADT])
        conv_diag = sb("conv_diag", [P, MC, TAPS, P])
        bias_in = sb("bias_in", [P, DI], BF16)
        ones = sb("ones", [P, P], BF16)
        a_th = sb("a_th", [P, MC * TOK])
        a_xc = sb("a_xc", [P, MC, TOK])
        a_bn = sb("a_bn", [P, 6])
        a_mv = sb("a_mv", [P, 2])
        a_ve = sb("a_ve", [P, 1])
        a_nmu = sb("a_nmu", [P, 1])
        a_nb = sb("a_nb", [P, 1])
        a_rs = sb("a_rs", [P, 1])
        a_z = sb("a_z", [P, DI])
        a_xg = sb("a_xg", [P, DI])
        a_xn = sb("a_xn", [P, DI])
        a_r1 = sb("a_r1", [P, DI])
        a_parts = sb("a_parts", [P, PARTS, DI], BF16)
        a_ss = sb("a_ss", [P, 1])
        a_nrm = sb("a_nrm", [P, 2])
        a_xnT = sb("a_xnT", [P, MC, TOK])
        a_dx = sb("a_dx", [P, DI])
        a_bc = sb("a_bc", [P, P])
        a_bcT = sb("a_bcT", [NPROJ, TOK])

        xs_sb = sb("xs_sb", [P, HALF, DI], BF16)
        raw = sb("raw", [P, 3, 2, S])
        ad = sb("ad", [P, 2, S])
        pr = sb("pr", [P, 2, S])
        rp = sb("rp", [P, 2, S])
        hi = sb("hi", [P, 2, S])
        lo = sb("lo", [P, 2, S])
        bd = sb("bd", [P, 2, S])
        cp = sb("cp", [P, 2, S])
        UNITS = STEPS // 2
        cms = sb("cms", [P, 2, 2, UNITS * 40])
        RING = 4
        gu = [sb(f"gu_{r}", [P, DI]) for r in range(2)]
        gc = [sb(f"gc_{r}", [P, RING, DI]) for r in range(2)]
        zeros = sb("zeros", [P, S])
        y_sb = sb("y_sb", [P, DI])

        band = gc[0][:, :, :].rearrange("p k (a m) -> p (k a) m", m=P)

        c_x = sb("c_x", [P, DM])
        c_dx = sb("c_dx", [P, DI])
        c_y = sb("c_y", [P, DI])
        c_s1 = sb("c_s1", [P, DM])
        c_wu = sb("c_wu", [P, 2, DM])
        c_xT = sb("c_xT", [P, KC, TOK])
        c_th = sb("c_th", [P, DI])
        c_sg = sb("c_sg", [P, DI])
        c_yd = sb("c_yd", [P, DI])
        c_yg = sb("c_yg", [P, DI])
        c_ygT = sb("c_ygT", [P, MC, TOK])
        c_x1 = sb("c_x1", [P, DM])
        c_kept = sb("c_kept", [P, DM])
        c_xm = sb("c_xm", [P, DM])
        c_bn = sb("c_bn", [P, 6])
        c_mv = sb("c_mv", [P, 2])
        c_ve = sb("c_ve", [P, 1])
        c_nmu = sb("c_nmu", [P, 1])
        c_nb = sb("c_nb", [P, 1])
        c_rs = sb("c_rs", [P, 1])
        c_z = sb("c_z", [P, DM])
        c_zT = sb("c_zT", [P, KC, TOK])
        c_vd = sb("c_vd", [P, KC, 2, 2, S])
        c_q = sb("c_q", [P, KC, TOK])
        c_vsT = sb("c_vsT", [P, KC, TOK])
        c_kbd = sb("c_kbd", [P, HPC, KC, TOK])
        c_vbd = sb("c_vbd", [P, 2, HEADS // 2, 2, VW])
        c_mx = sb("c_mx", [P, HEADS])
        c_s = sb("c_s", [P, KC, HPC, S])
        c_e = sb("c_e", [P, KC, HPC * S])
        c_pT = sb("c_pT", [P, KC, HPC // 2, TOK])
        c_rc = sb("c_rc", [P, HEADS])
        c_o = sb("c_o", [P, HEADS, HD])
        c_oT = sb("c_oT", [P, KC, TOK])
        c_f = sb("c_f", [P, 2, DM])
        c_f2 = sb("c_f2", [P, DM])
        c_out = sb("c_out", [P, DM])

        ps_x = [[pb(f"ps_x_{r}_{h}") for h in range(2)] for r in range(2)]
        ps_y = pb("ps_y")
        ps_a = pb("ps_a")
        ps_c1 = pb("ps_c1")
        ps_c2 = pb("ps_c2")

        names = """w_ld w_cst w_tp w_ev w_sq w_dp w_de w_dpow w_scale w_row w_a w_pool w_bc w_diag w_bias w_dm
            a_ld a_st a_xTp a_xT a_inp a_xr a_conv a_th a_xc a_xcT a_st1 a_seen a_mv a_nmu a_ve a_rs a_nb
            a_z a_xg a_xn a_p1 a_r1 a_p2 a_p3 a_ss a_nr a_nm a_xnTp a_xnT a_dx a_proj a_bc a_bcTp a_bcT
            b_ld_raw b_prep b_zero b_ld_xs0 b_ld_xs1 b_spread b_u b_g b_read b_yev b_cms b_yst
            c_ld_x c_ld_dx c_ld_s1 c_ld_wu c_xTp c_xT c_gate c_th c_sg c_yd c_yg c_ygTp c_ygT c_ld_y c_wout c_x1 c_xm c_st1 c_seen
            c_mv c_nmu c_ve c_rs c_nb c_z c_zTp c_zT c_qv c_q c_vs c_k c_kbd c_vd c_vTp c_vbd c_sc
            c_mx c_sub c_e c_pTp c_pT c_pv c_rc c_o c_oTp c_oT c_fin c_f c_f2 c_out c_st c_keep b_seen a_st_dx""".split()
        s = {n: sem(n) for n in names}
        head_start = {
            "dve": """a_xr:1 a_xc:1 a_st1:1 a_mv:1 a_nm:1 a_bc:2 b_prep:8 b_cms:2 b_u:20 b_g:16 c_sg:1 c_yg:1
                c_x1:1 c_st1:1 c_mv:1 c_q:1 c_vs:1 c_mx:2 c_sub:2 c_rc:1 c_o:1 c_f:1""",
            "pe": """a_xTp:1 a_inp:1 a_conv:1 a_xcT:1 a_xnTp:1 a_proj:1 a_bcTp:1 b_spread:16 b_read:16 c_xTp:1
                c_gate:1 c_ygTp:1 c_wout:1 c_zTp:1 c_qv:1 c_k:1 c_vTp:1 c_sc:2 c_pTp:2 c_pv:1 c_oTp:1 c_fin:1""",
            "act": """a_xT:1 a_th:1 a_z:1 a_p1:1 a_ss:1 a_p2:1 a_xnT:1 a_bcT:2 b_yev:1 c_xT:1 c_th:1 c_ygT:1 c_z:1 c_zT:1
                c_kbd:1 c_keep:1 c_vd:1 c_vbd:1 c_e:2 c_pT:2 c_oT:1""",
            "pool": """b_zero:2 a_nmu:1 a_ve:1 a_rs:1 a_nb:1 a_xg:1 a_xn:1 a_r1:1 a_p3:1 a_nr:1 a_dx:1 c_yd:1 c_xm:1
                c_nmu:1 c_ve:1 c_rs:1 c_nb:1 c_f2:1 c_out:1""",
            "sp": "a_ld:16 a_st:128 a_st_dx:16 b_ld_raw:96 b_ld_xs0:32 b_ld_xs1:32 b_yst:64 c_ld_x:16 c_ld_dx:16 c_ld_y:16 c_ld_s1:32 c_ld_wu:32 c_st:16",
        }

        def give_head_start(eng, name):
            for item in head_start[name].split():
                which, count = item.split(":")
                eng.sem_inc(s[which], int(count))

        TILES = PAIRS * TPP
        A_LEAD = TPP + 1
        C1_LAG = TPP
        C2_LAG = TPP + 1
        C3_LAG = TPP + 2
        last = PAIRS - 1
        SEGMENTS = [(0, 1, 0, TPP, True, False, False, False),
                    (1, 1, 0, 1, True, True, False, False), (1, 1, 1, 1, True, True, True, False),
                    (1, 1, 2, TPP - 2, True, True, True, True), (2, PAIRS - 4, 0, TPP, True, True, True, True),
                    (last - 1, 1, 0, TPP - 1, True, True, True, True),
                    (last - 1, 1, TPP - 1, 1, False, True, True, True), (last, 1, 0, TPP, False, True, True, True)]

        def nothing():
            pass

        def run(eng, fill, slice_, drain, before_scan=None, ahead=False, after_first=nothing, before_last=nothing):
            fill(0, True, False)
            after_first()
            with eng.Fori(1, A_LEAD) as t:
                fill(t, True, True)
            before_last()
            if ahead:
                before_scan(0)
            fill(A_LEAD, False, True)
            for i0, ni, j0, nj, *stages in SEGMENTS:
                def pair(i):
                    if j0 == 0 and before_scan and not ahead:
                        before_scan(i)
                    early = ahead and j0 + nj == TPP and i0 < last
                    inner = nj - 1 if early else nj
                    if inner == 1:
                        slice_(i, j0, *stages)
                    elif inner:
                        with eng.Fori(j0, j0 + inner) as j:
                            slice_(i, j, *stages)
                    if early:
                        before_scan(i + 1)
                        slice_(i, TPP - 1, *stages)
                if ni == 1:
                    pair(i0)
                else:
                    with eng.Fori(i0, i0 + ni) as i:
                        pair(i)
            with eng.Fori(0, TPP) as j:
                drain(last + 1, j, True, True, True)
            drain(last + 2, 0, False, True, True)
            drain(last + 2, 1, False, False, True)

        block = ctx.enter_context(nc.Block())

        groups = []
        for k in range(KC):
            for h in range(2):
                groups.append(([(q * P, st_in[:, 4 * h + q, k * P:(k + 1) * P]) for q in range(4)],
                               WinT[:, k, h * 512:(h + 1) * 512]))
        for mp in range(2):
            groups.append(([((2 * a + c) * P, st_out[:, c, (2 * mp + a) * P:(2 * mp + a + 1) * P])
                            for a in range(2) for c in range(2)],
                           WoutT[:, 2 * mp:2 * mp + 2, :].rearrange("p a o -> p (a o)")))
        for w in range(5):
            groups.append(([((2 * k + c) * P, st_l1[:, w, c, k * P:(k + 1) * P]) for k in range(2) for c in range(2)],
                           L1T[:, w, :, :].rearrange("p k o -> p (k o)")))
        groups.append(([(m * P, cond_nat[:, m * P:(m + 1) * P]) for m in range(MC)],
                       condT[:, :, :].rearrange("p m b -> p (m b)")))
        NG = len(groups)
        W_LOADS = 5 + 3
        W_CONSTS = 8 + TPP
        W_POOL = 12

        def bcast_mid(ap, n):
            return ap.unsqueeze(2).to_broadcast([ap.shape[0], ap.shape[1], n])

        x_tok = x.rearrange("b t c -> (b t) c")
        o_tok = out.rearrange("b t c -> (b t) c")

        @block.sync
        def _(sp):
            sp.dma_start(st_in, W_in.rearrange("(c p) i -> p c i", p=P)).then_inc(s["w_ld"], 16)
            sp.dma_start(st_out, W_out.rearrange("(c p) i -> p c i", p=P)).then_inc(s["w_ld"], 16)
            for w, src in enumerate((q_w, k_w, v_w, w_w, u_w)):
                sp.dma_start(st_l1[:, w], src.rearrange("(c p) i -> p c i", p=P)).then_inc(s["w_ld"], 16)
            sp.dma_start(cond_nat[:, :], cond).then_inc(s["w_ld"], 16)
            sp.dma_start(st_x, W_xproj).then_inc(s["w_cst"], 16)
            sp.dma_start(st_dt[:, :], W_xproj[2 * DS:3 * DS, :]).then_inc(s["w_cst"], 16)
            sp.dma_start(wdtT[:, :], W_dt.rearrange("a b -> b a"), allow_slow_non_contiguous=True).then_inc(s["w_cst"], 16)
            sp.dma_start(d_row[:, :], D.partition_broadcast(P)).then_inc(s["w_cst"], 16)
            sp.dma_start(conv_w[:, :, :], W_conv.rearrange("(m p) o k -> p m (o k)", p=P),
                         allow_slow_non_contiguous=True).then_inc(s["w_cst"], 16)
            sp.dma_start(g_row[:, :], ln_g.partition_broadcast(P)).then_inc(s["w_cst"], 16)
            sp.dma_start(b_row[:, :], ln_b.partition_broadcast(P)).then_inc(s["w_cst"], 16)
            for j in range(TPP):
                sp.dma_start(a_col[j * DS:(j + 1) * DS, 0:1], A_log.unsqueeze(1),
                             allow_slow_non_contiguous=True).then_inc(s["w_cst"], 16)
            sp.dma_start(bdt_col[2 * DS:3 * DS, :], b_dt.unsqueeze(1),
                         allow_slow_non_contiguous=True).then_inc(s["w_cst"], 16)
            sp.dma_start(a_xg[:, :], b_conv.partition_broadcast(P)).then_inc(s["w_bc"], 16)
            give_head_start(sp, "sp")
            sp.dma_start(a_x[:, :], x_tok[0:TOK, :]).then_inc(s["a_ld"], 16)
            sp.wait_ge(s["w_ld"], 16 * W_LOADS)
            sp.dma_start(row_dram[:, 0:DM], cond_nat[:, 0:DM]).then_inc(s["w_row"], 16)

            def load_xs(sl, at, h):
                sp.wait_ge(s["b_spread"], 2 * STEPS * sl - (1 - h) * STEPS)
                for r in range(2):
                    quad = 32 * (2 * h + r)
                    sp.dma_start(xs_sb[quad:quad + PARTS * TPP, :, :],
                                 xs_dram[ds(at, 1), r, :, h * HALF:(h + 1) * HALF, :]
                                 .rearrange("o q t c -> (o q) t c")).then_inc(s[f"b_ld_xs{h}"], 16)

            def load_ahead(a):
                sp.wait_ge(s["a_xTp"], a + 2)
                sp.dma_start(a_x[:, :], x_tok[ds((a + 1) % TILES * TOK, TOK), :]).then_inc(s["a_ld"], 16)

            def store_bct(a):
                sp.wait_ge(s["a_bcT"], 2 * a + 4)
                for r in range(2):
                    sp.dma_start(bct_dram[ds(a // TPP, 1), r, ds(a % TPP, 1)].rearrange("o u k t -> (o u k) t"),
                                 a_bcT[:, r * S:(r + 1) * S]).then_inc(s["a_st"], 16)

            def store_xn(a):
                sp.wait_ge(s["a_p3"], a + 2)
                sp.wait_ge(s["a_p2"], a + 2)
                for r in range(2):
                    for q in range(PARTS):
                        sp.dma_start(xs_dram[ds(a // TPP * SLICES, SLICES), r, ds(a % TPP + q * TPP, 1), :, :]
                                     .rearrange("l o t c -> l (o t) c"),
                                     a_parts[r * S:(r + 1) * S, q, :]).then_inc(s["a_st"], 16)

            def store_dx(a):
                sp.wait_ge(s["a_dx"], a + 2)
                sp.dma_start(dx_dram[ds(a, 1)].rearrange("u p c -> (u p) c"), a_dx[:, :]).then_inc(s["a_st_dx"], 16)

            def fill(t, front, back):
                if front:
                    load_ahead(t)
                if back:
                    store_xn(t - 1)
                    store_bct(t - 1)
                if front:
                    store_dx(t)

            def serve_c(i, j, C1, C2, C3):
                sl = i * SLICES + j
                if C1:
                    c = sl - C1_LAG
                    sp.wait_ge(s["c_yd"], c + 1)
                    sp.wait_ge(s["a_st_dx"], 16 * (c + 2))
                    sp.dma_start(c_dx[:, :], dx_dram[ds(c, 1)].rearrange("u p c -> (u p) c"))\
                        .then_inc(s["c_ld_dx"], 16)
                    sp.wait_ge(s["b_yst"], 64 * (SLICES * i + 1))
                    sp.dma_start(c_y[:, :], y_dram[ds(i - 1, 1), ds(j, 1)].rearrange("i j r t c -> (i j r t) c"))\
                        .then_inc(s["c_ld_y"], 16)
                    sp.wait_ge(s["c_xTp"], c + 1)
                    sp.wait_ge(s["c_x1"], c + 1)
                    sp.dma_start(c_x[:, :], x_tok[ds(c * TOK, TOK), :]).then_inc(s["c_ld_x"], 16)
                    sp.wait_ge(s["c_xm"], c + 1)
                    for r in range(2):
                        sp.dma_start(c_s1[r * S:(r + 1) * S, :],
                                     row_dram[ds(c * 2 + r, 1), 0:DM].to_broadcast([S, DM]))\
                            .then_inc(s["c_ld_s1"], 16)
                if C2:
                    c = sl - C2_LAG
                    sp.wait_ge(s["c_f"], c + 1)
                    for r in range(2):
                        sp.dma_start(c_wu[r * S:(r + 1) * S, :, :].rearrange("p w o -> p (w o)"),
                                     row_dram[ds(c * 2 + r, 1), DM:3 * DM].to_broadcast([S, 2 * DM]))\
                            .then_inc(s["c_ld_wu"], 16)
                if C3:
                    c = sl - C3_LAG
                    sp.wait_ge(s["c_out"], c + 2)
                    sp.dma_start(o_tok[ds(c * TOK, TOK), :], c_out[:, :]).then_inc(s["c_st"], 16)

            def slice_(i, j, A, C1, C2, C3):
                sl = i * SLICES + j
                if A:
                    load_ahead(sl + A_LEAD)
                serve_c(i, j, C1, C2, C3)
                if not (isinstance(i, int) and i == last):
                    sp.wait_ge(s["a_st"], 128 * (sl + A_LEAD + 1))
                load_xs(sl + 2, (sl + 1) % TILES, 0)
                load_xs(sl + 2, (sl + 1) % TILES, 1)
                if A:
                    store_bct(sl + A_LEAD)
                sp.wait_ge(s["b_yev"], sl + 2)
                for v in range(2):
                    for r in range(2):
                        quad = 32 * (2 * v + r)
                        sp.dma_start(y_dram[ds(i, 1), :, r, ds(j * STEPS + v, UNITS, 2), :]
                                     .rearrange("i b u c -> u (i b) c"),
                                     y_sb[quad:quad + 32, :]).then_inc(s["b_yst"], 16)
                if A:
                    store_dx(sl + A_LEAD)
                    store_xn(sl + A_LEAD)

            def drain(i, j, C1, C2, C3):
                serve_c(i, j, C1, C2, C3)

            def store_rows():
                sp.wait_ge(s["w_dpow"], 1)
                sp.dma_start(row_dram[:, DM:3 * DM], dco[:, 3:5, :].rearrange("p w o -> p (w o)")).then_inc(s["w_row"], 16)
                sp.wait_ge(s["w_row"], 32)

            def before_scan(i):
                used, stored = sp.snap(8 * (i + 1)), sp.snap(128 * (TPP * (i + 1) + 1))
                sp.wait_ge(s["b_prep"], used)
                sp.wait_ge(s["a_st"], stored)
                for r in range(2):
                    for k in range(3):
                        sp.dma_start(raw[:, k, r, :],
                                     bct_dram[ds(i, 1), r].rearrange("o j (k d) t -> k (o j) d t", k=3)[k])\
                            .then_inc(s["b_ld_raw"], 16)
                if isinstance(i, int) and i == 0:
                    for h in range(2):
                        load_xs(1, 0, h)

            run(sp, fill, slice_, drain, before_scan, ahead=True, before_last=store_rows)
            sp.wait_ge(s["c_st"], 16 * (TILES + 1))
            sp.wait_ge(s["a_st"], 128 * (TILES + 1))
            sp.wait_ge(s["a_st_dx"], 16 * (TILES + 1))
            sp.wait_ge(s["a_ld"], 16 * (TILES + 2))
            sp.wait_ge(s["b_yst"], 64 * (TILES + 1))
            sp.wait_ge(s["b_ld_xs0"], 32 * (TILES + 2))
            sp.wait_ge(s["b_ld_xs1"], 32 * (TILES + 2))

        @block.gpsimd
        def _(pool):
            give_head_start(pool, "pool")
            pool.memset(ident[:, :], 0.0).then_inc(s["w_pool"], 1)
            pool.memset(mask[:, :], 1.0).then_inc(s["w_pool"], 1)
            pool.memset(band, 1.0).then_inc(s["w_pool"], 1)
            pool.memset(half_pow[:, 0:1], -0.5).then_inc(s["w_pool"], 1)
            pool.memset(half_pow[:, 1:2], 0.5).then_inc(s["w_pool"], 1)
            pool.memset(eps[:, 0:1], 4e-5)
            pool.memset(eps[:, 1:2], 1e-5)
            pool.memset(neg_one[:, :], -1.0)
            pool.memset(bias_in[:, :], 0.0).then_inc(s["w_bc"], 1)
            pool.memset(a_bc[:, :], 0.0).then_inc(s["w_bc"], 1)
            pool.wait_ge(s["w_pool"], 5)
            pool.affine_select(out=ident[:, :], in_=ident[:, :], compare_op=ALU.not_equal, fill=1.0, base=0,
                               pattern=[[-1, P]], channel_multiplier=1).then_inc(s["w_pool"], 1)
            pool.affine_select(out=mask[:, :], in_=mask[:, :], compare_op=ALU.is_ge, fill=0.0, base=0,
                               pattern=[[-HD, HPC]], channel_multiplier=1).then_inc(s["w_pool"], 1)
            pool.affine_select(out=band, in_=band, compare_op=ALU.is_ge, fill=0.0, base=0,
                               pattern=[[DS * TPP, P // TPP], [1, P]], channel_multiplier=-DS).then_inc(s["w_pool"], 1)
            pool.wait_ge(s["w_pool"], 8)
            pool.affine_select(out=mask[:, :], in_=mask[:, :], compare_op=ALU.is_ge, fill=0.0, base=HD - 1,
                               pattern=[[HD, HPC]], channel_multiplier=-1).then_inc(s["w_pool"], 1)
            pool.affine_select(out=band, in_=band, compare_op=ALU.is_ge, fill=0.0, base=DS - 1,
                               pattern=[[-DS * TPP, P // TPP], [-1, P]], channel_multiplier=DS).then_inc(s["w_pool"], 1)

            def a_norm(n):
                pool.wait_ge(s["a_mv"], n + 1)
                pool.wait_ge(s["a_nb"], n)
                pool.tensor_tensor(a_ve[:, :], a_mv[:, 1:2], eps[:, 0:1], ALU.add).then_inc(s["a_ve"], 1)
                pool.tensor_tensor(a_nmu[:, :], a_mv[:, 0:1], neg_one[:, :], ALU.mult).then_inc(s["a_nmu"], 1)
                pool.wait_ge(s["a_ve"], n + 1)
                pool.wait_ge(s["a_z"], n)
                pool.tensor_tensor(a_rs[:, :], a_ve[:, :], half_pow[:, 0:1], ALU.pow).then_inc(s["a_rs"], 1)
                pool.wait_ge(s["a_nmu"], n + 1)
                pool.wait_ge(s["a_rs"], n + 1)
                pool.tensor_tensor(a_nb[:, :], a_rs[:, :], a_nmu[:, :], ALU.mult).then_inc(s["a_nb"], 1)

            def a_affine(n):
                pool.wait_ge(s["a_z"], n + 1)
                pool.tensor_tensor(a_xg[:, :], a_z[:, :], g_row[:, :], ALU.mult).then_inc(s["a_xg"], 1)
                pool.wait_ge(s["a_xg"], n + 1)
                pool.wait_ge(s["a_xnTp"], n)
                pool.wait_ge(s["a_dx"], n)
                pool.wait_ge(s["a_ss"], n)
                pool.wait_ge(s["a_p1"], n)
                pool.tensor_tensor(a_xn[:, :], a_xg[:, :], b_row[:, :], ALU.add).then_inc(s["a_xn"], 1)

            def a_first_rest(n):
                pool.wait_ge(s["a_p1"], n + 1)
                pool.wait_ge(s["a_p2"], n)
                pool.tensor_tensor(a_r1[:, :], a_xn[:, :], a_parts[:, 0, :], ALU.subtract).then_inc(s["a_r1"], 1)

            def a_norm_root(n):
                pool.wait_ge(s["a_ss"], n + 1)
                pool.wait_ge(s["a_nm"], n)
                pool.tensor_tensor(a_nrm[:, 0:1], a_ss[:, :], half_pow[:, 1:2], ALU.pow).then_inc(s["a_nr"], 1)

            def a_second_rest(n):
                pool.wait_ge(s["a_p2"], n + 1)
                pool.wait_ge(s["a_st"], 128 * n)
                pool.wait_ge(s["a_r1"], n + 1)
                pool.tensor_tensor(a_parts[:, 2, :], a_r1[:, :], a_parts[:, 1, :], ALU.subtract).then_inc(s["a_p3"], 1)

            def a_skip(n):
                pool.wait_ge(s["a_xn"], n + 1)
                pool.wait_ge(s["a_st_dx"], 16 * n)
                pool.tensor_tensor(a_dx[:, :], a_xn[:, :], d_row[:, :], ALU.mult).then_inc(s["a_dx"], 1)

            def c_sum_skip(n):
                pool.wait_ge(s["c_ld_dx"], 16 * (n + 1))
                pool.wait_ge(s["c_ld_y"], 16 * (n + 1))
                pool.wait_ge(s["c_yg"], n)
                pool.tensor_tensor(c_yd[:, :], c_dx[:, :], c_y[:, :], ALU.add).then_inc(s["c_yd"], 1)

            def c_style(n):
                pool.wait_ge(s["c_x1"], n + 1)
                pool.wait_ge(s["c_ld_s1"], 32 * (n + 1))
                pool.wait_ge(s["c_z"], n)
                pool.tensor_tensor(c_xm[:, :], c_x1[:, :], c_s1[:, :], ALU.mult).then_inc(s["c_xm"], 1)

            def c_norm(n):
                pool.wait_ge(s["c_mv"], n + 1)
                pool.wait_ge(s["c_nb"], n)
                pool.tensor_tensor(c_ve[:, :], c_mv[:, 1:2], eps[:, 1:2], ALU.add).then_inc(s["c_ve"], 1)
                pool.tensor_tensor(c_nmu[:, :], c_mv[:, 0:1], neg_one[:, :], ALU.mult).then_inc(s["c_nmu"], 1)
                pool.wait_ge(s["c_ve"], n + 1)
                pool.wait_ge(s["c_z"], n)
                pool.tensor_tensor(c_rs[:, :], c_ve[:, :], half_pow[:, 0:1], ALU.pow).then_inc(s["c_rs"], 1)
                pool.wait_ge(s["c_nmu"], n + 1)
                pool.wait_ge(s["c_rs"], n + 1)
                pool.tensor_tensor(c_nb[:, :], c_rs[:, :], c_nmu[:, :], ALU.mult).then_inc(s["c_nb"], 1)

            def c_final(n):
                pool.wait_ge(s["c_f"], n + 1)
                pool.tensor_tensor(c_f2[:, :], c_f[:, 0, :], c_f[:, 1, :], ALU.add).then_inc(s["c_f2"], 1)
                pool.wait_ge(s["c_f2"], n + 1)
                pool.wait_ge(s["c_keep"], n + 1)
                pool.wait_ge(s["c_st"], 16 * n)
                pool.tensor_tensor(c_out[:, :], c_f2[:, :], c_kept[:, :], ALU.add).then_inc(s["c_out"], 1)

            def fill(t, front, back):
                if back:
                    a_norm_root(t)
                    a_first_rest(t)
                    a_second_rest(t)
                if front:
                    a_norm(t + 1)
                    a_affine(t + 1)
                    a_skip(t + 1)

            def slice_(i, j, A, C1, C2, C3):
                sl = i * SLICES + j
                na, n1, n2, n3 = sl + A_LEAD + 1, sl - C1_LAG + 1, sl - C2_LAG + 1, sl - C3_LAG + 1
                if C3:
                    c_final(n3)
                if C2:
                    c_style(n2)
                    c_norm(n2)
                if C1:
                    c_sum_skip(n1)
                if A:
                    a_norm(na)
                    a_affine(na)
                    a_first_rest(na)
                    a_norm_root(na)
                    a_skip(na)
                    a_second_rest(na)

            def drain(i, j, C1, C2, C3):
                sl = i * SLICES + j
                n1, n2, n3 = sl - C1_LAG + 1, sl - C2_LAG + 1, sl - C3_LAG + 1
                if C2:
                    c_style(n2)
                    c_norm(n2)
                if C1:
                    c_sum_skip(n1)
                if C3:
                    c_final(n3)

            def zero_state(i):
                pool.wait_ge(s["b_read"], 2 * S * i + 2 * STEPS)
                pool.sem_inc(s["b_seen"], 1)
                for r in range(2):
                    pool.memset(gc[r][:, RING - 1, :], 0.0).then_inc(s["b_zero"], 1)

            run(pool, fill, slice_, drain, zero_state)

        @block.tensor
        def _(pe):
            give_head_start(pe, "pe")
            banks = (ps_c1, ps_c2)
            pe.wait_ge(s["w_pool"], W_POOL)
            pe.wait_ge(s["w_ld"], 16 * W_LOADS)
            for g, (moves, _) in enumerate(groups):
                if g >= 2:
                    pe.wait_ge(s["w_ev"], g - 1)
                for at, src in moves:
                    mm = pe.transpose(banks[g % 2][:, at:at + P], src, ident[:, :])
                mm.then_inc(s["w_tp"], 1)
            pe.wait_ge(s["w_cst"], W_CONSTS * 16)
            pe.wait_ge(s["w_ev"], NG)
            for m in range(MC):
                pe.transpose(ps_c1[:, m * NPROJ:(m + 1) * NPROJ], st_x[:, m * P:(m + 1) * P],
                             ident[0:NPROJ, 0:NPROJ])
            for m in range(MC):
                mm = pe.matmul(ps_c2[:, m * DS:(m + 1) * DS], st_dt[:, m * P:(m + 1) * P], wdtT[:, :],
                               start=True, stop=True)
            mm.then_inc(s["w_tp"], 1)
            pe.wait_ge(s["w_ev"], NG + 2)
            pe.wait_ge(s["w_diag"], 1)
            pe.wait_ge(s["w_bias"], 6)

            def sum_squares():
                pe.wait_ge(s["w_sq"], 2)
                for w, dst in enumerate((ps_y, ps_x[0][0], ps_x[0][1], ps_x[1][0], ps_x[1][1])):
                    if w < 3:
                        for c in range(KC):
                            for k in range(KC):
                                mm = pe.matmul(dst[:, c * B:(c + 1) * B], sq_l1[:, w, k, c * P:(c + 1) * P],
                                               sq_cond[:, k, :], start=(k == 0), stop=(k == KC - 1))
                    else:
                        for k in range(KC):
                            mm = pe.matmul(dst[:, 0:DM], sq_cond[:, KC + k, :], sq_l1[:, w, k, :],
                                           start=(k == 0), stop=(k == KC - 1))
                    mm.then_inc(s["w_dp"], 1)

            def sums_taken():
                pe.wait_ge(s["w_de"], 5)

            def a_transpose_x(n, two_banks=False):
                pe.wait_ge(s["a_ld"], 16 * (n + 1))
                if two_banks:
                    pe.wait_ge(s["a_z"], n)
                else:
                    pe.wait_ge(s["a_bcT"], 2 * n)
                for k in range(KC):
                    mm = pe.transpose(ps_a[:, k * TOK:(k + 1) * TOK], a_x[:, k * P:(k + 1) * P], ident[:, :])
                mm.then_inc(s["a_xTp"], 1)

            def a_project_in(n):
                pe.wait_ge(s["a_xT"], n + 1)
                for m in range(MC):
                    for k in range(KC):
                        mm = pe.matmul(ps_a[:, m * TOK:(m + 1) * TOK], WinT[:, k, m * P:(m + 1) * P], a_xT[:, k, :],
                                       start=(k == 0), stop=(k == KC - 1))
                mm.then_inc(s["a_inp"], 1)

            def a_convolve(n):
                pe.wait_ge(s["a_xr"], n + 1)
                for m in range(MC):
                    dst = ps_a[:, m * TOK:(m + 1) * TOK]
                    for tap in range(TAPS):
                        pe.matmul(dst.rearrange("p (r t) -> p r t", r=2), conv_diag[:, m, tap, :],
                                  a_xr[:, m, :, tap:tap + S], start=(tap == 0), stop=False)
                    mm = pe.matmul(dst, bias_in[:, m * P:(m + 1) * P], ones[:, :], start=False, stop=True)
                mm.then_inc(s["a_conv"], 1)

            def a_transpose_xc(n):
                pe.wait_ge(s["a_xc"], n + 1)
                for m in range(MC):
                    mm = pe.transpose(ps_a[:, m * P:(m + 1) * P], a_xc[:, m, :], ident[:, :])
                mm.then_inc(s["a_xcT"], 1)

            def a_transpose_xn(n, bank=ps_a):
                pe.wait_ge(s["a_z"], n + 1)
                pe.wait_ge(s["a_bcT"], 2 * n)
                pe.wait_ge(s["a_xn"], n + 1)
                for m in range(MC):
                    mm = pe.transpose(bank[:, m * TOK:(m + 1) * TOK], a_xn[:, m * P:(m + 1) * P], ident[:, :])
                mm.then_inc(s["a_xnTp"], 1)

            def a_project_bc(n, bank=ps_a):
                pe.wait_ge(s["a_xnT"], n + 1)
                for m in range(MC):
                    mm = pe.matmul(bank[:, 0:NPROJ], a_xnT[:, m, :], WxT[:, m, :], start=(m == 0), stop=(m == MC - 1))
                mm.then_inc(s["a_proj"], 1)

            def a_transpose_bc(n, bank=ps_a):
                pe.wait_ge(s["a_bc"], 2 * n + 2)
                pe.transpose(bank[:, 0:TOK], a_bc[:, :], ident[:, :]).then_inc(s["a_bcTp"], 1)

            def spread(sl, t, r):
                h, tt = t // HALF, t % HALF
                if tt == 0:
                    pe.wait_ge(s[f"b_ld_xs{h}"], 32 * (sl + 1))
                pe.wait_ge(s["b_u"], (sl * STEPS + t) * 2 + r + 1)
                quad = 32 * (2 * h + r)
                pe.matmul(ps_x[r][t % 2][:, :], sel[quad:quad + PARTS * TPP, :], xs_sb[quad:quad + PARTS * TPP, tt, :],
                          start=True, stop=True).then_inc(s["b_spread"], 1)

            def read_out(sl, u):
                if u == 0:
                    pe.wait_ge(s["b_cms"], 2 * sl + 2)
                    pe.wait_ge(s["b_yev"], sl)
                pe.wait_ge(s["b_g"], (sl * STEPS + 2 * u + 2) * 2)
                for v in range(2):
                    for r in range(2):
                        quad = 32 * (2 * v + r)
                        pe.matmul(ps_y[quad:quad + 32, :], cms[:, v, r, 32 * u:32 * (u + 1)],
                                  gc[r][:, (2 * u + v) % RING, :], start=(u == 0), stop=(u == UNITS - 1))\
                            .then_inc(s["b_read"], 1)

            def c_transpose_x(n, bank=ps_c1):
                pe.wait_ge(s["c_ld_x"], 16 * (n + 1))
                if bank is ps_c1:
                    pe.wait_ge(s["c_pT"], 2 * n - 1)
                else:
                    pe.wait_ge(s["c_x1"], n)
                for k in range(KC):
                    mm = pe.transpose(bank[:, k * TOK:(k + 1) * TOK], c_x[:, k * P:(k + 1) * P], ident[:, :])
                mm.then_inc(s["c_xTp"], 1)

            def c_project_gate(n, bank=ps_c1):
                pe.wait_ge(s["c_xT"], n + 1)
                for k in range(KC):
                    mm = pe.matmul(bank[:, :], c_xT[:, k, :], WinT[:, k, DI:2 * DI], start=(k == 0), stop=(k == KC - 1))
                mm.then_inc(s["c_gate"], 1)

            def c_transpose_yg(n, bank=ps_c1):
                pe.wait_ge(s["c_yg"], n + 1)
                for m in range(MC):
                    mm = pe.transpose(bank[:, m * TOK:(m + 1) * TOK], c_yg[:, m * P:(m + 1) * P], ident[:, :])
                mm.then_inc(s["c_ygTp"], 1)

            def c_project_out(n, bank=ps_c1):
                pe.wait_ge(s["c_ygT"], n + 1)
                for m in range(MC):
                    mm = pe.matmul(bank[:, 0:DM], c_ygT[:, m, :], WoutT[:, m, :], start=(m == 0), stop=(m == MC - 1))
                mm.then_inc(s["c_wout"], 1)

            def c_transpose_z(n):
                pe.wait_ge(s["c_z"], n + 1)
                pe.wait_ge(s["c_pT"], 2 * n - 1)
                for k in range(KC):
                    mm = pe.transpose(ps_c1[:, k * TOK:(k + 1) * TOK], c_z[:, k * P:(k + 1) * P], ident[:, :])
                mm.then_inc(s["c_zTp"], 1)

            def c_project_qv(n):
                pe.wait_ge(s["c_zT"], n + 1)
                pe.wait_ge(s["c_f"], n)
                for o, w in ((0, 0), (KC, 2)):
                    for c in range(KC):
                        for k in range(KC):
                            mm = pe.matmul(ps_c2[:, (o + c) * TOK:(o + c + 1) * TOK], L1T[:, w, k, c * P:(c + 1) * P],
                                           c_zT[:, k, :], start=(k == 0), stop=(k == KC - 1))
                mm.then_inc(s["c_qv"], 1)

            def c_project_k(n):
                pe.wait_ge(s["c_zT"], n + 1)
                for c in range(KC):
                    for k in range(KC):
                        mm = pe.matmul(ps_c1[:, c * TOK:(c + 1) * TOK], L1T[:, 1, k, c * P:(c + 1) * P],
                                       c_zT[:, k, :], start=(k == 0), stop=(k == KC - 1))
                mm.then_inc(s["c_k"], 1)

            def c_transpose_v(n):
                pe.wait_ge(s["c_vd"], n + 1)
                pe.wait_ge(s["c_q"], n + 1)
                for r in range(2):
                    for c in range(KC):
                        mm = pe.transpose(ps_c2[:, (r * KC + c) * P:(r * KC + c + 1) * P],
                                          c_vd[:, c, r].rearrange("p a t -> p (a t)"), ident[:, :])
                mm.then_inc(s["c_vTp"], 1)

            def c_scores(n, c):
                bank = (ps_c1, ps_c2)[c]
                pe.wait_ge(s["c_kbd"], n + 1)
                pe.wait_ge(s[("c_q", "c_vbd")[c]], n + 1)
                for r in range(2):
                    mm = pe.matmul(bank[r * S:(r + 1) * S, :], c_q[:, c, r * S:(r + 1) * S],
                                   c_kbd[:, :, c, r * S:(r + 1) * S], start=True, stop=True)
                mm.then_inc(s["c_sc"], 1)

            def c_transpose_p(n, c):
                bank = (ps_c1, ps_c2)[c]
                pe.wait_ge(s["c_e"], 2 * n + c + 1)
                for pair in range(HPC // 2):
                    mm = pe.transpose(bank[:, pair * TOK:(pair + 1) * TOK], c_e[:, c, pair * P:(pair + 1) * P],
                                      ident[:, :])
                mm.then_inc(s["c_pTp"], 1)

            def c_weigh_v(n):
                pe.wait_ge(s["c_pT"], 2 * n + 2)
                for pair in range(HEADS // 2):
                    for r in range(2):
                        mm = pe.matmul(ps_c2[r * S:(r + 1) * S, pair * 2 * VW:(pair + 1) * 2 * VW],
                                       c_pT[:, pair // 4, pair % 4, r * S:(r + 1) * S],
                                       c_vbd[:, r, pair, :, :].rearrange("p a v -> p (a v)"), start=True, stop=True)
                mm.then_inc(s["c_pv"], 1)

            def c_transpose_o(n):
                pe.wait_ge(s["c_o"], n + 1)
                for c in range(KC):
                    mm = pe.transpose(ps_c2[:, c * TOK:(c + 1) * TOK],
                                      c_o[:, c * HPC:(c + 1) * HPC, :].rearrange("p h d -> p (h d)"), ident[:, :])
                mm.then_inc(s["c_oTp"], 1)

            def c_project_wu(n):
                pe.wait_ge(s["c_oT"], n + 1)
                for a, (lhs, w) in enumerate(((c_oT, 3), (c_vsT, 4))):
                    for k in range(KC):
                        mm = pe.matmul(ps_c2[:, a * DM:(a + 1) * DM], lhs[:, k, :], L1T[:, w, k, :],
                                       start=(k == 0), stop=(k == KC - 1))
                mm.then_inc(s["c_fin"], 1)

            def fill(t, front, back):
                if front:
                    a_transpose_x(t + 1, two_banks=True)
                    a_project_in(t + 1)
                if back:
                    a_transpose_xn(t, ps_c1)
                if front:
                    a_convolve(t + 1)
                if back:
                    a_project_bc(t, ps_c1)
                if front:
                    a_transpose_xc(t + 1)
                if back:
                    a_transpose_bc(t, ps_c1)

            def slice_(i, j, A, C1, C2, C3):
                sl = i * SLICES + j
                na, n1, n2, n3 = sl + A_LEAD + 1, sl - C1_LAG + 1, sl - C2_LAG + 1, sl - C3_LAG + 1
                if A:
                    a_transpose_x(na)
                spread(sl + 1, 0, 0)
                spread(sl + 1, 0, 1)
                if C3:
                    c_transpose_o(n3)
                if C2:
                    c_transpose_yg(n2)
                spread(sl + 1, 1, 0)
                spread(sl + 1, 1, 1)
                if C3:
                    c_project_wu(n3)
                if A:
                    a_project_in(na)
                spread(sl + 1, 2, 0)
                spread(sl + 1, 2, 1)
                if C2:
                    c_project_out(n2)
                spread(sl + 1, 3, 0)
                spread(sl + 1, 3, 1)
                if A:
                    a_convolve(na)
                spread(sl + 1, 4, 0)
                spread(sl + 1, 4, 1)
                if C2:
                    c_transpose_z(n2)
                read_out(sl + 1, 0)
                if C2:
                    c_project_k(n2)
                if A:
                    a_transpose_xc(na)
                if C2:
                    c_project_qv(n2)
                spread(sl + 1, 5, 0)
                spread(sl + 1, 5, 1)
                spread(sl + 1, 6, 0)
                spread(sl + 1, 6, 1)
                if C2:
                    c_scores(n2, 0)
                    c_transpose_v(n2)
                spread(sl + 1, 7, 0)
                spread(sl + 1, 7, 1)
                read_out(sl + 1, 1)
                if C2:
                    c_scores(n2, 1)
                    c_transpose_p(n2, 0)
                if A:
                    a_transpose_xn(na)
                read_out(sl + 1, 2)
                if C1:
                    c_transpose_x(n1)
                if A:
                    a_project_bc(na)
                if C2:
                    c_transpose_p(n2, 1)
                if C1:
                    c_project_gate(n1)
                if C2:
                    c_weigh_v(n2)
                if A:
                    a_transpose_bc(na)
                read_out(sl + 1, 3)

            def drain(i, j, C1, C2, C3):
                sl = i * SLICES + j
                n1, n2, n3 = sl - C1_LAG + 1, sl - C2_LAG + 1, sl - C3_LAG + 1
                if C2:
                    c_transpose_yg(n2, ps_a)
                if C3:
                    c_transpose_o(n3)
                if C2:
                    c_project_out(n2, ps_a)
                if C3:
                    c_project_wu(n3)
                if C1:
                    c_transpose_x(n1, ps_a)
                if C2:
                    c_transpose_z(n2)
                    c_project_k(n2)
                    c_project_qv(n2)
                    c_transpose_v(n2)
                    c_scores(n2, 0)
                    c_scores(n2, 1)
                if C1:
                    c_project_gate(n1, ps_a)
                if C2:
                    c_transpose_p(n2, 0)
                    c_transpose_p(n2, 1)
                    c_weigh_v(n2)

            run(pe, fill, slice_, drain, after_first=sum_squares, before_last=sums_taken)

        @block.scalar
        def _(act):
            give_head_start(act, "act")
            banks = (ps_c1, ps_c2)
            for g, (_, dst) in enumerate(groups):
                act.wait_ge(s["w_tp"], g + 1)
                act.activation(dst, banks[g % 2][:, :], ACT.Copy).then_inc(s["w_ev"], 1)
            act.wait_ge(s["w_tp"], NG + 1)
            act.activation(WxT[:, :, 0:2 * DS],
                           ps_c1[:, 0:MC * NPROJ].rearrange("p (m k) -> p m k", m=MC)[:, :, 0:2 * DS],
                           ACT.Copy).then_inc(s["w_ev"], 1)
            act.activation(WxT[:, :, 2 * DS:NPROJ], ps_c2[:, 0:MC * DS].rearrange("p (m k) -> p m k", m=MC),
                           ACT.Copy).then_inc(s["w_ev"], 1)
            act.wait_ge(s["w_cst"], W_CONSTS * 16)
            act.activation(a_col[:, 1:2], a_col[:, 0:1], ACT.Tanh).then_inc(s["w_a"], 1)
            act.wait_ge(s["w_ev"], NG + 2)
            act.activation(stage[:, 0:2560], L1T[:, :, :, :].rearrange("p w k o -> p (w k o)"), ACT.Square)\
                .then_inc(s["w_sq"], 1)
            act.activation(stage[:, 2560:3072], condT[:, :, :].rearrange("p m b -> p (m b)"), ACT.Square)\
                .then_inc(s["w_sq"], 1)

            def take_sums():
                for w, src in enumerate((ps_y, ps_x[0][0], ps_x[0][1], ps_x[1][0], ps_x[1][1])):
                    act.wait_ge(s["w_dp"], w + 1)
                    act.activation(dm_x[:, w * DM:(w + 1) * DM], src[:, 0:DM], ACT.Copy, bias=1e-8)\
                        .then_inc(s["w_de"], 1)
                act.wait_ge(s["w_de"], 5)
                act.activation(dco[:, :, :].rearrange("p w o -> p (w o)"), dm_x, ACT.Sqrt).then_inc(s["w_de"], 1)
                act.activation(table_in[:, :], half_pow[:, 0:1], ACT.Tanh)

            def a_take_xT(n):
                act.wait_ge(s["a_xTp"], n + 1)
                act.wait_ge(s["a_inp"], n)
                act.activation(a_xT[:, :, :].rearrange("p k t -> p (k t)"), ps_a[:, 0:KC * TOK], ACT.Copy)\
                    .then_inc(s["a_xT"], 1)

            def a_tanh(n):
                act.wait_ge(s["a_conv"], n + 1)
                act.wait_ge(s["a_ss"], n)
                act.wait_ge(s["a_xc"], n)
                act.activation(a_th[:, :], ps_a[:, :], ACT.Tanh, scale=0.5).then_inc(s["a_th"], 1)

            def a_normalise(n):
                act.wait_ge(s["a_nb"], n + 1)
                act.wait_ge(s["a_st1"], n + 1)
                act.wait_ge(s["a_xg"], n)
                act.activation(a_z[:, :], ps_a[:, :], ACT.Identity, bias=a_nb[:, :], scale=a_rs[:, :])\
                    .then_inc(s["a_z"], 1)

            def a_first_part(n):
                act.wait_ge(s["a_xn"], n + 1)
                act.wait_ge(s["a_st"], 128 * n)
                act.wait_ge(s["a_r1"], n)
                act.activation(a_parts[:, 0, :], a_xn[:, :], ACT.Copy).then_inc(s["a_p1"], 1)

            def a_square_sum(n):
                act.wait_ge(s["a_xn"], n + 1)
                act.wait_ge(s["a_nr"], n)
                act.activation(a_th[:, :], a_xn[:, :], ACT.Square, accum_out=a_ss[:, :]).then_inc(s["a_ss"], 1)

            def a_second_part(n):
                act.wait_ge(s["a_r1"], n + 1)
                act.activation(a_parts[:, 1, :], a_r1[:, :], ACT.Copy).then_inc(s["a_p2"], 1)

            def a_take_xnT(n, bank=ps_a):
                act.wait_ge(s["a_xnTp"], n + 1)
                act.wait_ge(s["a_proj"], n)
                act.activation(a_xnT[:, :, :].rearrange("p m t -> p (m t)"), bank[:, :], ACT.Copy)\
                    .then_inc(s["a_xnT"], 1)

            def a_take_bcT(n, bank=ps_a):
                act.wait_ge(s["a_bcTp"], n + 1)
                act.wait_ge(s["a_st"], 128 * n)
                act.activation(a_bcT[0:2 * DS, :], bank[0:2 * DS, 0:TOK], ACT.Copy).then_inc(s["a_bcT"], 1)
                act.activation(a_bcT[2 * DS:NPROJ, :], bank[2 * DS:NPROJ, 0:TOK], ACT.Tanh,
                               bias=bdt_col[2 * DS:NPROJ, :]).then_inc(s["a_bcT"], 1)

            def b_take_y(sl):
                act.wait_ge(s["b_read"], 2 * STEPS * (sl + 1))
                act.wait_ge(s["b_yst"], 64 * sl)
                act.activation(y_sb[:, :], ps_y[:, :], ACT.Copy).then_inc(s["b_yev"], 1)

            def c_take_xT(n, bank=ps_c1):
                act.wait_ge(s["c_xTp"], n + 1)
                act.wait_ge(s["c_gate"], n)
                act.activation(c_xT[:, :, :].rearrange("p k t -> p (k t)"), bank[:, 0:KC * TOK], ACT.Copy)\
                    .then_inc(s["c_xT"], 1)

            def c_tanh(n, bank=ps_c1):
                act.wait_ge(s["c_gate"], n + 1)
                act.wait_ge(s["c_sg"], n)
                act.activation(c_th[:, :], bank[:, :], ACT.Tanh, scale=0.5).then_inc(s["c_th"], 1)

            def c_keep(n):
                act.wait_ge(s["c_x1"], n + 1)
                act.wait_ge(s["c_out"], n)
                act.activation(c_kept[:, :], c_x1[:, :], ACT.Copy).then_inc(s["c_keep"], 1)

            def c_take_ygT(n, bank=ps_c1):
                act.wait_ge(s["c_ygTp"], n + 1)
                act.wait_ge(s["c_wout"], n)
                act.activation(c_ygT[:, :, :].rearrange("p m t -> p (m t)"), bank[:, :], ACT.Copy)\
                    .then_inc(s["c_ygT"], 1)

            def c_normalise(n):
                act.wait_ge(s["c_nb"], n + 1)
                act.wait_ge(s["c_zTp"], n)
                act.activation(c_z[:, :], c_xm[:, :], ACT.Identity, bias=c_nb[:, :], scale=c_rs[:, :])\
                    .then_inc(s["c_z"], 1)

            def c_take_zT(n):
                act.wait_ge(s["c_zTp"], n + 1)
                act.wait_ge(s["c_k"], n)
                act.activation(c_zT[:, :, :].rearrange("p k t -> p (k t)"), ps_c1[:, 0:KC * TOK], ACT.Copy)\
                    .then_inc(s["c_zT"], 1)

            def c_double_v(n):
                act.wait_ge(s["c_vs"], n + 1)
                act.wait_ge(s["c_vTp"], n)
                act.activation(c_vd[:, :, :, :, :].rearrange("p k r a t -> p (k r) a t"),
                               c_vsT[:, :, :].rearrange("p k (r t) -> p (k r) t", r=2).unsqueeze(2)
                               .to_broadcast([P, 2 * KC, 2, S]), ACT.Copy).then_inc(s["c_vd"], 1)

            def c_block_keys(n):
                act.wait_ge(s["c_k"], n + 1)
                act.wait_ge(s["c_sc"], 2 * n)
                for h in range(HPC):
                    ins = act.activation(c_kbd[:, h, :, :].rearrange("p k t -> p (k t)"), ps_c1[:, 0:KC * TOK],
                                         ACT.Copy, scale=mask[:, h:h + 1])
                ins.then_inc(s["c_kbd"], 1)

            def c_block_values(n):
                act.wait_ge(s["c_vTp"], n + 1)
                act.wait_ge(s["c_pv"], n)
                for r in range(2):
                    for a in range(2):
                        ins = act.activation(
                            c_vbd[a * S:(a + 1) * S, r, :, a, 0:HD],
                            ps_c2[a * S:(a + 1) * S, r * DM:(r + 1) * DM]
                            .rearrange("p (h a d) -> p h a d", a=2, d=HD)[:, :, a, :], ACT.Copy)
                ins.then_inc(s["c_vbd"], 1)

            def c_exp(n, c):
                act.wait_ge(s["c_sub"], 2 * n + c + 1)
                act.wait_ge(s["c_pTp"], 2 * n)
                act.activation(c_e[:, c, :], c_s[:, c, :, :].rearrange("p h t -> p (h t)"), ACT.Exp)\
                    .then_inc(s["c_e"], 1)

            def c_take_pT(n, c):
                act.wait_ge(s["c_pTp"], 2 * n + c + 1)
                act.wait_ge(s["c_pv"], n)
                act.activation(c_pT[:, c, :, :].rearrange("p a t -> p (a t)"), (ps_c1, ps_c2)[c][:, :], ACT.Copy)\
                    .then_inc(s["c_pT"], 1)

            def c_take_oT(n):
                act.wait_ge(s["c_oTp"], n + 1)
                act.wait_ge(s["c_fin"], n)
                act.activation(c_oT[:, :, :].rearrange("p c t -> p (c t)"), ps_c2[:, 0:KC * TOK], ACT.Copy)\
                    .then_inc(s["c_oT"], 1)

            def fill(t, front, back):
                if front:
                    a_take_xT(t + 1)
                if back:
                    a_first_part(t)
                    a_square_sum(t)
                    a_take_xnT(t, ps_c1)
                    a_second_part(t)
                if front:
                    a_tanh(t + 1)
                if back:
                    a_take_bcT(t, ps_c1)
                if front:
                    a_normalise(t + 1)

            def slice_(i, j, A, C1, C2, C3):
                sl = i * SLICES + j
                na, n1, n2, n3 = sl + A_LEAD + 1, sl - C1_LAG + 1, sl - C2_LAG + 1, sl - C3_LAG + 1
                if C3:
                    c_take_oT(n3)
                if C2:
                    c_take_ygT(n2)
                if A:
                    a_take_xT(na)
                if C2:
                    c_normalise(n2)
                if A:
                    a_tanh(na)
                if C2:
                    c_take_zT(n2)
                    c_block_keys(n2)
                    c_double_v(n2)
                if A:
                    a_normalise(na)
                if C2:
                    c_block_values(n2)
                    c_keep(n2)
                    c_exp(n2, 0)
                    c_take_pT(n2, 0)
                if A:
                    a_take_xnT(na)
                if C2:
                    c_exp(n2, 1)
                if C1:
                    c_take_xT(n1)
                if A:
                    a_first_part(na)
                if C2:
                    c_take_pT(n2, 1)
                if A:
                    a_square_sum(na)
                if C1:
                    c_tanh(n1)
                if A:
                    a_take_bcT(na)
                    a_second_part(na)
                b_take_y(sl + 1)

            def drain(i, j, C1, C2, C3):
                sl = i * SLICES + j
                n1, n2, n3 = sl - C1_LAG + 1, sl - C2_LAG + 1, sl - C3_LAG + 1
                if C2:
                    c_take_ygT(n2, ps_a)
                if C3:
                    c_take_oT(n3)
                if C2:
                    c_normalise(n2)
                    c_take_zT(n2)
                    c_block_keys(n2)
                    c_double_v(n2)
                if C1:
                    c_take_xT(n1, ps_a)
                if C2:
                    c_keep(n2)
                    c_block_values(n2)
                    c_exp(n2, 0)
                    c_exp(n2, 1)
                if C1:
                    c_tanh(n1, ps_a)
                if C2:
                    c_take_pT(n2, 0)
                    c_take_pT(n2, 1)

            run(act, fill, slice_, drain, after_first=take_sums)

        @block.vector
        def _(dve):
            dve.memset(a_xr[:, :, :, :], 0.0).then_inc(s["w_scale"], 1)
            dve.memset(c_vbd[:, :, :, :, :], 0.0).then_inc(s["w_scale"], 1)
            dve.memset(zeros[:, :], 0.0).then_inc(s["w_scale"], 1)
            dve.memset(cms[:, :, :, :], 0.0).then_inc(s["w_scale"], 1)
            dve.memset(ones[:, :], 1.0).then_inc(s["w_scale"], 1)
            give_head_start(dve, "dve")
            dve.wait_ge(s["w_scale"], 5)
            for a in range(2):
                dve.memset(c_vbd[a * S:(a + 1) * S, :, :, a, HD:VW], 1.0).then_inc(s["w_scale"], 1)
            dve.wait_ge(s["w_pool"], W_POOL - 2)
            dve.tensor_reduce(gc[1][:, 0, 0:P], band.rearrange("p g m -> p m g"), AX_X, ALU.add).then_inc(s["w_pool"], 1)
            dve.wait_ge(s["w_pool"], W_POOL - 1)
            dve.tensor_copy(sel[:, :], gc[1][:, 0, 0:P]).then_inc(s["w_pool"], 1)
            dve.wait_ge(s["w_cst"], W_CONSTS * 16)
            for m in range(MC):
                for tap in range(TAPS):
                    ins = dve.tensor_scalar(conv_diag[:, m, tap, :], ident[:, :], conv_w[:, m, tap:tap + 1], None,
                                            ALU.mult)
            ins.then_inc(s["w_diag"], 1)
            dve.wait_ge(s["w_bc"], 18)
            dve.tensor_copy(a_parts[:, 0, :], a_xg[:, :]).then_inc(s["w_bias"], 1)
            dve.wait_ge(s["w_bias"], 1)
            dve.tensor_tensor(a_r1[:, :], a_xg[:, :], a_parts[:, 0, :], ALU.subtract).then_inc(s["w_bias"], 1)
            dve.wait_ge(s["w_bias"], 2)
            dve.tensor_copy(a_parts[:, 1, :], a_r1[:, :]).then_inc(s["w_bias"], 1)
            dve.wait_ge(s["w_bias"], 3)
            dve.tensor_copy(bias_in[0:1, :], a_parts[0:1, 0, :]).then_inc(s["w_bias"], 1)
            dve.tensor_copy(bias_in[32:33, :], a_parts[32:33, 1, :]).then_inc(s["w_bias"], 1)
            dve.tensor_tensor(bias_in[64:65, :], a_r1[64:65, :], a_parts[64:65, 1, :], ALU.subtract)\
                .then_inc(s["w_bias"], 1)
            dve.wait_ge(s["w_a"], 1)
            dve.tensor_scalar(a_col[:, 1:2], a_col[:, 1:2], -0.01, None, ALU.mult).then_inc(s["w_scale"], 1)
            rsq = dco[:, :, :].rearrange("p w o -> p (w o)")
            dve.wait_ge(s["w_scale"], 8)

            def invert_roots():
                dve.wait_ge(s["w_de"], 6)
                dve.reciprocal(rsq, rsq).then_inc(s["w_dm"], 1)

            def demodulate():
                dve.wait_ge(s["w_dm"], 1)
                dve.tensor_tensor(dm_t, rsq, rsq, ALU.mult).then_inc(s["w_dm"], 1)
                dve.wait_ge(s["w_dm"], 2)
                dve.tensor_tensor(dm_t, dm_t, dm_x, ALU.mult).then_inc(s["w_dm"], 1)
                dve.wait_ge(s["w_dm"], 3)
                dve.tensor_scalar(dm_t, dm_t, -0.5, 1.5, ALU.mult, ALU.add).then_inc(s["w_dm"], 1)
                dve.wait_ge(s["w_dm"], 4)
                dve.tensor_tensor(rsq, rsq, dm_t, ALU.mult).then_inc(s["w_dpow"], 1)
                dve.wait_ge(s["w_dpow"], 1)
                dve.scalar_tensor_tensor(qk_scale[:, :, :].rearrange("p c b -> p (c b)"), dco[:, 0, :], HD ** -0.5,
                                         dco[:, 1, :], ALU.mult, ALU.mult).then_inc(s["w_scale"], 1)
                dve.tensor_tensor(v_scale[:, :, :].rearrange("p c b -> p (c b)"), dco[:, 2, :],
                                  condT[:, KC:2 * KC, :].rearrange("p c b -> p (c b)"), ALU.mult)\
                    .then_inc(s["w_scale"], 1)
                dve.wait_ge(s["w_scale"], 10)

            def a_add_style(a, n):
                dve.wait_ge(s["a_inp"], n + 1)
                dve.wait_ge(s["a_conv"], n)
                dve.tensor_tensor(a_xr[:, :, :, TAPS - 1:PADT],
                                  ps_a[:, :].rearrange("p (m r t) -> p m r t", m=MC, r=2),
                                  condT[:, :, ds(a * 2, 2)].unsqueeze(3).to_broadcast([P, MC, 2, S]), ALU.add)\
                    .then_inc(s["a_xr"], 1)

            def a_silu(n):
                dve.wait_ge(s["a_th"], n + 1)
                dve.wait_ge(s["a_xcT"], n)
                dve.scalar_tensor_tensor(a_xc[:, :, :].rearrange("p m t -> p (m t)"), a_th[:, :], 1.0,
                                         ps_a[:, :], ALU.add, ALU.mult).then_inc(s["a_xc"], 1)

            def a_stats(n):
                dve.wait_ge(s["a_xcT"], n + 1)
                dve.bn_stats(a_bn[:, :], ps_a[:, :]).then_inc(s["a_st1"], 1)

            def a_mean_var(n):
                dve.wait_ge(s["a_ve"], n)
                dve.wait_ge(s["a_nmu"], n)
                dve.wait_ge(s["a_st1"], n + 1)
                dve.sem_inc(s["a_seen"], 1)
                dve.bn_aggr(a_mv[:, :], a_bn[:, :]).then_inc(s["a_mv"], 1)

            def a_bound_norm(n):
                dve.wait_ge(s["a_nr"], n + 1)
                dve.tensor_scalar(a_nrm[:, 1:2], a_nrm[:, 0:1], 1.0, None, ALU.min).then_inc(s["a_nm"], 1)

            def a_scale_b(n, bank=ps_a):
                dve.wait_ge(s["a_proj"], n + 1)
                dve.wait_ge(s["a_nm"], n + 1)
                dve.wait_ge(s["a_bcTp"], n)
                dve.tensor_copy(a_bc[:, DS:NPROJ], bank[:, DS:NPROJ]).then_inc(s["a_bc"], 1)
                dve.tensor_scalar(a_bc[:, 0:DS], bank[:, 0:DS], a_nrm[:, 1:2], None, ALU.mult).then_inc(s["a_bc"], 1)

            def prep_b(i):
                dve.wait_ge(s["b_ld_raw"], 96 * (i + 2))
                dve.tensor_scalar(ad[:, :, :], raw[:, 2, :, :], a_col[:, 1:2], 1.0, ALU.mult, ALU.add)\
                    .then_inc(s["b_prep"], 1)
                dve.wait_ge(s["b_prep"], 8 * (i + 1) + 1)
                for r in range(2):
                    dve.tensor_tensor_scan(pr[:, r, :], ad[:, r, :], zeros[:, :], 1.0, ALU.mult, ALU.add)\
                        .then_inc(s["b_prep"], 1)
                dve.wait_ge(s["b_prep"], 8 * (i + 1) + 3)
                dve.reciprocal(rp[:, :, :], pr[:, :, :]).then_inc(s["b_prep"], 1)
                dve.tensor_tensor(cp[:, :, :], raw[:, 1, :, :], pr[:, :, :], ALU.mult).then_inc(s["b_prep"], 1)
                dve.wait_ge(s["b_prep"], 8 * (i + 1) + 4)
                dve.tensor_scalar(hi[:, :, :], rp[:, :, :], CLIP, None, ALU.mult).then_inc(s["b_prep"], 1)
                dve.tensor_scalar(lo[:, :, :], rp[:, :, :], -CLIP, None, ALU.mult).then_inc(s["b_prep"], 1)
                dve.tensor_tensor(bd[:, :, :], raw[:, 0, :, :], rp[:, :, :], ALU.mult).then_inc(s["b_prep"], 1)

            def scan_add(sl, at, t, r):
                step = sl * STEPS + t
                dve.wait_ge(s["b_spread"], 2 * step + r + 1)
                dve.wait_ge(s["b_g"], 2 * step + r - 1)
                dve.scalar_tensor_tensor(gu[r][:, :], ps_x[r][t % 2][:, :], bd[:, r, ds(at, 1)],
                                         gc[r][:, (t - 1) % RING, :], ALU.mult, ALU.add).then_inc(s["b_u"], 1)

            def scan_clip(sl, at, t, r):
                step = sl * STEPS + t
                dve.wait_ge(s["b_u"], 2 * step + r + 1 + 4)
                dve.wait_ge(s["b_read"], 2 * STEPS * sl + 4 * (t // 2) - 4)
                dve.tensor_scalar(gc[r][:, t % RING, :], gu[r][:, :], hi[:, r, ds(at, 1)],
                                  lo[:, r, ds(at, 1)], ALU.min, ALU.max).then_inc(s["b_g"], 1)

            def spread_c(i, j):
                sl = i * SLICES + j + 1
                dve.wait_ge(s["b_read"], 2 * STEPS * sl)
                for v in range(2):
                    dve.tensor_tensor(
                        cms[:, v].rearrange("p r (u c) -> p r u c", c=40)[:, :, :, 0:TPP],
                        cp[:, :, ds(j * STEPS + v, UNITS, 2)].unsqueeze(3).to_broadcast([P, 2, UNITS, TPP]),
                        mask[:, :].unsqueeze(1).unsqueeze(1).to_broadcast([P, 2, UNITS, TPP]), ALU.mult)\
                        .then_inc(s["b_cms"], 1)

            def c_silu(n, bank=ps_c1):
                dve.wait_ge(s["c_th"], n + 1)
                dve.wait_ge(s["c_yg"], n)
                dve.scalar_tensor_tensor(c_sg[:, :], c_th[:, :], 1.0, bank[:, :], ALU.add, ALU.mult)\
                    .then_inc(s["c_sg"], 1)

            def c_gate_product(n):
                dve.wait_ge(s["c_sg"], n + 1)
                dve.wait_ge(s["c_yd"], n + 1)
                dve.wait_ge(s["c_ygTp"], n)
                dve.tensor_tensor(c_yg[:, :], c_yd[:, :], c_sg[:, :], ALU.mult).then_inc(s["c_yg"], 1)

            def c_residual(n, bank=ps_c1):
                dve.wait_ge(s["c_wout"], n + 1)
                dve.wait_ge(s["c_keep"], n)
                dve.scalar_tensor_tensor(c_x1[:, :], bank[:, 0:DM], 0.5, c_x[:, :], ALU.mult, ALU.add)\
                    .then_inc(s["c_x1"], 1)

            def c_stats(n):
                dve.wait_ge(s["c_xm"], n + 1)
                dve.bn_stats(c_bn[:, :], c_xm[:, :]).then_inc(s["c_st1"], 1)

            def c_mean_var(n):
                dve.wait_ge(s["c_ve"], n)
                dve.wait_ge(s["c_nmu"], n)
                dve.wait_ge(s["c_st1"], n + 1)
                dve.sem_inc(s["c_seen"], 1)
                dve.bn_aggr(c_mv[:, :], c_bn[:, :]).then_inc(s["c_mv"], 1)

            def c_scale_qv(c, n):
                dve.wait_ge(s["c_qv"], n + 1)
                dve.wait_ge(s["c_sc"], 2 * n)
                dve.wait_ge(s["c_fin"], n)
                for dst, at, scale, done in ((c_vsT, KC * TOK, v_scale, "c_vs"), (c_q, 0, qk_scale, "c_q")):
                    dve.tensor_tensor(dst[:, :, :].rearrange("p c (r t) -> p c r t", r=2),
                                      ps_c2[:, at:at + KC * TOK].rearrange("p (c r t) -> p c r t", c=KC, r=2),
                                      scale[:, :, ds(c * 2, 2)].unsqueeze(3).to_broadcast([P, KC, 2, S]),
                                      ALU.mult).then_inc(s[done], 1)

            def c_max(n, c):
                sc = (ps_c1, ps_c2)[c][:, :].rearrange("p (h t) -> p h t", h=HPC)
                dve.wait_ge(s["c_sc"], 2 * n + c + 1)
                dve.reduce_max(c_mx[:, c * HPC:(c + 1) * HPC], sc, AX_X).then_inc(s["c_mx"], 1)

            def c_subtract(n, c):
                sc = (ps_c1, ps_c2)[c][:, :].rearrange("p (h t) -> p h t", h=HPC)
                dve.wait_ge(s["c_mx"], 2 * n + c + 1)
                dve.wait_ge(s["c_e"], 2 * n)
                dve.tensor_tensor(c_s[:, c], sc, bcast_mid(c_mx[:, c * HPC:(c + 1) * HPC], S), ALU.subtract)\
                    .then_inc(s["c_sub"], 1)

            def c_divide(n):
                pv = ps_c2[:, 0:HEADS * VW].rearrange("p (h v) -> p h v", h=HEADS)
                dve.wait_ge(s["c_pv"], n + 1)
                dve.reciprocal(c_rc[:, :].unsqueeze(2), pv[:, :, HD:VW]).then_inc(s["c_rc"], 1)
                dve.wait_ge(s["c_rc"], n + 1)
                dve.wait_ge(s["c_oTp"], n)
                dve.tensor_tensor(c_o[:, :, :], pv[:, :, 0:HD], bcast_mid(c_rc[:, :], HD), ALU.mult)\
                    .then_inc(s["c_o"], 1)

            def c_demodulate(n):
                dve.wait_ge(s["c_fin"], n + 1)
                dve.wait_ge(s["c_f2"], n)
                dve.wait_ge(s["c_ld_wu"], 32 * (n + 1))
                dve.tensor_tensor(c_f[:, :, :].rearrange("p w o -> p (w o)"), ps_c2[:, :],
                                  c_wu[:, :, :].rearrange("p w o -> p (w o)"), ALU.mult).then_inc(s["c_f"], 1)

            def fill(t, front, back):
                if front:
                    a_add_style(t, t + 1)
                    a_silu(t + 1)
                    a_stats(t + 1)
                    a_mean_var(t + 1)
                if back:
                    a_bound_norm(t)
                    a_scale_b(t, ps_c1)

            def slice_(i, j, A, C1, C2, C3):
                sl = i * SLICES + j
                na, n1, n2, n3 = sl + A_LEAD + 1, sl - C1_LAG + 1, sl - C2_LAG + 1, sl - C3_LAG + 1
                a = sl + A_LEAD
                c2 = sl - C2_LAG
                dve.wait_ge(s["b_prep"], 8 * (i + 2))
                dve.wait_ge(s["b_zero"], 2 * (i + 2))
                scan_add(sl + 1, j * STEPS, 0, 0)
                scan_add(sl + 1, j * STEPS, 0, 1)
                scan_clip(sl + 1, j * STEPS, 0, 0)
                spread_c(i, j)
                scan_clip(sl + 1, j * STEPS, 0, 1)
                scan_add(sl + 1, j * STEPS + 1, 1, 0)
                if C3:
                    c_demodulate(n3)
                scan_add(sl + 1, j * STEPS + 1, 1, 1)
                scan_clip(sl + 1, j * STEPS + 1, 1, 0)
                if A:
                    a_add_style(a, na)
                scan_clip(sl + 1, j * STEPS + 1, 1, 1)
                scan_add(sl + 1, j * STEPS + 2, 2, 0)
                if C2:
                    c_residual(n2)
                scan_add(sl + 1, j * STEPS + 2, 2, 1)
                scan_clip(sl + 1, j * STEPS + 2, 2, 0)
                if C2:
                    c_stats(n2)
                    c_mean_var(n2)
                scan_clip(sl + 1, j * STEPS + 2, 2, 1)
                scan_add(sl + 1, j * STEPS + 3, 3, 0)
                scan_add(sl + 1, j * STEPS + 3, 3, 1)
                scan_clip(sl + 1, j * STEPS + 3, 3, 0)
                scan_clip(sl + 1, j * STEPS + 3, 3, 1)
                if A:
                    a_silu(na)
                scan_add(sl + 1, j * STEPS + 4, 4, 0)
                scan_add(sl + 1, j * STEPS + 4, 4, 1)
                if A:
                    a_stats(na)
                    a_mean_var(na)
                scan_clip(sl + 1, j * STEPS + 4, 4, 0)
                scan_clip(sl + 1, j * STEPS + 4, 4, 1)
                if C2:
                    c_scale_qv(c2, n2)
                scan_add(sl + 1, j * STEPS + 5, 5, 0)
                scan_add(sl + 1, j * STEPS + 5, 5, 1)
                if C2:
                    c_max(n2, 0)
                    c_subtract(n2, 0)
                scan_clip(sl + 1, j * STEPS + 5, 5, 0)
                scan_clip(sl + 1, j * STEPS + 5, 5, 1)
                if C2:
                    c_max(n2, 1)
                    c_subtract(n2, 1)
                scan_add(sl + 1, j * STEPS + 6, 6, 0)
                scan_add(sl + 1, j * STEPS + 6, 6, 1)
                scan_clip(sl + 1, j * STEPS + 6, 6, 0)
                scan_clip(sl + 1, j * STEPS + 6, 6, 1)
                scan_add(sl + 1, j * STEPS + 7, 7, 0)
                scan_add(sl + 1, j * STEPS + 7, 7, 1)
                scan_clip(sl + 1, j * STEPS + 7, 7, 0)
                if A:
                    a_bound_norm(na)
                scan_clip(sl + 1, j * STEPS + 7, 7, 1)
                if C1:
                    c_silu(n1)
                if A:
                    a_scale_b(na)
                if C2:
                    c_divide(n2)
                if C1:
                    c_gate_product(n1)

            def drain(i, j, C1, C2, C3):
                sl = i * SLICES + j
                n1, n2, n3 = sl - C1_LAG + 1, sl - C2_LAG + 1, sl - C3_LAG + 1
                c2 = sl - C2_LAG
                if C2:
                    c_residual(n2, ps_a)
                    c_stats(n2)
                    c_mean_var(n2)
                if C3:
                    c_demodulate(n3)
                if C2:
                    c_scale_qv(c2, n2)
                    c_max(n2, 0)
                    c_subtract(n2, 0)
                    c_max(n2, 1)
                    c_subtract(n2, 1)
                if C1:
                    c_silu(n1, ps_a)
                    c_gate_product(n1)
                if C2:
                    c_divide(n2)

            run(dve, fill, slice_, drain, prep_b, after_first=invert_roots, before_last=demodulate)


_INS = ['x', 'cond_2048', 'L0_cond_W_in', 'L0_cond_W_conv', 'L0_cond_b_conv', 'L0_cond_ln_g', 'L0_cond_ln_b',
        'L0_cond_W_xproj', 'L0_cond_W_dt', 'L0_cond_b_dt', 'L0_cond_A_log', 'L0_cond_D', 'L0_cond_W_out',
        'L1_cond_q_weight', 'L1_cond_k_weight', 'L1_cond_v_weight', 'L1_cond_w_weight', 'L1_cond_u_weight']
_OUTS = [((128, 64, 256), 'float32')]


def kernel(**inputs):
    import numpy as _np
    import concourse.bacc as _bacc
    from concourse import mybir as _mybir
    from concourse.bass_utils import run_bass_kernel_spmd as _run

    nc = _bacc.Bacc("TRN2", target_bir_lowering=False, num_devices=1)
    arrays, args = {}, []
    for name in _INS:
        a = _np.ascontiguousarray(inputs[name])
        arrays[f"in_{name}_dram"] = a
        args.append(nc.dram_tensor(f"in_{name}_dram", a.shape, _mybir.dt.from_np(a.dtype), kind="ExternalInput").ap())
    for i, (shape, dtype) in enumerate(_OUTS):
        dt = _mybir.dt.from_np(_np.dtype(dtype))
        args.append(nc.dram_tensor(f"out_{i}_dram", shape, dt, kind="ExternalOutput").ap())
    mamba_attention_kernel(nc, *args)
    r = _run(nc, [arrays], core_ids=[0])
    got = tuple(r.results[0][f"out_{i}_dram"] for i in range(len(_OUTS)))
    return got[0]
```
